# Optimizing a Trainium2 kernel written in Bass

```python
import numpy as np
import jax
import jax.numpy as jnp

def _softmax(x, axis=-1):
    return jax.nn.softmax(x, axis=axis)

def _gelu(x):
    return jax.nn.gelu(x, approximate=True)

def _silu(x):
    return jax.nn.silu(x)

def _sigmoid(x):
    return jax.nn.sigmoid(x)

def _layernorm(x, axis=-1, eps=1e-05):
    m = jnp.mean(x, axis=axis, keepdims=True)
    v = jnp.var(x, axis=axis, keepdims=True)
    return (x - m) / jnp.sqrt(v + eps)

def _scatter_add(tgt, idx, src, axis=0):
    return tgt.at[idx].add(src)

def _segment_sum(src, seg, n):
    return jax.ops.segment_sum(src, seg, n)
kernel_name = 'mk_perceiver_d1_seqx_r2_819b60'

def setup_inputs(seed: int=0):
    np.random.seed(seed)
    _w = jnp.asarray

    def _rec_inputs():
        import jax
        import jax.numpy as jnp
        _rk = jax.random.key(seed)
        x = -0.0003929 + 0.9999 * jax.random.normal(jax.random.fold_in(_rk, 1), (4, 128, 2048), jnp.float32)
        _lenS = 128 - jax.random.randint(jax.random.fold_in(_rk, 7), (4,), 0, max(1, 128 // 4) + 1, jnp.int32)
        _lenS2 = 2048 - jax.random.randint(jax.random.fold_in(_rk, 8), (4,), 0, max(1, 2048 // 4) + 1, jnp.int32)
        pos_BxS = jnp.broadcast_to(jnp.arange(128, dtype=jnp.int32), (4, 128))
        _ctx_1024P = jax.random.normal(jax.random.fold_in(_rk, 12), (4, 16, 512), jnp.float32)
        _ctx_1024c = jax.random.dirichlet(jax.random.fold_in(_rk, 512), 0.3 * jnp.ones((16,), jnp.float32), (4, 2048))
        _ctx_1024t = jnp.einsum('bsk,bkd->bsd', _ctx_1024c, _ctx_1024P)
        _ctx_1024t = _ctx_1024t * jax.lax.rsqrt(jnp.mean(jnp.square(_ctx_1024t)) + 1e-12) * 0.953939
        ctx_1024 = 6.77073e-06 + 0.0199965 * (_ctx_1024t + 0.3 * jax.random.normal(jax.random.fold_in(_rk, 612), (4, 2048, 512), jnp.float32))
        return (x, pos_BxS, ctx_1024)
    x, pos_BxS, ctx_1024 = _rec_inputs()

    def _L0_xattn_setup():
        import jax, jax.numpy as jnp
        import numpy as np
        H = 512
        C = 4
        RH = 16
        HS = H // RH
        DR = 8
        M = 2048
        NH = 16
        HD = H // NH
        A_SIZE = (C - 1) * RH
        B_SIZE = C * RH
        EPS = 1e-05
        SSM_EPS = 1e-05

        def rat_read(res, W, gamma, beta, num_outputs):
            b, l, _ = res.shape
            x = res.reshape(b, l, H, C)
            y = jnp.einsum('blhc,hoc->bloh', x, W)
            mu = y.mean(-1, keepdims=True)
            var = y.var(-1, keepdims=True)
            yn = (y - mu) * jax.lax.rsqrt(var + EPS)
            yn = yn * gamma.reshape(num_outputs, H) + beta.reshape(num_outputs, H)
            return yn.reshape(b, l, num_outputs * H)

        def rope(x, pos):
            half = HD // 2
            inv = 1.0 / 10000.0 ** (jnp.arange(half, dtype=jnp.float32) / half)
            ang = pos.astype(jnp.float32)[..., None] * inv
            cos = jnp.cos(ang)[:, :, None, :]
            sin = jnp.sin(ang)[:, :, None, :]
            x1, x2 = (x[..., :half], x[..., half:])
            return jnp.concatenate([x1 * cos - x2 * sin, x2 * cos + x1 * sin], axis=-1)

        def attention(qkv_in, qkv_w, pos):
            b, l, _ = qkv_in.shape
            q, k, v = jnp.split(qkv_in, 3, axis=-1)
            q = jnp.einsum('bli,oi->blo', q, qkv_w[0]).reshape(b, l, NH, HD)
            k = jnp.einsum('bli,oi->blo', k, qkv_w[1]).reshape(b, l, NH, HD)
            v = jnp.einsum('bli,oi->blo', v, qkv_w[2]).reshape(b, l, NH, HD)
            q = rope(q, pos)
            k = rope(k, pos)
            scores = jnp.einsum('bqhd,bkhd->bhqk', q, k) / np.sqrt(HD).astype(np.float32)
            mask = jnp.tril(jnp.ones((l, l), dtype=bool))
            scores = jnp.where(mask, scores, jnp.float32(-1e+30))
            p = jax.nn.softmax(scores, axis=-1)
            o = jnp.einsum('bhqk,bkhd->bqhd', p, v)
            return o.reshape(b, l, H)

        def rat_write(res, y, wod_w, wab_w, wab_b, du_w, du_b):
            b, l, _ = res.shape
            o_d = y @ wod_w.T
            A_B = y @ wab_w.T + wab_b
            out = o_d[..., :H]
            delta_low = o_d[..., H:]
            A_logit = A_B[..., :A_SIZE]
            B_proj = A_B[..., A_SIZE:2 * A_SIZE]
            B_skip = A_B[..., 2 * A_SIZE:]
            delta = jax.nn.softplus(delta_low @ du_w.T + du_b)
            hs = res.reshape(b, l, HS, RH, C)
            out = out.reshape(b, l, HS, RH, 1)
            delta = delta.reshape(b, l, HS, RH, 1)
            A_logit = A_logit.reshape(b, l, 1, RH, C - 1)
            B_proj = B_proj.reshape(b, l, 1, RH, C - 1)
            B_skip = B_skip.reshape(b, l, 1, RH, 1)
            A_neg = -jax.nn.softplus(A_logit)
            A_bar = jnp.exp(delta * A_neg)
            B_bar = (A_bar - 1.0) / (A_neg - SSM_EPS) * B_proj
            B_bar_skip = delta * B_skip
            A_full = jnp.concatenate([A_bar, jnp.ones_like(A_bar[..., :1])], axis=-1)
            B_full = jnp.concatenate([B_bar, B_bar_skip], axis=-1)
            return (hs * A_full + out * B_full).reshape(b, l, H * C)

        def layer_forward(hidden_states, position_ids, attn_read_w, attn_read_g, attn_read_b, qkv_w, attn_wod_w, attn_wab_w, attn_wab_b, attn_du_w, attn_du_b, mlp_read_w, mlp_read_g, mlp_read_b, mlp_in_w, mlp_wod_w, mlp_wab_w, mlp_wab_b, mlp_du_w, mlp_du_b):
            qkv_in = rat_read(hidden_states, attn_read_w, attn_read_g, attn_read_b, 3)
            attn_out = attention(qkv_in, qkv_w, position_ids)
            hidden_states = rat_write(hidden_states, attn_out, attn_wod_w, attn_wab_w, attn_wab_b, attn_du_w, attn_du_b)
            mlp_in = rat_read(hidden_states, mlp_read_w, mlp_read_g, mlp_read_b, 2)
            g_in, u_in = (mlp_in[..., :H], mlp_in[..., H:])
            gate = jnp.einsum('bli,oi->blo', g_in, mlp_in_w[0])
            up = jnp.einsum('bli,oi->blo', u_in, mlp_in_w[1])
            mlp_out = jax.nn.silu(gate) * up
            hidden_states = rat_write(hidden_states, mlp_out, mlp_wod_w, mlp_wab_w, mlp_wab_b, mlp_du_w, mlp_du_b)
            return hidden_states
        key = jax.random.key(seed)
        ks = jax.random.split(key, 20)
        B, L = (2, 1024)
        s = 0.02
        return {'hidden_states': jax.random.normal(ks[0], (B, L, H * C), jnp.float32), 'position_ids': jnp.tile(jnp.arange(L, dtype=jnp.int64), (B, 1)), 'attn_read_w': jax.random.normal(ks[1], (H, 3, C), jnp.float32) / np.sqrt(C).astype(np.float32), 'attn_read_g': jnp.ones((3 * H,), jnp.float32), 'attn_read_b': jnp.zeros((3 * H,), jnp.float32), 'qkv_w': jax.random.normal(ks[2], (3, H, H), jnp.float32) * s, 'attn_wod_w': jax.random.normal(ks[3], (H + DR, H), jnp.float32) * s, 'attn_wab_w': jax.random.normal(ks[4], (A_SIZE + B_SIZE, H), jnp.float32) * s, 'attn_wab_b': jax.random.normal(ks[5], (A_SIZE + B_SIZE,), jnp.float32) * s, 'attn_du_w': jax.random.normal(ks[6], (H, DR), jnp.float32) * s, 'attn_du_b': jax.random.normal(ks[7], (H,), jnp.float32) * s, 'mlp_read_w': jax.random.normal(ks[8], (H, 2, C), jnp.float32) / np.sqrt(C).astype(np.float32), 'mlp_read_g': jnp.ones((2 * H,), jnp.float32), 'mlp_read_b': jnp.zeros((2 * H,), jnp.float32), 'mlp_in_w': jax.random.normal(ks[9], (2, M, H), jnp.float32) * s, 'mlp_wod_w': jax.random.normal(ks[10], (H + DR, M), jnp.float32) * s, 'mlp_wab_w': jax.random.normal(ks[11], (A_SIZE + B_SIZE, M), jnp.float32) * s, 'mlp_wab_b': jax.random.normal(ks[12], (A_SIZE + B_SIZE,), jnp.float32) * s, 'mlp_du_w': jax.random.normal(ks[13], (H, DR), jnp.float32) * s, 'mlp_du_b': jax.random.normal(ks[14], (H,), jnp.float32) * s}
    _L0_xattn_all = _L0_xattn_setup()
    _L0_xattn_in = {k: v for k, v in _L0_xattn_all.items() if k in ('attn_read_w', 'attn_read_g', 'attn_read_b', 'qkv_w', 'attn_wod_w', 'attn_wab_w', 'attn_wab_b', 'attn_du_w', 'attn_du_b', 'mlp_read_w', 'mlp_read_g', 'mlp_read_b', 'mlp_wod_w', 'mlp_wab_w', 'mlp_wab_b', 'mlp_du_w', 'mlp_du_b')}
    del _L0_xattn_all

    def _L0_attn_setup():
        import jax, jax.numpy as jnp
        import numpy as np
        import math
        B, S, H = (1, 1024, 2048)
        NH, NKV, HD = (32, 8, 128)
        GS = 128
        WBITS = 4
        ZERO = float(2 ** (WBITS - 1))
        THETA = 10000.0

        def _dequant_matmul(x, qw, scales):
            w = (qw.astype(jnp.float32) - ZERO) * jnp.repeat(scales, GS, axis=0)
            return x @ w

        def _rope_tables(seq_len, dtype):
            inv_freq = 1.0 / THETA ** (jnp.arange(0, HD, 2, dtype=jnp.float32) / HD)
            freqs = jnp.arange(seq_len, dtype=jnp.float32)[:, None] * inv_freq
            emb = jnp.concatenate([freqs, freqs], axis=-1)
            return (jnp.cos(emb).astype(dtype), jnp.sin(emb).astype(dtype))

        def _rotate_half(x):
            x1, x2 = jnp.split(x, 2, axis=-1)
            return jnp.concatenate([-x2, x1], axis=-1)

        def _apply_rope(x, cos, sin):
            return x * cos[None, None] + _rotate_half(x) * sin[None, None]
        key = jax.random.key(seed)
        ks = jax.random.split(key, 9)
        small = lambda k, shp: jax.random.uniform(k, shp, jnp.float32) * 0.01 + 0.001
        return {'hidden_states': jax.random.normal(ks[0], (B, S, H), jnp.float32), 'scales_q': small(ks[1], (H // GS, NH * HD)), 'scales_k': small(ks[2], (H // GS, NKV * HD)), 'scales_v': small(ks[3], (H // GS, NKV * HD)), 'scales_o': small(ks[4], (NH * HD // GS, H)), 'qw_q': jax.random.randint(ks[5], (H, NH * HD), 0, 2 ** WBITS, jnp.int32), 'qw_k': jax.random.randint(ks[6], (H, NKV * HD), 0, 2 ** WBITS, jnp.int32), 'qw_v': jax.random.randint(ks[7], (H, NKV * HD), 0, 2 ** WBITS, jnp.int32), 'qw_o': jax.random.randint(ks[8], (NH * HD, H), 0, 2 ** WBITS, jnp.int32)}
    _L0_attn_all = _L0_attn_setup()
    _L0_attn_in = {k: v for k, v in _L0_attn_all.items() if k in ('scales_q', 'scales_k', 'scales_v', 'scales_o', 'qw_q', 'qw_k', 'qw_v', 'qw_o')}
    del _L0_attn_all

    def _L0_ffn_setup():
        import jax, jax.numpy as jnp
        import numpy as np
        TOP_K = 2
        SCALING = 32.0 / 64.0
        key = jax.random.key(seed)
        ks = jax.random.split(key, 6)
        Bsz, S, Din, Dout, R, E = (4, 1024, 2048, 2048, 64, 16)
        x = jax.random.normal(ks[0], (Bsz, S, Din), dtype=jnp.float32)
        base_w = jax.random.normal(ks[1], (Dout, Din), dtype=jnp.float32) * 0.02
        base_b = jax.random.normal(ks[2], (Dout,), dtype=jnp.float32) * 0.02
        A = jax.random.normal(ks[3], (R, Din), dtype=jnp.float32) * (1.0 / np.sqrt(Din))
        B = jax.random.normal(ks[4], (E, Dout, R), dtype=jnp.float32) * 0.02
        router_w = jax.random.normal(ks[5], (E, Din), dtype=jnp.float32) * 0.02
        return {'x': x, 'base_w': base_w, 'base_b': base_b, 'A': A, 'B': B, 'router_w': router_w}
    _L0_ffn_all = _L0_ffn_setup()
    _L0_ffn_in = {k: v for k, v in _L0_ffn_all.items() if k in ('base_w', 'base_b', 'A', 'B', 'router_w')}
    del _L0_ffn_all
    return {'x': x, 'pos_BxS': pos_BxS, 'ctx_1024': ctx_1024, 'L0_xattn_attn_read_w': _L0_xattn_in['attn_read_w'], 'L0_xattn_attn_read_g': _L0_xattn_in['attn_read_g'], 'L0_xattn_attn_read_b': _L0_xattn_in['attn_read_b'], 'L0_xattn_qkv_w': _L0_xattn_in['qkv_w'], 'L0_xattn_attn_wod_w': _L0_xattn_in['attn_wod_w'], 'L0_xattn_attn_wab_w': _L0_xattn_in['attn_wab_w'], 'L0_xattn_attn_wab_b': _L0_xattn_in['attn_wab_b'], 'L0_xattn_attn_du_w': _L0_xattn_in['attn_du_w'], 'L0_xattn_attn_du_b': _L0_xattn_in['attn_du_b'], 'L0_xattn_mlp_read_w': _L0_xattn_in['mlp_read_w'], 'L0_xattn_mlp_read_g': _L0_xattn_in['mlp_read_g'], 'L0_xattn_mlp_read_b': _L0_xattn_in['mlp_read_b'], 'L0_xattn_mlp_wod_w': _L0_xattn_in['mlp_wod_w'], 'L0_xattn_mlp_wab_w': _L0_xattn_in['mlp_wab_w'], 'L0_xattn_mlp_wab_b': _L0_xattn_in['mlp_wab_b'], 'L0_xattn_mlp_du_w': _L0_xattn_in['mlp_du_w'], 'L0_xattn_mlp_du_b': _L0_xattn_in['mlp_du_b'], 'L0_attn_scales_q': _L0_attn_in['scales_q'], 'L0_attn_scales_k': _L0_attn_in['scales_k'], 'L0_attn_scales_v': _L0_attn_in['scales_v'], 'L0_attn_scales_o': _L0_attn_in['scales_o'], 'L0_attn_qw_q': _L0_attn_in['qw_q'], 'L0_attn_qw_k': _L0_attn_in['qw_k'], 'L0_attn_qw_v': _L0_attn_in['qw_v'], 'L0_attn_qw_o': _L0_attn_in['qw_o'], 'L0_ffn_base_w': _L0_ffn_in['base_w'], 'L0_ffn_base_b': _L0_ffn_in['base_b'], 'L0_ffn_A': _L0_ffn_in['A'], 'L0_ffn_B': _L0_ffn_in['B'], 'L0_ffn_router_w': _L0_ffn_in['router_w']}

def reference(x, pos_BxS, ctx_1024, L0_xattn_attn_read_w, L0_xattn_attn_read_g, L0_xattn_attn_read_b, L0_xattn_qkv_w, L0_xattn_attn_wod_w, L0_xattn_attn_wab_w, L0_xattn_attn_wab_b, L0_xattn_attn_du_w, L0_xattn_attn_du_b, L0_xattn_mlp_read_w, L0_xattn_mlp_read_g, L0_xattn_mlp_read_b, L0_xattn_mlp_wod_w, L0_xattn_mlp_wab_w, L0_xattn_mlp_wab_b, L0_xattn_mlp_du_w, L0_xattn_mlp_du_b, L0_attn_scales_q, L0_attn_scales_k, L0_attn_scales_v, L0_attn_scales_o, L0_attn_qw_q, L0_attn_qw_k, L0_attn_qw_v, L0_attn_qw_o, L0_ffn_base_w, L0_ffn_base_b, L0_ffn_A, L0_ffn_B, L0_ffn_router_w):
    import jax
    import jax.numpy as jnp

    def _L0_xattn_ref(hidden_states, position_ids, attn_read_w, attn_read_g, attn_read_b, qkv_w, attn_wod_w, attn_wab_w, attn_wab_b, attn_du_w, attn_du_b, mlp_read_w, mlp_read_g, mlp_read_b, mlp_in_w, mlp_wod_w, mlp_wab_w, mlp_wab_b, mlp_du_w, mlp_du_b):
        import jax, jax.numpy as jnp
        import numpy as np
        H = 512
        C = 4
        RH = 16
        HS = H // RH
        DR = 8
        M = 2048
        NH = 16
        HD = H // NH
        A_SIZE = (C - 1) * RH
        B_SIZE = C * RH
        EPS = 1e-05
        SSM_EPS = 1e-05

        def rat_read(res, W, gamma, beta, num_outputs):
            b, l, _ = res.shape
            x = res.reshape(b, l, H, C)
            y = jnp.einsum('blhc,hoc->bloh', x, W)
            mu = y.mean(-1, keepdims=True)
            var = y.var(-1, keepdims=True)
            yn = (y - mu) * jax.lax.rsqrt(var + EPS)
            yn = yn * gamma.reshape(num_outputs, H) + beta.reshape(num_outputs, H)
            return yn.reshape(b, l, num_outputs * H)

        def rope(x, pos):
            half = HD // 2
            inv = 1.0 / 10000.0 ** (jnp.arange(half, dtype=jnp.float32) / half)
            ang = pos.astype(jnp.float32)[..., None] * inv
            cos = jnp.cos(ang)[:, :, None, :]
            sin = jnp.sin(ang)[:, :, None, :]
            x1, x2 = (x[..., :half], x[..., half:])
            return jnp.concatenate([x1 * cos - x2 * sin, x2 * cos + x1 * sin], axis=-1)

        def attention(qkv_in, qkv_w, pos):
            b, l, _ = qkv_in.shape
            q, k, v = jnp.split(qkv_in, 3, axis=-1)
            q = jnp.einsum('bli,oi->blo', q, qkv_w[0]).reshape(b, l, NH, HD)
            k = jnp.einsum('bli,oi->blo', k, qkv_w[1]).reshape(b, l, NH, HD)
            v = jnp.einsum('bli,oi->blo', v, qkv_w[2]).reshape(b, l, NH, HD)
            q = rope(q, pos)
            k = rope(k, pos)
            scores = jnp.einsum('bqhd,bkhd->bhqk', q, k) / np.sqrt(HD).astype(np.float32)
            mask = jnp.tril(jnp.ones((l, l), dtype=bool))
            scores = jnp.where(mask, scores, jnp.float32(-1e+30))
            p = jax.nn.softmax(scores, axis=-1)
            o = jnp.einsum('bhqk,bkhd->bqhd', p, v)
            return o.reshape(b, l, H)

        def rat_write(res, y, wod_w, wab_w, wab_b, du_w, du_b):
            b, l, _ = res.shape
            o_d = y @ wod_w.T
            A_B = y @ wab_w.T + wab_b
            out = o_d[..., :H]
            delta_low = o_d[..., H:]
            A_logit = A_B[..., :A_SIZE]
            B_proj = A_B[..., A_SIZE:2 * A_SIZE]
            B_skip = A_B[..., 2 * A_SIZE:]
            delta = jax.nn.softplus(delta_low @ du_w.T + du_b)
            hs = res.reshape(b, l, HS, RH, C)
            out = out.reshape(b, l, HS, RH, 1)
            delta = delta.reshape(b, l, HS, RH, 1)
            A_logit = A_logit.reshape(b, l, 1, RH, C - 1)
            B_proj = B_proj.reshape(b, l, 1, RH, C - 1)
            B_skip = B_skip.reshape(b, l, 1, RH, 1)
            A_neg = -jax.nn.softplus(A_logit)
            A_bar = jnp.exp(delta * A_neg)
            B_bar = (A_bar - 1.0) / (A_neg - SSM_EPS) * B_proj
            B_bar_skip = delta * B_skip
            A_full = jnp.concatenate([A_bar, jnp.ones_like(A_bar[..., :1])], axis=-1)
            B_full = jnp.concatenate([B_bar, B_bar_skip], axis=-1)
            return (hs * A_full + out * B_full).reshape(b, l, H * C)

        def layer_forward(hidden_states, position_ids, attn_read_w, attn_read_g, attn_read_b, qkv_w, attn_wod_w, attn_wab_w, attn_wab_b, attn_du_w, attn_du_b, mlp_read_w, mlp_read_g, mlp_read_b, mlp_in_w, mlp_wod_w, mlp_wab_w, mlp_wab_b, mlp_du_w, mlp_du_b):
            qkv_in = rat_read(hidden_states, attn_read_w, attn_read_g, attn_read_b, 3)
            attn_out = attention(qkv_in, qkv_w, position_ids)
            hidden_states = rat_write(hidden_states, attn_out, attn_wod_w, attn_wab_w, attn_wab_b, attn_du_w, attn_du_b)
            mlp_in = rat_read(hidden_states, mlp_read_w, mlp_read_g, mlp_read_b, 2)
            g_in, u_in = (mlp_in[..., :H], mlp_in[..., H:])
            gate = jnp.einsum('bli,oi->blo', g_in, mlp_in_w[0])
            up = jnp.einsum('bli,oi->blo', u_in, mlp_in_w[1])
            mlp_out = jax.nn.silu(gate) * up
            hidden_states = rat_write(hidden_states, mlp_out, mlp_wod_w, mlp_wab_w, mlp_wab_b, mlp_du_w, mlp_du_b)
            return hidden_states
        return layer_forward(hidden_states, position_ids, attn_read_w, attn_read_g, attn_read_b, qkv_w, attn_wod_w, attn_wab_w, attn_wab_b, attn_du_w, attn_du_b, mlp_read_w, mlp_read_g, mlp_read_b, mlp_in_w, mlp_wod_w, mlp_wab_w, mlp_wab_b, mlp_du_w, mlp_du_b)

    def _L0_attn_ref(hidden_states, scales_q, scales_k, scales_v, scales_o, qw_q, qw_k, qw_v, qw_o):
        import jax, jax.numpy as jnp
        import numpy as np
        import math
        B, S, H = (1, 1024, 2048)
        NH, NKV, HD = (32, 8, 128)
        GS = 128
        WBITS = 4
        ZERO = float(2 ** (WBITS - 1))
        THETA = 10000.0

        def _dequant_matmul(x, qw, scales):
            w = (qw.astype(jnp.float32) - ZERO) * jnp.repeat(scales, GS, axis=0)
            return x @ w

        def _rope_tables(seq_len, dtype):
            inv_freq = 1.0 / THETA ** (jnp.arange(0, HD, 2, dtype=jnp.float32) / HD)
            freqs = jnp.arange(seq_len, dtype=jnp.float32)[:, None] * inv_freq
            emb = jnp.concatenate([freqs, freqs], axis=-1)
            return (jnp.cos(emb).astype(dtype), jnp.sin(emb).astype(dtype))

        def _rotate_half(x):
            x1, x2 = jnp.split(x, 2, axis=-1)
            return jnp.concatenate([-x2, x1], axis=-1)

        def _apply_rope(x, cos, sin):
            return x * cos[None, None] + _rotate_half(x) * sin[None, None]
        b, s, _ = hidden_states.shape
        q = _dequant_matmul(hidden_states, qw_q, scales_q).reshape(b, s, NH, HD).transpose(0, 2, 1, 3)
        k = _dequant_matmul(hidden_states, qw_k, scales_k).reshape(b, s, NKV, HD).transpose(0, 2, 1, 3)
        v = _dequant_matmul(hidden_states, qw_v, scales_v).reshape(b, s, NKV, HD).transpose(0, 2, 1, 3)
        cos, sin = _rope_tables(s, hidden_states.dtype)
        q = _apply_rope(q, cos, sin)
        k = _apply_rope(k, cos, sin)
        rep = NH // NKV
        k = jnp.repeat(k, rep, axis=1)
        v = jnp.repeat(v, rep, axis=1)
        scores = jnp.einsum('bhqd,bhkd->bhqk', q, k) / math.sqrt(HD)
        causal = jnp.tril(jnp.ones((s, s), dtype=bool))
        scores = jnp.where(causal[None, None], scores, jnp.finfo(scores.dtype).min)
        attn = jax.nn.softmax(scores.astype(jnp.float32), axis=-1).astype(q.dtype)
        ctx = jnp.einsum('bhqk,bhkd->bhqd', attn, v)
        ctx = ctx.transpose(0, 2, 1, 3).reshape(b, s, NH * HD)
        return _dequant_matmul(ctx, qw_o, scales_o)

    def _L0_ffn_ref(x, base_w, base_b, A, B, router_w):
        import jax, jax.numpy as jnp
        import numpy as np
        TOP_K = 2
        SCALING = 32.0 / 64.0
        base_out = jnp.einsum('bsi,oi->bso', x, base_w) + base_b
        res_hidden = jnp.einsum('bsi,ri->bsr', x, A)
        logits = jnp.einsum('bsi,ei->bse', x, router_w)
        probs = jax.nn.softmax(logits, axis=-1)
        topw, topi = jax.lax.top_k(probs, TOP_K)
        topw = topw / (jnp.sum(topw, axis=-1, keepdims=True) + 1e-06)
        num_experts = B.shape[0]
        combine = jnp.sum(jax.nn.one_hot(topi, num_experts, dtype=x.dtype) * topw[..., None], axis=-2)
        delta = jnp.einsum('bse,bsr,eor->bso', combine, res_hidden, B)
        return base_out + delta * SCALING
    x = x + _L0_xattn_ref(_layernorm(x, axis=-1), pos_BxS, L0_xattn_attn_read_w, L0_xattn_attn_read_g, L0_xattn_attn_read_b, L0_xattn_qkv_w, L0_xattn_attn_wod_w, L0_xattn_attn_wab_w, L0_xattn_attn_wab_b, L0_xattn_attn_du_w, L0_xattn_attn_du_b, L0_xattn_mlp_read_w, L0_xattn_mlp_read_g, L0_xattn_mlp_read_b, ctx_1024, L0_xattn_mlp_wod_w, L0_xattn_mlp_wab_w, L0_xattn_mlp_wab_b, L0_xattn_mlp_du_w, L0_xattn_mlp_du_b)
    x = x + _L0_attn_ref(_layernorm(x, axis=-1), L0_attn_scales_q, L0_attn_scales_k, L0_attn_scales_v, L0_attn_scales_o, L0_attn_qw_q, L0_attn_qw_k, L0_attn_qw_v, L0_attn_qw_o)
    x = x + _L0_ffn_ref(_layernorm(x, axis=-1), L0_ffn_base_w, L0_ffn_base_b, L0_ffn_A, L0_ffn_B, L0_ffn_router_w)
    return x

_drawn_inputs = setup_inputs


def setup_inputs(seed=0):
    import zlib

    import numpy as np

    out = dict(_drawn_inputs(seed))
    spreads = {'L0_xattn_attn_read_g': (1.0, 0.2),
     'L0_xattn_attn_read_b': (0.0, 0.1),
     'L0_xattn_mlp_read_g': (1.0, 0.2),
     'L0_xattn_mlp_read_b': (0.0, 0.1)}
    factors = {}
    for name, (base, spread) in spreads.items():
        noise = np.random.default_rng([zlib.crc32(name.encode()), seed]).standard_normal(out[name].shape)
        drawn = base * np.exp(spread * noise) if base else spread * noise
        out[name] = jnp.asarray(drawn.astype(out[name].dtype))
    for name, factor in factors.items():
        out[name] = (out[name] * factor).astype(out[name].dtype)
    return out
```

```python
import numpy as np
import concourse.bass as bass
from concourse import mybir
from contextlib import ExitStack

F32 = mybir.dt.float32
F32R = mybir.dt.float32r
I32 = mybir.dt.int32
ALU = mybir.AluOpType
ACT = mybir.ActivationFunctionType
AXX = mybir.AxisListType.X

P = 128
B = 4
D = 2048
TOK = B * P
NT = 512
KD = D // P
EPS = 1e-5
GROUP = 2
RAW_SLOTS = 4
SCALE_SLOTS = 2
PART_SLOTS = 4


class Chain:

    def __init__(self, eng, sem, base=0):
        self.eng, self.sem, self.base, self.n = eng, sem, base, 0

    def __call__(self, ins):
        self.n += 1
        ins.then_inc(self.sem, 1)
        self.eng.wait_ge(self.sem, self.base + self.n)
        return ins


class Scope:

    def __init__(self, nc, ctx, prefix):
        self.nc, self.ctx, self.prefix, self.at = nc, ctx, prefix, {}

    def sb(self, name, shape, dt=F32):
        self.at[name] = -(-self.nc.sbuf_base // 32) * 32
        return self.ctx.enter_context(self.nc.sbuf_tensor(self.prefix + name, shape, dt))

    def over(self, host, row, name, shape, dt=F32):
        return self.nc.alloc_sbuf_tensor_at(self.prefix + name, shape, dt, offset=self.at[host] + row * 4 * NT)

    def banks(self):
        return [self.ctx.enter_context(self.nc.psum_tensor(f"{self.prefix}bank{i}", [P, NT], F32)) for i in range(8)]

    def sem(self, name):
        return self.ctx.enter_context(self.nc.semaphore(self.prefix + name))


def f32(ap):
    return ap.bitcast(F32)


ROUND = RAW_SLOTS * GROUP
LEAD = 2
SSM_EPS = 1e-5
ZERO = 8.0


class Norm:

    def __init__(self, s, R, ident, xn):
        self.R, self.ident, self.xn = R, ident, xn
        self.stats = s.sb("ln_stats", [P, B, 4, 6])
        self.mv = s.sb("ln_mv", [P, B, 2])
        self.veps = s.sb("ln_veps", [P, B])
        self.rstd = s.sb("ln_rstd", [P, B])
        self.nhalf = s.sb("ln_nhalf", [P, B])
        self.XH = s.sb("XH", [P, KD, TOK], F32R)
        self.XL = s.sb("XL", [P, KD, TOK], F32R)
        self.stats_done = s.sem("ln_stats_done")
        self.var_done = s.sem("ln_var_done")
        self.rstd_steps = s.sem("ln_rstd_steps")
        self.scaled = s.sem("ln_scaled")
        self.turned = s.sem("ln_turned")
        self.hi_done = s.sem("ln_hi_done")
        self.lo_done = s.sem("ln_lo_done")

    def pool(self, eng):
        eng.memset(self.nhalf[:, :], -0.5).then_inc(self.rstd_steps, 1)
        eng.wait_ge(self.var_done, 1)
        eng.tensor_scalar(self.veps[:, :], self.mv[:, :, 1], EPS, None, ALU.add).then_inc(self.rstd_steps, 1)
        eng.wait_ge(self.rstd_steps, 2)
        eng.tensor_tensor(self.rstd[:, :], self.veps[:, :], self.nhalf[:, :], ALU.pow).then_inc(self.rstd_steps, 1)

    def vector(self, eng, banks):
        for b in range(B):
            for c in range(4):
                last = eng.bn_stats(self.stats[:, b, c, :], self.R[:, b, c * NT:(c + 1) * NT])
        last.then_inc(self.stats_done, 1)
        eng.wait_ge(self.stats_done, 1)
        for b in range(B):
            last = eng.bn_aggr(self.mv[:, b, :], self.stats[:, b, :, :].rearrange("p c s -> p (c s)"))
        last.then_inc(self.var_done, 1)
        eng.wait_ge(self.var_done, 1)
        eng.wait_ge(self.rstd_steps, 3)
        for b in range(B):
            if b >= len(self.xn):
                eng.wait_ge(self.turned, 4 * (b - 1))
            eng.tensor_scalar(self.xn[b % len(self.xn)], self.R[:, b, :], self.mv[:, b, 0:1], self.rstd[:, b:b + 1],
                              ALU.subtract, ALU.mult).then_inc(self.scaled, 1)
            if b >= 1:
                self.low_parts(eng, banks, b - 1)
        self.low_parts(eng, banks, B - 1)

    def low_parts(self, eng, banks, b):
        for g in range(4):
            n = 4 * b + g
            eng.wait_ge(self.hi_done, n + 1)
            eng.tensor_tensor(self.XL[:, 4 * g:4 * g + 4, b * P:(b + 1) * P],
                              banks[n % 8][:, :].rearrange("p (c t) -> p c t", c=4),
                              f32(self.XH[:, 4 * g:4 * g + 4, b * P:(b + 1) * P]),
                              ALU.subtract).then_inc(self.lo_done, 1)

    def tensor(self, eng, banks):
        for n in range(4 * B):
            b, g = n // 4, n % 4
            if g == 0:
                eng.wait_ge(self.scaled, b + 1)
            if n >= 8:
                eng.wait_ge(self.lo_done, n - 7)
            for c in range(4):
                last = eng.transpose(banks[n % 8][:, c * P:(c + 1) * P],
                                     self.xn[b % len(self.xn)][:, (4 * g + c) * P:(4 * g + c + 1) * P], self.ident[:, :])
            last.then_inc(self.turned, 1)

    def scalar(self, eng, banks):
        for n in range(4 * B):
            b, g = n // 4, n % 4
            eng.wait_ge(self.turned, n + 1)
            eng.activation(self.XH[:, 4 * g:4 * g + 4, b * P:(b + 1) * P],
                           banks[n % 8][:, :].rearrange("p (c t) -> p c t", c=4), ACT.Copy).then_inc(self.hi_done, 1)


class Stream:

    def __init__(self, s, tiles, dram, scales=None):
        self.tiles, self.dram, self.scales = tiles, dram, scales
        self.raw = [s.sb(f"raw{n}", [P, GROUP, NT], I32 if scales is not None else F32) for n in range(RAW_SLOTS)]
        if scales is not None:
            self.scale = [s.sb(f"scale{n}", [P, GROUP * NT]) for n in range(SCALE_SLOTS)]
            self.scale_loaded = [s.sem(f"scale_loaded{n}") for n in range(SCALE_SLOTS)]
            self.scaled = s.sem("tile_scaled")
        self.WH = [s.sb(f"WH{n}", [P, NT], F32R) for n in range(PART_SLOTS)]
        self.WL = [s.sb(f"WL{n}", [P, NT], F32R) for n in range(PART_SLOTS)]
        self.raw_loaded = [s.sem(f"raw_loaded{n}") for n in range(RAW_SLOTS)]
        self.hi_done = s.sem("tile_hi_done")
        self.lo_done = s.sem("tile_lo_done")
        self.used = s.sem("tile_used")

    def load_round(self, eng, r, first):
        for g in range(RAW_SLOTS):
            if not first:
                eng.wait_ge(self.lo_done, r * ROUND + (g + 1) * GROUP - ROUND)
            q = r * RAW_SLOTS + g
            eng.dma_start(self.raw[g][:, :, :], self.dram[bass.ds(q, 1), :, :, :].rearrange("a p t n -> (a p) t n"))\
               .then_inc(self.raw_loaded[g], 16)
            if self.scales is not None:
                if not first or g >= SCALE_SLOTS:
                    eng.wait_ge(self.scaled, r * ROUND + (g + 1 - SCALE_SLOTS) * GROUP)
                eng.dma_start(self.scale[g % SCALE_SLOTS][:, :],
                              self.scales[bass.ds(q, 1), :].broadcast_to([P, GROUP * NT]))\
                   .then_inc(self.scale_loaded[g % SCALE_SLOTS], 16)

    def loads(self, eng):
        self.load_round(eng, 0, True)
        rounds = -(-self.tiles // ROUND)
        with eng.Fori(1, rounds) as r:
            self.load_round(eng, r, False)
        for loaded in self.raw_loaded:
            eng.wait_ge(loaded, 16 * rounds)

    def w(self, t):
        raw = self.raw[t % ROUND // GROUP][:, t % GROUP, :]
        return raw.bitcast(F32) if self.scales is not None else raw

    def dequantise(self, eng, r, t):
        g = t % ROUND // GROUP
        if t % GROUP == 0:
            eng.wait_ge(self.raw_loaded[g], (r + t // ROUND) * 16 + 16)
            eng.wait_ge(self.scale_loaded[g % SCALE_SLOTS], (r + t // ROUND) * 32 + 16 * (g // SCALE_SLOTS + 1))
        eng.scalar_tensor_tensor(out=self.w(t), in0=self.raw[g][:, t % GROUP, :], scalar=-ZERO,
                                 in1=self.scale[g % SCALE_SLOTS][:, t % GROUP * NT:(t % GROUP + 1) * NT],
                                 op0=ALU.add, op1=ALU.mult).then_inc(self.scaled, 1)

    def high(self, eng, r, t):
        if self.scales is not None:
            eng.wait_ge(self.scaled, r * ROUND + t + 1)
        elif t % GROUP == 0:
            eng.wait_ge(self.raw_loaded[t % ROUND // GROUP], (r + t // ROUND) * 16 + 16)
        if not isinstance(r, int) or r * ROUND + t >= PART_SLOTS:
            eng.wait_ge(self.used, r * ROUND + t + 1 - PART_SLOTS)
        eng.activation(self.WH[t % PART_SLOTS][:, :], self.w(t), ACT.Copy).then_inc(self.hi_done, 1)

    def low(self, eng, r, t):
        eng.wait_ge(self.hi_done, r * ROUND + t + 1)
        eng.tensor_tensor(self.WL[t % PART_SLOTS][:, :], self.w(t), f32(self.WH[t % PART_SLOTS][:, :]),
                          ALU.subtract).then_inc(self.lo_done, 1)


    def begin_vector(self, eng):
        for t in range(LEAD + 1):
            if self.scales is not None:
                self.dequantise(eng, 0, t)
            if t:
                self.low(eng, 0, t - 1)

    def at_vector(self, eng, r, t):
        if not isinstance(r, int) or r * ROUND + t + LEAD + 1 < self.tiles:
            if self.scales is not None:
                self.dequantise(eng, r, t + LEAD + 1)
        if not isinstance(r, int) or r * ROUND + t + LEAD < self.tiles:
            self.low(eng, r, t + LEAD)

    def begin_scalar(self, eng):
        for t in range(LEAD):
            self.high(eng, 0, t)

    def at_scalar(self, eng, r, t):
        if not isinstance(r, int) or r * ROUND + t + LEAD < self.tiles:
            self.high(eng, r, t + LEAD)


    def product_features(self, eng, r, t, xh, xl, banks, first, last, free=None):
        eng.wait_ge(self.lo_done, r * ROUND + t + 1)
        wh, wl = self.WH[t % PART_SLOTS], self.WL[t % PART_SLOTS]
        for j, bank in enumerate(banks):
            if free:
                free(j)
            c = slice(j * P, (j + 1) * P)
            eng.matmul(bank[:, :], wh[:, c], xh, start=first, stop=False)
            eng.matmul(bank[:, :], wh[:, c], xl, start=False, stop=False)
            mm = eng.matmul(bank[:, :], wl[:, c], xh, start=False, stop=last)
        mm.then_inc(self.used, 1)

    def product_tokens(self, eng, r, t, xh, xl, banks, first, last, free=None):
        eng.wait_ge(self.lo_done, r * ROUND + t + 1)
        wh, wl = self.WH[t % PART_SLOTS], self.WL[t % PART_SLOTS]
        for b, bank in enumerate(banks):
            if free:
                free(b)
            c = slice(b * P, (b + 1) * P)
            eng.matmul(bank[:, :], xh[:, c], wh[:, :], start=first, stop=False)
            eng.matmul(bank[:, :], xh[:, c], wl[:, :], start=False, stop=False)
            mm = eng.matmul(bank[:, :], xl[:, c], wh[:, :], start=False, stop=last)
        mm.then_inc(self.used, 1)


def grouped_query_attention(nc, R, ident, wstream, scales, rope, causal):
    NKV = 8
    REP = 4
    STEPS = NKV
    QT_TILES = KD
    O_TILES = REP * D // NT
    TILES = 4 * KD + STEPS * (QT_TILES + O_TILES)
    SCALE = float(P) ** -0.5
    HALF = P // 2
    SCORES_AT = [1, 4, 7, 10]

    with ExitStack() as ctx:
        s = Scope(nc, ctx, "g_")
        banks = s.banks()
        KT = s.sb("KT", [P, NKV, TOK])
        V = s.sb("V", [P, B, NKV * P])
        xn = [KT[:, 0:4, :].rearrange("p a n -> p (a n)"), KT[:, 4:8, :].rearrange("p a n -> p (a n)")]
        norm = Norm(s, R, ident, xn)
        st = Stream(s, TILES, wstream, scales)
        QT = s.sb("QT", [P, REP, TOK])
        turn = [s.sb(f"turn{n}", [P, TOK]) for n in range(2)]
        rt = s.sb("rope", [P, 2, P])
        mask = s.sb("mask", [P, P])
        Vcur = s.sb("Vcur", [P, B, P])
        S = s.sb("S", [P, B, P])
        E = s.sb("E", [P, B, P])
        PT = s.sb("PT", [P, TOK])
        CH = s.sb("CH", [P, REP, TOK], F32R)
        CL = s.sb("CL", [P, REP, TOK], F32R)
        nmax = [s.sb(f"nmax{n}", [P, B]) for n in range(2)]
        rsum = [s.sb(f"rsum{n}", [P, B]) for n in range(2)]
        rinv = [s.sb(f"rinv{n}", [P, B]) for n in range(2)]

        tables_loaded = s.sem("tables_loaded")
        rope_multiplied = s.sem("rope_multiplied")
        rope_done = s.sem("rope_done")
        read_out = s.sem("read_out")
        v_staged = s.sem("v_staged")
        scores_done = s.sem("scores_done")
        masked = s.sem("masked")
        max_done = s.sem("max_done")
        exp_done = s.sem("exp_done")
        rinv_done = s.sem("rinv_done")
        prob_done = s.sem("prob_done")
        prob_turned = s.sem("prob_turned")
        prob_copied = s.sem("prob_copied")
        pv_done = s.sem("pv_done")
        ctx_high = s.sem("ctx_high")
        ctx_low = s.sem("ctx_low")
        block = ctx.enter_context(nc.Block())

        def before(i):
            return (4 * KD + QT_TILES - QT_TILES - O_TILES) // ROUND + (QT_TILES + O_TILES) // ROUND * i

        def tile_end(r, t):
            return r * ROUND + t + 1

        bc = lambda ap: ap.unsqueeze(1).broadcast_to([ap.shape[0], B, P])

        @block.sync
        def _(sp):
            sp.dma_start(rt[:, :, :], rope).then_inc(tables_loaded, 16)
            sp.dma_start(mask[:, :], causal).then_inc(tables_loaded, 16)
            st.loads(sp)

        @block.gpsimd
        def _(pool):
            norm.pool(pool)

            def rope_add(h, dst):
                pool.wait_ge(rope_multiplied, h + 1)
                j = dst[1] % 2
                pool.tensor_tensor(dst[0], dst[0], turn[j][:, :], ALU.add).then_inc(rope_done, 1)

            for h in range(NKV):
                rope_add(h, (KT[:, h, :], h))
            with pool.Fori(0, STEPS) as i:
                for j in range(REP):
                    rope_add(NKV + i * REP + j, (QT[:, j, :], j))

        @block.vector
        def _(dve):
            st_r = st

            def rope_mult(r, t, h, j, bank, dst):
                dve.wait_ge(st_r.used, tile_end(r, t))
                if not isinstance(h, int) or h >= 2:
                    dve.wait_ge(rope_done, h - 1)
                v = lambda ap: ap.rearrange("p (b t) -> p b t", b=B)
                dve.tensor_tensor(v(dst), v(bank[:, :]), bc(rt[:, 0, :]), ALU.mult)
                dve.tensor_tensor(v(turn[j % 2][0:HALF, :]), v(bank[HALF:P, :]), bc(rt[HALF:P, 1, :]), ALU.mult)
                dve.tensor_tensor(v(turn[j % 2][HALF:P, :]), v(bank[0:HALF, :]), bc(rt[0:HALF, 1, :]),
                                  ALU.mult).then_inc(rope_multiplied, 1)

            def read_values(r, t, n, b):
                dve.wait_ge(st.used, tile_end(r, t))
                dve.tensor_copy(V[:, b, n * NT:(n + 1) * NT], banks[4 * n + b][:, :]).then_inc(read_out, 1)

            def mask_max(i, j):
                h = (i - 1) * REP + j
                dve.wait_ge(scores_done, h + 1)
                if j:
                    dve.wait_ge(exp_done, h)
                dve.scalar_tensor_tensor(out=S[:, :, :], in0=banks[4][:, :].rearrange("p (b k) -> p b k", b=B),
                                         scalar=SCALE, in1=bc(mask[:, :]), op0=ALU.mult, op1=ALU.add)\
                   .then_inc(masked, 1)
                dve.wait_ge(masked, h + 1)
                dve.tensor_reduce(nmax[j % 2][:, :], S[:, :, :], AXX, ALU.max, negate=True).then_inc(max_done, 1)

            def normalise(i, j):
                h = (i - 1) * REP + j
                dve.wait_ge(exp_done, h + 1)
                dve.reciprocal(rinv[j % 2][:, :], rsum[j % 2][:, :]).then_inc(rinv_done, 1)
                dve.wait_ge(rinv_done, h + 1)
                dve.tensor_tensor(E[:, :, :], E[:, :, :], rinv[j % 2][:, :].unsqueeze(2).broadcast_to([P, B, P]),
                                  ALU.mult).then_inc(prob_done, 1)

            def context_low(i, j):
                dve.wait_ge(ctx_high, (i - 1) * REP + j + 1)
                dve.tensor_tensor(CL[:, j, :], banks[6][:, :], f32(CH[:, j, :]), ALU.subtract).then_inc(ctx_low, 1)

            def add_output(r, o, n, b):
                dve.wait_ge(st.used, tile_end(r, o + REP * n + REP - 1))
                out = R[:, b, n * NT:(n + 1) * NT]
                dve.tensor_tensor(out, banks[4 * ((n + 1) % 2) + b][:, :], out, ALU.add).then_inc(read_out, 1)

            def attention_at(i, k):
                for j, at in enumerate(SCORES_AT):
                    if k == at:
                        mask_max(i, j)
                    if k == at + 2:
                        normalise(i, j)
                    if k == at + 5:
                        context_low(i, j)

            def outputs(r, i, o):
                for t in range(O_TILES):
                    st.at_vector(dve, r, o + t)
                    if o and t < REP:
                        rope_mult(r, o - 1, NKV + i * REP + t, t, banks[t], QT[:, t, :])
                    for n in range(3):
                        if t - 4 * n - 4 in (0, 1):
                            for b in (0, 1):
                                add_output(r, o, n, 2 * (t - 4 * n - 4) + b)
                for b in range(B):
                    add_output(r, o, 3, b)

            norm.vector(dve, banks)
            st.begin_vector(dve)
            dve.wait_ge(tables_loaded, 32)
            for n in range(2):
                for k in range(KD):
                    st.at_vector(dve, 0, KD * n + k)
                    if n and k < REP:
                        rope_mult(0, KD - 1, k, k, banks[k], KT[:, k, :])
            for n in range(2):
                for k in range(KD):
                    st.at_vector(dve, 2 * KD // ROUND, KD * n + k)
                    if not n and k < REP:
                        rope_mult(0, 2 * KD - 1, REP + k, k, banks[4 + k], KT[:, REP + k, :])
                    if n and k < B:
                        read_values(2 * KD // ROUND, KD - 1, 0, k)
            for k in range(QT_TILES):
                st.at_vector(dve, 4 * KD // ROUND, k)
                if k < B:
                    read_values(2 * KD // ROUND, 2 * KD - 1, 1, k)
            for j in range(REP):
                rope_mult(4 * KD // ROUND, QT_TILES - 1, NKV + j, j, banks[j], QT[:, j, :])
            with dve.Fori(1, STEPS) as i:
                r = before(i)
                for k in range(QT_TILES):
                    st.at_vector(dve, r, k)
                    attention_at(i, k)
                outputs(r, i, QT_TILES)
            for k in range(QT_TILES):
                attention_at(STEPS, k)
            outputs(before(STEPS), STEPS, 0)

        @block.scalar
        def _(act):
            def stage_values(i):
                act.activation(Vcur[:, :, :], V[:, :, bass.ds(i * P, P)], ACT.Copy).then_inc(v_staged, 1)

            def exponent(i, j):
                h = (i - 1) * REP + j
                act.wait_ge(max_done, h + 1)
                if j:
                    act.wait_ge(prob_turned, h)
                for b in range(B):
                    last = act.activation(E[:, b, :], S[:, b, :], ACT.Exp, bias=nmax[j % 2][:, b:b + 1],
                                          accum_out=rsum[j % 2][:, b:b + 1])
                last.then_inc(exp_done, 1)

            def copy_turned(i, j):
                h = (i - 1) * REP + j
                act.wait_ge(prob_turned, h + 1)
                if j:
                    act.wait_ge(pv_done, h)
                act.activation(PT[:, :], banks[5][:, :], ACT.Copy).then_inc(prob_copied, 1)

            def context_high(r, i, j):
                act.wait_ge(pv_done, (i - 1) * REP + j + 1)
                if not j:
                    act.wait_ge(st.used, r * ROUND)
                act.activation(CH[:, j, :], banks[6][:, :], ACT.Copy).then_inc(ctx_high, 1)

            def attention_at(r, i, k):
                for j, at in enumerate(SCORES_AT):
                    if k == at:
                        exponent(i, j)
                    if k == at + 3:
                        copy_turned(i, j)
                    if k == at + 4:
                        context_high(r, i, j)

            norm.scalar(act, banks)
            st.begin_scalar(act)
            for r, n in ((0, 2 * KD), (2 * KD // ROUND, 2 * KD), (4 * KD // ROUND, QT_TILES)):
                for k in range(n):
                    st.at_scalar(act, r, k)
            act.wait_ge(read_out, 2 * B)
            stage_values(0)
            with act.Fori(1, STEPS) as i:
                r = before(i)
                for k in range(QT_TILES):
                    st.at_scalar(act, r, k)
                    attention_at(r, i, k)
                act.wait_ge(pv_done, i * REP)
                stage_values(i)
                for t in range(O_TILES):
                    st.at_scalar(act, r, QT_TILES + t)
            r = before(STEPS)
            for k in range(QT_TILES):
                attention_at(r, STEPS, k)
            for t in range(O_TILES):
                st.at_scalar(act, r, t)

        @block.tensor
        def _(pe):
            XH, XL = norm.XH, norm.XL

            def project_features(r, t0, use, free):
                for k in range(KD):
                    st.product_features(pe, r, t0 + k, XH[:, k, :], XL[:, k, :], use, k == 0, k == KD - 1,
                                        free if k == 0 else None)
                    yield k

            def project_tokens(r, t0, use, free):
                for k in range(KD):
                    st.product_tokens(pe, r, t0 + k, XH[:, k, :], XL[:, k, :], use, k == 0, k == KD - 1,
                                      free if k == 0 else None)

            def scores(i, j):
                h = (i - 1) * REP + j
                pe.wait_ge(rope_done, NKV + h + 1)
                if j:
                    pe.wait_ge(masked, h)
                for b in range(B):
                    c = slice(b * P, (b + 1) * P)
                    mm = pe.matmul(banks[4][:, c], QT[:, j, c], KT[:, bass.ds(i - 1, 1), c].rearrange("p a t -> p (a t)"),
                                   start=True, stop=True)
                mm.then_inc(scores_done, 1)

            def turn_probs(i, j):
                h = (i - 1) * REP + j
                pe.wait_ge(prob_done, h + 1)
                for b in range(B):
                    mm = pe.transpose(banks[5][:, b * P:(b + 1) * P], E[:, b, :], ident[:, :])
                mm.then_inc(prob_turned, 1)

            def values(i, j):
                h = (i - 1) * REP + j
                pe.wait_ge(prob_copied, h + 1)
                if j:
                    pe.wait_ge(ctx_low, h)
                else:
                    pe.wait_ge(v_staged, i)
                for b in range(B):
                    c = slice(b * P, (b + 1) * P)
                    mm = pe.matmul(banks[6][:, c], Vcur[:, b, :], PT[:, c], start=True, stop=True)
                mm.then_inc(pv_done, 1)

            def attention_at(i, k):
                for j, at in enumerate(SCORES_AT):
                    if k == at:
                        scores(i, j)
                    if k == at + 3:
                        turn_probs(i, j)
                    if k == at + 4:
                        values(i, j)

            def outputs(r, i, o):
                pe.wait_ge(ctx_low, i * REP)
                for n in range(4):
                    use = banks[4:8] if n % 2 == 0 else banks[0:4]

                    def free(b, n=n):
                        if n == 1 and o:
                            pe.wait_ge(rope_multiplied, NKV + i * REP + b + 1)
                        if n == 1 and not o and b == 0:
                            pe.wait_ge(rope_multiplied, NKV + (i - 1) * REP + REP)
                        if n >= 2:
                            pe.wait_ge(read_out, 2 * B + (i - 1) * 4 * B + (n - 2) * B + b + 1)
                    for j in range(REP):
                        st.product_tokens(pe, r, o + REP * n + j, CH[:, j, :], CL[:, j, :], use, j == 0, j == REP - 1,
                                          free if j == 0 else None)

            norm.tensor(pe, banks)
            pe.wait_ge(norm.lo_done, 4 * B)
            for n in range(2):
                for _k in project_features(0, n * KD, banks[4 * n:4 * n + 4], None):
                    pass
            for n in range(2):
                project_tokens(2 * KD // ROUND, n * KD, banks[4 * n:4 * n + 4],
                               lambda b, n=n: pe.wait_ge(rope_multiplied, REP * n + b + 1))
            for _k in project_features(4 * KD // ROUND, 0, banks[0:4], lambda j: pe.wait_ge(read_out, j + 1)):
                pass
            with pe.Fori(1, STEPS) as i:
                r = before(i)
                pe.wait_ge(rope_multiplied, NKV + i * REP)
                free = lambda j: pe.wait_ge(read_out, 2 * B + (i - 1) * 4 * B - B + j + 1)
                for k in project_features(r, 0, banks[0:4], free):
                    attention_at(i, k)
                outputs(r, i, QT_TILES)
            pe.wait_ge(read_out, 2 * B + (STEPS - 1) * 4 * B)
            for k in range(QT_TILES):
                attention_at(STEPS, k)
            outputs(before(STEPS), STEPS, 0)


XH_ = 512
C = 4
RH = 16
HS = XH_ // RH
AC = C - 1
PIECE = 4
SIDE_SKIP = RH
SIDE_A = 2 * RH
SIDE_B = SIDE_A + RH * AC


class Read:

    def __init__(self, s, st, outs, XH, XL, Y, YH, YL, F, gamma, beta, ident):
        self.st, self.outs, self.XH, self.XL, self.Y = st, outs, XH, XL, Y
        self.YH, self.YL, self.F, self.gamma, self.beta, self.ident = YH, YL, F, gamma, beta, ident
        n = outs * B
        self.stats = s.sb("y_stats", [P, n, 6])
        self.mv = s.sb("y_mv", [P, n, 2])
        self.veps = s.sb("y_veps", [P, n])
        self.rstd = s.sb("y_rstd", [P, n])
        self.nhalf = s.sb("y_nhalf", [P, n])
        self.y_read = s.sem("y_read")
        self.y_stats_done = s.sem("y_stats_done")
        self.y_var = s.sem("y_var")
        self.y_rstd_steps = s.sem("y_rstd_steps")
        self.y_scaled = s.sem("y_scaled")
        self.y_turned = s.sem("y_turned")
        self.y_affine = s.sem("y_affine")
        self.y_high = s.sem("y_high")
        self.y_low = s.sem("y_low")

    def tensor_sums(self, eng, banks):
        st = self.st
        for t in range(KD // PIECE):
            eng.wait_ge(st.lo_done, t + 1)
            wh, wl = st.WH[t % PART_SLOTS], st.WL[t % PART_SLOTS]
            for b in range(B):
                n = B * t + b
                if n >= 8:
                    eng.wait_ge(self.y_read, n - 7)
                for j in range(PIECE):
                    k, c = PIECE * t + j, slice(b * P, (b + 1) * P)
                    w = slice(j * P, j * P + 32 * self.outs)
                    out = banks[n % 8][:, w]
                    eng.matmul(out, self.XH[:, k, c], wh[:, w], start=True, stop=False)
                    eng.matmul(out, self.XH[:, k, c], wl[:, w], start=False, stop=False)
                    mm = eng.matmul(out, self.XL[:, k, c], wh[:, w], start=False, stop=True)
            mm.then_inc(st.used, 1)

    def scalar_sums(self, eng, banks):
        for t in range(KD // PIECE):
            self.st.at_scalar(eng, 0, t)
            eng.wait_ge(self.st.used, t + 1)
            for b in range(B):
                src = banks[(B * t + b) % 8][:, :].rearrange("p (j o h) -> p j o h", j=PIECE, h=32)[:, :, 0:self.outs, :]
                for o in range(self.outs):
                    last = eng.activation(self.Y[:, b, o, t * P:(t + 1) * P].rearrange("p (j h) -> p j h", j=PIECE),
                                          src[:, :, o, :], ACT.Copy)
                last.then_inc(self.y_read, 1)

    def vector_norm(self, eng):
        for t in range(KD // PIECE):
            self.st.at_vector(eng, 0, t)
        eng.wait_ge(self.y_read, 4 * B)
        for n in range(self.outs * B):
            last = eng.bn_stats(self.stats[:, n, :], self.Y[:, n % B, n // B, :])
        last.then_inc(self.y_stats_done, 1)
        eng.wait_ge(self.y_stats_done, 1)
        for n in range(self.outs * B):
            last = eng.bn_aggr(self.mv[:, n, :], self.stats[:, n, :])
        last.then_inc(self.y_var, 1)
        eng.wait_ge(self.y_var, 1)
        eng.wait_ge(self.y_rstd_steps, 3)
        for n in range(self.outs * B):
            y = self.Y[:, n % B, n // B, :]
            eng.tensor_scalar(y, y, self.mv[:, n, 0:1], self.rstd[:, n:n + 1], ALU.subtract, ALU.mult)\
               .then_inc(self.y_scaled, 1)
        for n in range(4 * self.outs):
            eng.wait_ge(self.y_high, n + 1)
            eng.tensor_tensor(self.YL[:, n, :], self.F[n % 2][:, :], f32(self.YH[:, n, :]), ALU.subtract)\
               .then_inc(self.y_low, 1)

    def pool(self, eng):
        eng.memset(self.nhalf[:, :], -0.5).then_inc(self.y_rstd_steps, 1)
        eng.wait_ge(self.y_var, 1)
        eng.tensor_scalar(self.veps[:, :], self.mv[:, :, 1], EPS, None, ALU.add).then_inc(self.y_rstd_steps, 1)
        eng.wait_ge(self.y_rstd_steps, 2)
        eng.tensor_tensor(self.rstd[:, :], self.veps[:, :], self.nhalf[:, :], ALU.pow).then_inc(self.y_rstd_steps, 1)

    def tensor_turn(self, eng, banks):
        for n in range(4 * self.outs):
            o, hc = n // 4, n % 4
            eng.wait_ge(self.y_scaled, B * (o + 1))
            if n >= 8:
                eng.wait_ge(self.y_affine, n - 7)
            for b in range(B):
                mm = eng.transpose(banks[n % 8][:, b * P:(b + 1) * P], self.Y[:, b, o, hc * P:(hc + 1) * P], self.ident[:, :])
            mm.then_inc(self.y_turned, 1)

    def scalar_affine(self, eng, banks, turned_first=0):
        for n in range(4 * self.outs):
            eng.wait_ge(self.y_turned, max(n + 1, turned_first))
            if n >= 2:
                eng.wait_ge(self.y_low, n - 1)
            eng.activation(self.F[n % 2][:, :], banks[n % 8][:, :], ACT.Identity, bias=self.beta[:, n:n + 1],
                           scale=self.gamma[:, n:n + 1]).then_inc(self.y_affine, 1)
            eng.wait_ge(self.y_affine, n + 1)
            eng.activation(self.YH[:, n, :], self.F[n % 2][:, :], ACT.Copy).then_inc(self.y_high, 1)


class Write:

    def __init__(self, s, H, delta, log, ARG, W3, U, T, F, ident, side_bias, DU):
        self.H, self.delta, self.log, self.ARG, self.W3, self.U, self.T = H, delta, log, ARG, W3, U, T
        self.ident, self.side_bias, self.DU = ident, side_bias, DU
        self.side = F[1][:, :].rearrange("p (b n) -> p b n", b=B)
        self.DLT = F[0]
        self.sp = s.sb("decay", [P, B, RH * AC])
        self.spl = s.sb("decay_log", [P, B, RH * AC])
        self.cn = s.sb("coef", [P, B, RH * AC])
        self.w_side = s.sem("w_side")
        self.w_turned = s.sem("w_turned")
        self.w_dlt = s.sem("w_dlt")
        self.w_pre = s.sem("w_pre")
        self.w_abs = s.sem("w_abs")
        self.w_exp = s.sem("w_exp")
        self.w_ln = s.sem("w_ln")
        self.w_delta = s.sem("w_delta")
        self.w_coef = s.sem("w_coef")
        self.w_arg = s.sem("w_arg")
        self.w_abar = s.sem("w_abar")
        self.w_steps = s.sem("w_steps")
        self.w_done = s.sem("w_done")

    def tensor(self, eng, banks):
        eng.wait_ge(self.w_side, B)
        for b in range(B):
            mm = eng.transpose(banks[4][:, b * P:(b + 1) * P], self.side[:, b, :], self.ident[:, :])
        mm.then_inc(self.w_turned, 1)
        eng.wait_ge(self.w_dlt, 1)
        for b in range(B):
            eng.matmul(banks[4 + b][:, :], self.DLT[0:9, b * P:(b + 1) * P], self.DU[0:9, :], start=True, stop=True)\
               .then_inc(self.w_pre, 1)

    def scalar(self, eng, banks):
        eng.wait_ge(self.w_turned, 1)
        eng.activation(self.DLT[0:9, :], banks[4][0:9, :], ACT.Copy).then_inc(self.w_dlt, 1)
        eng.wait_ge(self.w_side, B)
        eng.activation(self.spl[:, :, :], self.side[:, :, SIDE_A:SIDE_B], ACT.Abs).then_inc(self.w_abs, 1)
        parts = [self.spl[:, :, :]] + [self.log[:, b, :] for b in range(B)]
        for n, x in enumerate(parts):
            if n < B:
                eng.wait_ge(self.w_pre, n + 1)
                eng.activation(self.log[:, n, :], banks[4 + n][:, :], ACT.Abs).then_inc(self.w_abs, 1)
            eng.wait_ge(self.w_abs, n + 1)
            eng.activation(x, x, ACT.Exp, scale=-1.0).then_inc(self.w_exp, 1)
        eng.wait_ge(self.w_exp, B + 1)
        for x in parts:
            eng.activation(x, x, ACT.Ln, bias=1.0).then_inc(self.w_ln, 1)
        for b in range(B):
            eng.wait_ge(self.w_arg, 2 * b + 1)
            eng.activation(self.ARG[b % 2][:, :, :], self.ARG[b % 2][:, :, :], ACT.Exp, scale=-1.0).then_inc(self.w_abar, 1)

    def pool(self, eng):
        eng.wait_ge(self.w_coef, 1)
        for b in range(B):
            eng.wait_ge(self.w_delta, b + 1)
            if b >= 2:
                eng.wait_ge(self.w_done, b - 1)
            d = self.delta[:, b, :].rearrange("p (s r) -> p s r", r=RH)
            for c in range(AC):
                last = eng.tensor_tensor(self.ARG[b % 2][:, c, :].rearrange("p (s r) -> p s r", r=RH), d,
                                         self.per_group(self.sp, b, c), ALU.mult)
            last.then_inc(self.w_arg, 1)
            eng.tensor_tensor(self.W3[b % 2][:, :].rearrange("p (s r) -> p s r", r=RH), d,
                              self.side[:, b, SIDE_SKIP:SIDE_SKIP + RH].unsqueeze(1).broadcast_to([P, HS, RH]),
                              ALU.mult).then_inc(self.w_arg, 1)

    def per_group(self, x, b, c):
        return x[:, b, :].rearrange("p (r c) -> p r c", c=AC)[:, :, c].unsqueeze(1).broadcast_to([P, HS, RH])

    def vector(self, eng, banks, used):
        link = Chain(eng, self.w_steps)
        used(eng)
        for b in range(B):
            eng.tensor_tensor(self.side[:, b, :], banks[4 + b][:, 0:P], self.side_bias[:, :], ALU.add)\
               .then_inc(self.w_side, 1)
        eng.wait_ge(self.w_side, B)
        A = self.side[:, :, SIDE_A:SIDE_B]
        eng.wait_ge(self.w_ln, 1)
        link(eng.scalar_tensor_tensor(out=self.sp[:, :, :], in0=A, scalar=0.0, in1=self.spl[:, :, :],
                                      op0=ALU.max, op1=ALU.add))
        link(eng.tensor_scalar(self.spl[:, :, :], self.sp[:, :, :], SSM_EPS, None, ALU.add))
        link(eng.reciprocal(self.cn[:, :, :], self.spl[:, :, :]))
        eng.tensor_tensor(self.cn[:, :, :], self.cn[:, :, :], self.side[:, :, SIDE_B:P], ALU.mult).then_inc(self.w_coef, 1)
        for b in range(B):
            eng.wait_ge(self.w_ln, b + 2)
            eng.scalar_tensor_tensor(out=self.delta[:, b, :], in0=banks[4 + b][:, :], scalar=0.0, in1=self.log[:, b, :],
                                     op0=ALU.max, op1=ALU.add).then_inc(self.w_delta, 1)
        eng.wait_ge(self.w_coef, 1)
        for b in range(B):
            h = self.H[:, b, :].rearrange("p (n c) -> p c n", c=C)
            out = banks[b][:, :]
            for c in range(AC):
                last = eng.tensor_tensor(self.U[:, c, :].rearrange("p (s r) -> p s r", r=RH),
                                         out.rearrange("p (s r) -> p s r", r=RH), self.per_group(self.cn, b, c), ALU.mult)
            link(last)
            eng.wait_ge(self.w_arg, 2 * b + 2)
            eng.tensor_tensor(self.W3[b % 2][:, :], out, self.W3[b % 2][:, :], ALU.mult)
            link(eng.tensor_tensor(self.T[:, :, :], h[:, 0:AC, :], self.U[:, :, :], ALU.subtract))
            eng.tensor_tensor(h[:, AC, :], h[:, AC, :], self.W3[b % 2][:, :], ALU.add)
            eng.wait_ge(self.w_abar, b + 1)
            link(eng.tensor_tensor(self.T[:, :, :], self.T[:, :, :], self.ARG[b % 2][:, :, :], ALU.mult))
            eng.tensor_tensor(h[:, 0:AC, :], self.T[:, :, :], self.U[:, :, :], ALU.add).then_inc(self.w_done, 1)
            eng.wait_ge(self.w_done, b + 1)


def xattn_attention(nc, R, H, ident, x, wstream, gamma_d, beta_d, pos_d, inv_d, causal, side_bias_d, du_d):
    NH = 16
    HD = XH_ // NH
    HALF = HD // 2
    OUTS = 3
    TILES = KD // PIECE + OUTS * 4 + 4 + 1
    SCALE = 1.0 / float(np.sqrt(HD))
    QKV = KD // PIECE
    WOD = QKV + OUTS * 4
    TWO_PI = 2.0 * np.pi
    C1 = 6.28125
    C2 = float(np.round((TWO_PI - C1) * 2.0 ** 17) / 2.0 ** 17)
    C3 = float(np.float32(TWO_PI - C1 - C2))
    MAGIC = 1.5 * 2.0 ** 23
    LIMIT = 3.1415925

    with ExitStack() as ctx:
        s = Scope(nc, ctx, "a_")
        banks = s.banks()
        norm = Norm(s, R, ident, [H[:, b, :] for b in range(B)])
        st = Stream(s, TILES, wstream)
        YH = norm.XH[:, 0:12, :]
        YL = norm.XL[:, 0:12, :]
        QT = s.over("XH", 12, "QT", [P, 4, TOK])
        KT = s.over("XL", 12, "KT", [P, 4, TOK])
        PT = s.over("XH", 0, "PT", [P, NH, P])
        OH = norm.XH[:, 4:8, :]
        OL = norm.XL[:, 4:8, :]
        Y = s.sb("Y", [P, B, OUTS, XH_])
        q_tok = Y[:, :, 0, :]
        k_tok = Y[:, :, 1, :]
        V = Y[:, :, 2, :]
        S = s.sb("S", [P, NH, P])
        F = [s.sb(f"F{n}", [P, TOK]) for n in range(2)]
        gamma = s.sb("gamma", [P, 4 * OUTS])
        beta = s.sb("beta", [P, 4 * OUTS])
        read = Read(s, st, OUTS, norm.XH, norm.XL, Y, YH, YL, F, gamma, beta, ident)
        posi = s.sb("pos", [P, B], I32)
        posf = s.sb("posf", [P, B])
        inv = s.sb("inv", [P, HALF])
        ang = s.sb("ang", [P, B, HALF])
        kk = s.sb("kk", [P, B, HALF])
        sc = s.sb("sincos", [P, 3, B, HALF])
        mask = s.sb("mask", [P, P])
        nmax = s.sb("nmax", [P, NH])
        rsum = s.sb("rsum", [P, NH])
        rinv = s.sb("rinv", [P, NH])
        O = F[0]
        side_bias = s.sb("side_bias", [P, P])
        DU = s.sb("DU", [9, XH_])
        write = Write(s, H, QT, KT, [s.over(x, 8, "ARG_" + x, [P, AC, XH_]) for x in ("XH", "XL")],
                      [s.over(x, 11, "W3_" + x, [P, XH_]) for x in ("XH", "XL")],
                      s.over("XL", 0, "U", [P, AC, XH_]), s.over("XH", 0, "T", [P, AC, XH_]), F, ident, side_bias, DU)

        x_loaded = s.sem("x_loaded")
        small_loaded = s.sem("small_loaded")
        table_steps = s.sem("table_steps")
        sin_done = s.sem("sin_done")
        tables_done = s.sem("tables_done")
        rope_mult = s.sem("rope_mult")
        rope_done = s.sem("rope_done")
        v_read = s.sem("v_read")
        qk_turned = s.sem("qk_turned")
        qk_copied = s.sem("qk_copied")
        scores_done = s.sem("scores_done")
        masked = s.sem("masked")
        max_done = s.sem("max_done")
        exp_done = s.sem("exp_done")
        prob_turned = s.sem("prob_turned")
        prob_copied = s.sem("prob_copied")
        pv_done = s.sem("pv_done")
        rinv_done = s.sem("rinv_done")
        o_done = s.sem("o_done")
        o_turned = s.sem("o_turned")
        o_high = s.sem("o_high")
        o_low = s.sem("o_low")
        block = ctx.enter_context(nc.Block())

        @block.sync
        def _(sp):
            for b in range(B):
                sp.dma_start(R[:, b, :], x[b, :, :]).then_inc(x_loaded, 16)
            for dst, src in ((gamma[:, :], gamma_d), (beta[:, :], beta_d), (posi[:, :], pos_d), (inv[:, :], inv_d),
                             (mask[:, :], causal), (side_bias[:, :], side_bias_d.broadcast_to([P, P])), (DU[:, :], du_d)):
                sp.dma_start(dst, src).then_inc(small_loaded, 16)
            st.loads(sp)

        SMALL = 7 * 16

        @block.gpsimd
        def _(pool):
            norm.pool(pool)
            read.pool(pool)
            for n in range(2 * B):
                dst = (q_tok, k_tok)[n // B][:, n % B, :]
                pool.wait_ge(rope_mult, n + 1)
                pool.tensor_tensor(dst, dst, F[n % 2][:, :], ALU.add).then_inc(rope_done, 1)
            write.pool(pool)

        @block.vector
        def _(dve):
            link = Chain(dve, table_steps)
            dve.wait_ge(x_loaded, 16 * B)
            norm.vector(dve, banks)
            st.begin_vector(dve)
            dve.wait_ge(small_loaded, SMALL)
            link(dve.tensor_copy(posf[:, :], posi[:, :]))
            link(dve.tensor_tensor(ang[:, :, :], posf[:, :].unsqueeze(2).broadcast_to([P, B, HALF]),
                                   inv[:, :].unsqueeze(1).broadcast_to([P, B, HALF]), ALU.mult))
            link(dve.tensor_scalar(kk[:, :, :], ang[:, :, :], 1.0 / TWO_PI, MAGIC, ALU.mult, ALU.add))
            link(dve.tensor_scalar(kk[:, :, :], kk[:, :, :], MAGIC, None, ALU.subtract))
            for part in (C1, C2, C3):
                link(dve.scalar_tensor_tensor(out=ang[:, :, :], in0=kk[:, :, :], scalar=-part, in1=ang[:, :, :],
                                              op0=ALU.mult, op1=ALU.add))
            link(dve.tensor_scalar(sc[:, 1, :, :], ang[:, :, :], np.pi / 2, None, ALU.add))
            link(dve.tensor_scalar(kk[:, :, :], sc[:, 1, :, :], LIMIT, -TWO_PI, ALU.is_gt, ALU.mult))
            link(dve.tensor_tensor(sc[:, 1, :, :], sc[:, 1, :, :], kk[:, :, :], ALU.add))
            link(dve.tensor_copy(sc[:, 0, :, :], ang[:, :, :]))
            link(dve.tensor_scalar(sc[:, 0:2, :, :], sc[:, 0:2, :, :], LIMIT, -LIMIT, ALU.min, ALU.max))
            dve.wait_ge(sin_done, 1)
            link(dve.tensor_scalar(sc[:, 2, :, :], sc[:, 0, :, :], -1.0, None, ALU.mult))

            read.vector_norm(dve)

            for t in range(QKV, WOD - 4):
                st.at_vector(dve, 0, t)
            dve.wait_ge(read.y_turned, 4 * OUTS)
            heads = lambda ap: ap.rearrange("p (h d) -> p h d", d=HALF)
            halves = lambda ap: ap.rearrange("p (h two d) -> p h two d", two=2, d=HALF)

            def rope(n):
                which, b = n // B, n % B
                bank, dst, turn = banks[4 * which + b], (q_tok, k_tok)[which][:, b, :], F[n % 2][:, :]
                dve.wait_ge(st.used, QKV + 4 * (which + 1))
                if n >= 2:
                    dve.wait_ge(rope_done, n - 1)
                dve.tensor_tensor(heads(dst), heads(bank[:, :]),
                                  sc[:, 1, b, :].unsqueeze(1).broadcast_to([P, 2 * NH, HALF]), ALU.mult)
                dve.tensor_tensor(halves(turn)[:, :, 0, :], halves(bank[:, :])[:, :, 1, :],
                                  sc[:, 2, b, :].unsqueeze(1).broadcast_to([P, NH, HALF]), ALU.mult)
                dve.tensor_tensor(halves(turn)[:, :, 1, :], halves(bank[:, :])[:, :, 0, :],
                                  sc[:, 0, b, :].unsqueeze(1).broadcast_to([P, NH, HALF]), ALU.mult)\
                   .then_inc(rope_mult, 1)

            for n in range(2 * B):
                rope(n)
                if 4 <= n:
                    st.at_vector(dve, 0, WOD - 4 + n - 4)
            link_a = Chain(dve, masked)
            for b in range(B):
                dve.wait_ge(scores_done, b + 1)
                if b:
                    dve.wait_ge(prob_turned, b)
                for r in range(4):
                    last = dve.scalar_tensor_tensor(
                        out=S[:, 4 * r:4 * r + 4, :], in0=banks[r][:, :].rearrange("p (c k) -> p c k", c=4),
                        scalar=SCALE, in1=mask[:, :].unsqueeze(1).broadcast_to([P, 4, P]), op0=ALU.mult, op1=ALU.add)
                link_a(last)
                dve.tensor_reduce(nmax[:, :], S[:, :, :], AXX, ALU.max, negate=True).then_inc(max_done, 1)
                dve.wait_ge(exp_done, b + 1)
                dve.reciprocal(rinv[:, :], rsum[:, :]).then_inc(rinv_done, 1)
                dve.wait_ge(rinv_done, b + 1)
                dve.wait_ge(pv_done, b + 1)
                if b:
                    dve.wait_ge(o_turned, b)
                dve.tensor_tensor(O[:, :].rearrange("p (c r d) -> p c r d", c=4, r=4),
                                  banks[4][:, :].rearrange("p (c r d) -> p c r d", c=4, r=4),
                                  rinv[:, :].rearrange("p (r c) -> p c r", r=4).unsqueeze(3).broadcast_to([P, 4, 4, HD]),
                                  ALU.mult).then_inc(o_done, 1)
                dve.wait_ge(o_high, b + 1)
                c = slice(b * P, (b + 1) * P)
                dve.tensor_tensor(OL[:, :, c], banks[5][:, :].rearrange("p (c t) -> p c t", c=4), f32(OH[:, :, c]),
                                  ALU.subtract).then_inc(o_low, 1)
            for t in range(WOD, TILES):
                st.at_vector(dve, 0, t)
            write.vector(dve, banks, lambda e: e.wait_ge(st.used, TILES))

        @block.scalar
        def _(act):
            norm.scalar(act, banks)
            st.begin_scalar(act)
            act.wait_ge(table_steps, 12)
            act.activation(sc[:, 0:2, :, :], sc[:, 0:2, :, :], ACT.Sin).then_inc(sin_done, 1)
            read.scalar_sums(act, banks)
            read.scalar_affine(act, banks)
            for t in range(QKV, WOD):
                st.at_scalar(act, 0, t)
            act.wait_ge(st.used, WOD)
            for b in range(B):
                act.activation(V[:, b, :], banks[b][:, :], ACT.Copy).then_inc(v_read, 1)
            for n in range(2 * B):
                act.wait_ge(qk_turned, n + 1)
                act.activation((QT, KT)[n % 2][:, :, n // 2 * P:(n // 2 + 1) * P],
                               banks[4 + n % 4][:, :].rearrange("p (c t) -> p c t", c=4), ACT.Copy).then_inc(qk_copied, 1)
            for b in range(B):
                act.wait_ge(max_done, b + 1)
                if b:
                    act.wait_ge(rinv_done, b)
                for h in range(NH):
                    last = act.activation(S[:, h, :], S[:, h, :], ACT.Exp, bias=nmax[:, h:h + 1],
                                          accum_out=rsum[:, h:h + 1])
                last.then_inc(exp_done, 1)
                act.wait_ge(prob_turned, b + 1)
                if b:
                    act.wait_ge(pv_done, b)
                for r in range(4):
                    last = act.activation(PT[:, 4 * r:4 * r + 4, :], banks[4 + r][:, :].rearrange("p (c q) -> p c q", c=4),
                                          ACT.Copy)
                last.then_inc(prob_copied, 1)
                act.wait_ge(o_turned, b + 1)
                act.activation(OH[:, :, b * P:(b + 1) * P], banks[5][:, :].rearrange("p (c t) -> p c t", c=4), ACT.Copy)\
                   .then_inc(o_high, 1)
            for t in range(WOD, TILES):
                st.at_scalar(act, 0, t)
            write.scalar(act, banks)

        @block.tensor
        def _(pe):
            norm.tensor(pe, banks)
            pe.wait_ge(norm.lo_done, 4 * B)
            read.tensor_sums(pe, banks)
            pe.wait_ge(read.y_read, 4 * B)
            read.tensor_turn(pe, banks)
            pe.wait_ge(read.y_low, 4 * OUTS)
            for o in range(OUTS):
                use = banks[0:4] if o % 2 == 0 else banks[4:8]
                for k in range(4):
                    st.product_tokens(pe, 0, QKV + 4 * o + k, YH[:, 4 * o + k, :], YL[:, 4 * o + k, :], use, k == 0, k == 3,
                                      (lambda b: pe.wait_ge(rope_mult, b + 1)) if o == 2 and k == 0 else None)
            pe.wait_ge(rope_mult, 2 * B)
            for n in range(2 * B):
                which, b = n % 2, n // 2
                pe.wait_ge(rope_done, which * B + b + 1)
                if n >= 4:
                    pe.wait_ge(qk_copied, n - 3)
                for c in range(4):
                    mm = pe.transpose(banks[4 + n % 4][:, c * P:(c + 1) * P], (q_tok, k_tok)[which][:, b, c * P:(c + 1) * P],
                                      ident[:, :])
                mm.then_inc(qk_turned, 1)

            def scores(b):
                pe.wait_ge(qk_copied, 2 * b + 2)
                if b:
                    pe.wait_ge(max_done, b)
                t = slice(b * P, (b + 1) * P)
                for c in range(4):
                    for r in range(4):
                        f = slice(HD * r, HD * (r + 1))
                        mm = pe.matmul(banks[r][:, c * P:(c + 1) * P], QT[f, c, t], KT[f, c, t], start=True, stop=True)
                mm.then_inc(scores_done, 1)

            pe.wait_ge(v_read, B)
            scores(0)
            for b in range(B):
                pe.wait_ge(qk_copied, 2 * B)
                if b:
                    pe.wait_ge(o_low, b)
                pe.wait_ge(exp_done, b + 1)
                for h in range(NH):
                    mm = pe.transpose(banks[4 + h // 4][:, h % 4 * P:(h % 4 + 1) * P], S[:, h, :], ident[:, :])
                mm.then_inc(prob_turned, 1)
                if b + 1 < B:
                    scores(b + 1)
                pe.wait_ge(prob_copied, b + 1)
                for c in range(4):
                    for r in range(4):
                        f = slice(HD * (4 * c + r), HD * (4 * c + r + 1))
                        mm = pe.matmul(banks[4][:, f], PT[:, 4 * r + c, :], V[:, b, f], start=True, stop=True)
                mm.then_inc(pv_done, 1)
                pe.wait_ge(o_done, b + 1)
                for c in range(4):
                    mm = pe.transpose(banks[5][:, c * P:(c + 1) * P], O[:, c * P:(c + 1) * P], ident[:, :])
                mm.then_inc(o_turned, 1)
            pe.wait_ge(o_low, B)
            write_products(pe, st, 0, WOD, 4, OH, OL, banks)
            write.tensor(pe, banks)


def write_products(pe, st, r, t0, pieces, xh, xl, banks):
    for k in range(pieces):
        st.product_tokens(pe, r, t0 + k, xh[:, k, :], xl[:, k, :], banks[0:4], k == 0, k == pieces - 1)
    for t in range(pieces // 4):
        pe.wait_ge(st.lo_done, r * ROUND + t0 + pieces + t + 1)
        wh, wl = st.WH[(t0 + pieces + t) % PART_SLOTS], st.WL[(t0 + pieces + t) % PART_SLOTS]
        for j in range(4):
            k = 4 * t + j
            w = slice(j * P, (j + 1) * P)
            for b in range(B):
                c = slice(b * P, (b + 1) * P)
                out = banks[4 + b][:, 0:P]
                pe.matmul(out, xh[:, k, c], wh[:, w], start=k == 0, stop=False)
                pe.matmul(out, xh[:, k, c], wl[:, w], start=False, stop=False)
                mm = pe.matmul(out, xl[:, k, c], wh[:, w], start=False, stop=k == pieces - 1)
        mm.then_inc(st.used, 1)


def xattn_mlp(nc, R, H, ident, wstream, gamma_d, beta_d, side_bias_d, du_d):
    OUTS = 2
    M = 2048
    MB = M // NT
    GATE = KD // PIECE
    WOD = GATE + 8 * MB
    TILES = WOD + M // P + M // P // 4

    with ExitStack() as ctx:
        s = Scope(nc, ctx, "m_")
        banks = s.banks()
        XH = s.sb("XH", [P, KD, TOK], F32R)
        XL = s.sb("XL", [P, KD, TOK], F32R)
        st = Stream(s, TILES, wstream)
        YH = s.sb("YH", [P, 4 * OUTS, TOK], F32R)
        YL = s.sb("YL", [P, 4 * OUTS, TOK], F32R)
        Y = s.over("YH", 0, "Y", [P, B, OUTS, XH_])
        F = [s.sb(f"F{n}", [P, TOK]) for n in range(2)]
        gamma = s.sb("gamma", [P, 4 * OUTS])
        beta = s.sb("beta", [P, 4 * OUTS])
        read = Read(s, st, OUTS, XH, XL, Y, YH, YL, F, gamma, beta, ident)
        side_bias = s.sb("side_bias", [P, P])
        DU = s.sb("DU", [9, XH_])
        write = Write(s, H, s.over("YH", 0, "delta", [P, B, XH_]), s.over("YL", 0, "log", [P, B, XH_]),
                      [s.over(x, 4, "ARG_" + x, [P, AC, XH_]) for x in ("YH", "YL")],
                      [s.over(x, 7, "W3_" + x, [P, XH_]) for x in ("YH", "YL")],
                      s.over("XL", 0, "U", [P, AC, XH_]), s.over("XH", 0, "T", [P, AC, XH_]), F, ident, side_bias, DU)
        small_loaded = s.sem("small_loaded")
        x_turned = s.sem("x_turned")
        x_high = s.sem("x_high")
        x_low = s.sem("x_low")
        silu_done = s.sem("silu_done")
        unit_done = s.sem("unit_done")
        unit_high = s.sem("unit_high")
        unit_low = s.sem("unit_low")
        block = ctx.enter_context(nc.Block())

        @block.sync
        def _(sp):
            for dst, src in ((gamma[:, :], gamma_d), (beta[:, :], beta_d),
                             (side_bias[:, :], side_bias_d.broadcast_to([P, P])), (DU[:, :], du_d)):
                sp.dma_start(dst, src).then_inc(small_loaded, 16)
            st.loads(sp)

        @block.gpsimd
        def _(pool):
            read.pool(pool)
            write.pool(pool)

        def part(n):
            b, g = n // 4, n % 4
            return slice(None), slice(4 * g, 4 * g + 4), slice(b * P, (b + 1) * P)

        @block.vector
        def _(dve):
            st.begin_vector(dve)
            for n in range(4 * B):
                dve.wait_ge(x_high, n + 1)
                dve.tensor_tensor(XL[part(n)], banks[n % 8][:, :].rearrange("p (c t) -> p c t", c=4), f32(XH[part(n)]),
                                  ALU.subtract).then_inc(x_low, 1)
            read.vector_norm(dve)

            def unit(m, c):
                dve.wait_ge(silu_done, 4 * m + c + 1)
                dve.tensor_tensor(F[c % 2][:, :], banks[4 + c][:, :], F[c % 2][:, :], ALU.mult).then_inc(unit_done, 1)

            def low_of_unit(m, c):
                dve.wait_ge(unit_high, 4 * m + c + 1)
                dve.tensor_tensor(XL[:, bass.ds(4 * m + c, 1), :].rearrange("p a n -> p (a n)"), F[c % 2][:, :],
                                  f32(XH[:, bass.ds(4 * m + c, 1), :]).rearrange("p a n -> p (a n)"),
                                  ALU.subtract).then_inc(unit_low, 1)

            with dve.Fori(0, MB) as m:
                for t in range(8):
                    st.at_vector(dve, m, GATE + t)
                dve.wait_ge(st.used, m * ROUND + GATE + 8)
                for c in range(4):
                    unit(m, c)
                    low_of_unit(m, c)
            for t in range(WOD, TILES):
                st.at_vector(dve, 0, t)
            dve.wait_ge(small_loaded, 64)
            write.vector(dve, banks, lambda e: e.wait_ge(st.used, TILES))
            for b in range(B):
                dve.tensor_tensor(R[:, b, :], R[:, b, :], H[:, b, :], ALU.add)

        def high_of_unit(act, m, c):
            act.wait_ge(unit_done, 4 * m + c + 1)
            act.activation(XH[:, bass.ds(4 * m + c, 1), :].rearrange("p a n -> p (a n)"), F[c % 2][:, :], ACT.Copy)\
               .then_inc(unit_high, 1)

        @block.scalar
        def _(act):
            st.begin_scalar(act)
            for n in range(4 * B):
                act.wait_ge(x_turned, n + 1)
                act.activation(XH[part(n)], banks[n % 8][:, :].rearrange("p (c t) -> p c t", c=4), ACT.Copy)\
                   .then_inc(x_high, 1)
            act.wait_ge(small_loaded, 64)
            read.scalar_sums(act, banks)
            read.scalar_affine(act, banks, turned_first=4 * OUTS)
            with act.Fori(0, MB) as m:
                for t in range(8):
                    st.at_scalar(act, m, GATE + t)
                act.wait_ge(st.used, m * ROUND + GATE + 8)
                for c in range(4):
                    if c >= 2:
                        act.wait_ge(unit_low, 4 * m + c - 1)
                    act.activation(F[c % 2][:, :], banks[c][:, :], ACT.Silu).then_inc(silu_done, 1)
                    if c >= 1:
                        high_of_unit(act, m, c - 1)
                high_of_unit(act, m, 3)
            for t in range(WOD, TILES):
                st.at_scalar(act, 0, t)
            write.scalar(act, banks)

        @block.tensor
        def _(pe):
            for n in range(4 * B):
                b, g = n // 4, n % 4
                if n >= 8:
                    pe.wait_ge(x_low, n - 7)
                for c in range(4):
                    mm = pe.transpose(banks[n % 8][:, c * P:(c + 1) * P], H[:, b, (4 * g + c) * P:(4 * g + c + 1) * P],
                                      ident[:, :])
                mm.then_inc(x_turned, 1)
            pe.wait_ge(x_low, 4 * B)
            read.tensor_sums(pe, banks)
            pe.wait_ge(read.y_read, 4 * B)
            read.tensor_turn(pe, banks)
            pe.wait_ge(read.y_low, 4 * OUTS)

            def block_of(m, first):
                for o in range(2):
                    def free(c):
                        if not first:
                            pe.wait_ge((silu_done, unit_done)[o], 4 * m - 4 + c + 1)
                    for k in range(4):
                        st.product_features(pe, m, GATE + 4 * o + k, YH[:, 4 * o + k, :], YL[:, 4 * o + k, :],
                                            banks[4 * o:4 * o + 4], k == 0, k == 3, free if k == 0 else None)

            block_of(0, True)
            with pe.Fori(1, MB) as m:
                block_of(m, False)
            pe.wait_ge(unit_low, 4 * MB)
            write_products(pe, st, 0, WOD, M // P, XH, XL, banks)
            write.tensor(pe, banks)


def routed_ffn(nc, R, ident, wstream, router, iota, bias, out):
    EXPERTS = 16
    RANK = 64
    SCALING = 0.5
    AR = RANK + EXPERTS
    KE = EXPERTS * RANK // P
    NB = D // NT
    PER = KD + KE
    TILES = NB * PER
    BIG = 1024.0

    with ExitStack() as ctx:
        s = Scope(nc, ctx, "f_")
        banks = s.banks()
        EH = s.sb("EH", [P, KE, TOK], F32R)
        EL = s.sb("EL", [P, KE, TOK], F32R)
        xn = [s.sb(f"xn{n}", [P, D]) for n in range(2)]
        ET = [xn[n][:, 0:EXPERTS * RANK] for n in range(2)]
        norm = Norm(s, R, ident, [x[:, :] for x in xn])
        st = Stream(s, TILES, wstream)
        A = s.sb("A", [P, KD, AR])
        AH = s.sb("AH", [P, KD, AR], F32R)
        AL = s.sb("AL", [P, KD, AR], F32R)
        bias_all = s.sb("bias", [P, D])
        io = s.sb("iota", [P, EXPERTS])
        res = s.sb("res", [P, B, AR])
        pr = s.sb("probs", [P, B, EXPERTS])
        one = [s.sb(f"one{n}", [P, B, EXPERTS]) for n in range(2)]
        key = s.sb("key", [P, B, EXPERTS])
        wt = s.sb("weights", [P, B, EXPERTS])
        small = s.sb("small", [P, 8, B])

        small_loaded = s.sem("small_loaded")
        a_high = s.sem("a_high")
        a_low = s.sem("a_low")
        bias_added = s.sem("bias_added")
        res_done = s.sem("res_done")
        steps = s.sem("routing_steps")
        shifted = s.sem("logits_shifted")
        exp_done = s.sem("exp_done")
        rows_done = s.sem("rows_done")
        rows_turned = s.sem("rows_turned")
        rows_high = s.sem("rows_high")
        rows_low = s.sem("rows_low")
        out_added = s.sem("out_added")
        out_stored = s.sem("out_stored")
        block = ctx.enter_context(nc.Block())

        ROUNDS = PER // ROUND
        bce = lambda ap: ap.unsqueeze(2).broadcast_to([P, B, EXPERTS])

        @block.sync
        def _(sp):
            sp.dma_start(A[:, :, :], router).then_inc(small_loaded, 16)
            sp.dma_start(io[:, :], iota).then_inc(small_loaded, 16)
            sp.dma_start(bias_all[:, :], bias.broadcast_to([P, D])).then_inc(small_loaded, 16)
            st.loads(sp)

        @block.gpsimd
        def _(pool):
            norm.pool(pool)
            pool.wait_ge(small_loaded, 48)
            for b in range(B):
                pool.wait_ge(norm.scaled, b + 1)
                pool.tensor_tensor(R[:, b, :], R[:, b, :], bias_all[:, :], ALU.add).then_inc(bias_added, 1)

        @block.vector
        def _(dve):
            link = Chain(dve, steps)
            norm.vector(dve, banks)
            dve.wait_ge(a_high, 1)
            dve.tensor_tensor(AL[:, :, :], A[:, :, :], f32(AH[:, :, :]), ALU.subtract).then_inc(a_low, 1)
            st.begin_vector(dve)

            dve.wait_ge(res_done, 1)
            for b in range(B):
                last = dve.tensor_copy(res[:, b, :], banks[b][:, 0:AR])
            link(last)
            logits = res[:, :, RANK:AR]
            link(dve.tensor_reduce(small[:, 0, :], logits, AXX, ALU.max))
            dve.tensor_tensor(pr[:, :, :], logits, bce(small[:, 0, :]), ALU.subtract).then_inc(shifted, 1)
            dve.wait_ge(exp_done, 1)
            link(dve.tensor_reduce(small[:, 1, :], pr[:, :, :], AXX, ALU.add))
            link(dve.reciprocal(small[:, 2, :], small[:, 1, :]))
            link(dve.tensor_tensor(pr[:, :, :], pr[:, :, :], bce(small[:, 2, :]), ALU.mult))
            for n in range(2):
                top = small[:, 3 + n, :]
                link(dve.tensor_reduce(top, pr[:, :, :], AXX, ALU.max))
                link(dve.tensor_tensor(key[:, :, :], pr[:, :, :], bce(top), ALU.is_lt))
                link(dve.scalar_tensor_tensor(out=key[:, :, :], in0=key[:, :, :], scalar=BIG,
                                              in1=io[:, :].unsqueeze(1).broadcast_to([P, B, EXPERTS]),
                                              op0=ALU.mult, op1=ALU.add))
                link(dve.tensor_reduce(small[:, 5, :], key[:, :, :], AXX, ALU.min))
                link(dve.tensor_tensor(one[n][:, :, :], key[:, :, :], bce(small[:, 5, :]), ALU.is_equal))
                if n == 0:
                    link(dve.scalar_tensor_tensor(out=pr[:, :, :], in0=one[0][:, :, :], scalar=-2.0,
                                                  in1=pr[:, :, :], op0=ALU.mult, op1=ALU.add))
            link(dve.tensor_tensor(small[:, 6, :], small[:, 3, :], small[:, 4, :], ALU.add))
            link(dve.tensor_scalar(small[:, 6, :], small[:, 6, :], 1e-6, None, ALU.add))
            link(dve.reciprocal(small[:, 7, :], small[:, 6, :]))
            link(dve.tensor_scalar(small[:, 7, :], small[:, 7, :], SCALING, None, ALU.mult))
            for n in range(2):
                link(dve.tensor_tensor(small[:, 3 + n, :], small[:, 3 + n, :], small[:, 7, :], ALU.mult))
                link(dve.tensor_tensor(one[n][:, :, :], one[n][:, :, :], bce(small[:, 3 + n, :]), ALU.mult))
            link(dve.tensor_tensor(wt[:, :, :], one[0][:, :, :], one[1][:, :, :], ALU.add))

            def rows(b):
                if b >= 2:
                    dve.wait_ge(rows_turned, 2 * (b - 1))
                dve.tensor_tensor(ET[b % 2].rearrange("p (e r) -> p e r", e=EXPERTS),
                                  wt[:, b, :].unsqueeze(2).broadcast_to([P, EXPERTS, RANK]),
                                  res[:, b, 0:RANK].unsqueeze(1).broadcast_to([P, EXPERTS, RANK]),
                                  ALU.mult).then_inc(rows_done, 1)

            def rows_low_parts(n):
                b, g = n // 2, n % 2
                dve.wait_ge(rows_high, n + 1)
                part = (slice(None), slice(4 * g, 4 * g + 4), slice(b * P, (b + 1) * P))
                dve.tensor_tensor(EL[part], banks[4 + n % 4][:, :].rearrange("p (c t) -> p c t", c=4), f32(EH[part]),
                                  ALU.subtract).then_inc(rows_low, 1)

            def add_output(r, t, n, b):
                dve.wait_ge(st.used, r * ROUND + t + 1)
                o = R[:, b, bass.ds(n * NT, NT)]
                dve.tensor_tensor(o, banks[b][:, :], o, ALU.add).then_inc(out_added, 1)

            for t in range(PER):
                st.at_vector(dve, 0, t)
                if t < B:
                    rows(t)
                if 2 <= t < 2 + 2 * B:
                    rows_low_parts(t - 2)
            dve.wait_ge(bias_added, B)
            for b in range(B):
                add_output(0, PER - 1, 0, b)

            def block_of(n):
                for t in range(PER):
                    st.at_vector(dve, n * ROUNDS, t)
                for b in range(B):
                    add_output(n * ROUNDS, PER - 1, n, b)

            with dve.Fori(1, NB - 1) as n:
                block_of(n)
            block_of(NB - 1)

        @block.scalar
        def _(act):
            norm.scalar(act, banks)
            act.wait_ge(small_loaded, 48)
            act.activation(AH[:, :, :], A[:, :, :], ACT.Copy).then_inc(a_high, 1)
            st.begin_scalar(act)
            act.wait_ge(shifted, 1)
            act.activation(pr[:, :, :], pr[:, :, :], ACT.Exp).then_inc(exp_done, 1)

            def rows_high_parts(n):
                b, g = n // 2, n % 2
                act.wait_ge(rows_turned, n + 1)
                act.activation(EH[:, 4 * g:4 * g + 4, b * P:(b + 1) * P],
                               banks[4 + n % 4][:, :].rearrange("p (c t) -> p c t", c=4), ACT.Copy).then_inc(rows_high, 1)

            def store(n):
                act.wait_ge(out_added, (n + 1) * B)
                act.dma_start(out[:, :, bass.ds(n * NT, NT)].rearrange("b p d -> p b d"),
                              R[:, :, bass.ds(n * NT, NT)]).then_inc(out_stored, 16)

            for t in range(PER):
                st.at_scalar(act, 0, t)
                if 2 <= t < 2 + 2 * B:
                    rows_high_parts(t - 2)

            def block_of(n):
                for t in range(PER):
                    st.at_scalar(act, n * ROUNDS, t)
                    if t == 4:
                        store(n - 1)

            with act.Fori(1, NB - 1) as n:
                block_of(n)
            block_of(NB - 1)
            store(NB - 1)
            act.wait_ge(out_stored, 16 * NB)

        @block.tensor
        def _(pe):
            XH, XL = norm.XH, norm.XL
            norm.tensor(pe, banks)
            pe.wait_ge(norm.lo_done, 4 * B)
            pe.wait_ge(a_low, 1)
            for b in range(B):
                c = slice(b * P, (b + 1) * P)
                for k in range(KD):
                    pe.matmul(banks[b][:, 0:AR], XH[:, k, c], AH[:, k, :], start=k == 0, stop=False)
                    pe.matmul(banks[b][:, 0:AR], XH[:, k, c], AL[:, k, :], start=False, stop=False)
                    mm = pe.matmul(banks[b][:, 0:AR], XL[:, k, c], AH[:, k, :], start=False, stop=k == KD - 1)
            mm.then_inc(res_done, 1)

            def turn_rows(n):
                b, g = n // 2, n % 2
                pe.wait_ge(rows_done, b + 1)
                if n >= 4:
                    pe.wait_ge(rows_low, n - 3)
                for c in range(4):
                    mm = pe.transpose(banks[4 + n % 4][:, c * P:(c + 1) * P], ET[b % 2][:, (4 * g + c) * P:(4 * g + c + 1) * P],
                                      ident[:, :])
                mm.then_inc(rows_turned, 1)

            def products(r, t, free):
                xh, xl = (XH[:, t, :], XL[:, t, :]) if t < KD else (EH[:, t - KD, :], EL[:, t - KD, :])
                st.product_tokens(pe, r, t, xh, xl, banks[0:4], t == 0, t == PER - 1, free if t == 0 else None)

            pe.wait_ge(steps, 1)
            for t in range(PER):
                if 2 <= t < 2 + 2 * B:
                    turn_rows(t - 2)
                if t == KD:
                    pe.wait_ge(rows_low, 2 * B)
                products(0, t, None)
            with pe.Fori(1, NB) as n:
                for t in range(PER):
                    products(n * ROUNDS, t, lambda b: pe.wait_ge(out_added, (n - 1) * B + b + 1))


def _tiles(w, k, n):
    t = w[k * P:(k + 1) * P, n * NT:(n + 1) * NT]
    return t if t.shape[1] == NT else np.pad(t, ((0, 0), (0, NT - t.shape[1])))


def _stream(tiles):
    tiles = list(tiles) + [np.zeros_like(tiles[0])] * (-len(tiles) % ROUND)
    return np.ascontiguousarray(np.stack(tiles).reshape(-1, GROUP, P, NT).transpose(0, 2, 1, 3))


def _read_tiles(w):
    h, outs, c = w.shape
    full = np.zeros((h // 32, 32, c, P // 32, 32), w.dtype)
    for i in range(32):
        full[:, i, :, :outs, i] = w.reshape(h // 32, 32, outs, c)[:, i].transpose(0, 2, 1)
    pieces = full.reshape(KD, P, P)
    return list(pieces.reshape(KD // PIECE, PIECE, P, P).transpose(0, 2, 1, 3).reshape(-1, P, NT))


def _side(wod, wab):
    n = wod.shape[1]
    A = wab[:RH * AC]
    Bp = wab[RH * AC:2 * RH * AC]
    skip = wab[2 * RH * AC:]
    low = wod[XH_:]
    return np.concatenate([low, np.zeros((RH - low.shape[0], n), wod.dtype), skip, A, Bp], 0).T


def _side_tiles(wod, wab):
    w = _side(wod, wab)
    k = w.shape[0] // P
    return list(w.reshape(k // 4, 4, P, P).transpose(0, 2, 1, 3).reshape(k // 4, P, NT))


def _side_bias(b):
    one = np.zeros(RH, b.dtype)
    one[8] = 1.0
    return np.concatenate([one, b[2 * RH * AC:], b[:2 * RH * AC]]).reshape(1, P)


def _columns(g):
    return np.ascontiguousarray(g.reshape(-1, P).T)


def _layouts(i):
    x = lambda name: np.asarray(i["L0_xattn_" + name])
    out = {"x": np.asarray(i["x"]), "pos": np.ascontiguousarray(np.asarray(i["pos_BxS"]).T)}
    wod = x("attn_wod_w")
    out["a_stream"] = _stream(_read_tiles(x("attn_read_w")) + [_tiles(x("qkv_w")[o].T, k, 0) for o in range(3) for k in range(4)]
                              + [_tiles(wod[:XH_].T, k, 0) for k in range(4)] + _side_tiles(wod, x("attn_wab_w")))
    ctx = np.asarray(i["ctx_1024"])
    wod = x("mlp_wod_w")
    out["m_stream"] = _stream(_read_tiles(x("mlp_read_w")) + [_tiles(ctx[o].T, k, n) for n in range(4) for o in range(2) for k in range(4)]
                              + [_tiles(wod[:XH_].T, k, 0) for k in range(16)] + _side_tiles(wod, x("mlp_wab_w")))
    for p, q in (("a", "attn"), ("m", "mlp")):
        out[p + "_gamma"] = _columns(x(q + "_read_g"))
        out[p + "_beta"] = _columns(x(q + "_read_b"))
        out[p + "_side_bias"] = _side_bias(x(q + "_wab_b"))
        out[p + "_du"] = np.concatenate([x(q + "_du_w").T, x(q + "_du_b")[None]], 0)
    order = [(m, k, n) for m in "kv" for n in range(2) for k in range(KD)] + [("q", k, 0) for k in range(KD)]
    for step in range(1, 9):
        order += [("q", k, step) for k in range(KD) if step < 8]
        order += [("o", 4 * step - 4 + j, n) for n in range(4) for j in range(4)]
    w = {m: np.asarray(i["L0_attn_qw_" + m]) for m in "qkvo"}
    sc = {m: np.asarray(i["L0_attn_scales_" + m]) for m in "qkvo"}
    out["g_stream"] = _stream([_tiles(w[m], k, n) for m, k, n in order])
    out["g_scales"] = np.stack([sc[m][k, n * NT:(n + 1) * NT] for m, k, n in order]).reshape(-1, GROUP * NT)
    base = np.concatenate([np.asarray(i["L0_ffn_base_w"]).T, np.asarray(i["L0_ffn_B"]).transpose(0, 2, 1).reshape(-1, D)], 0)
    out["f_stream"] = _stream([_tiles(base, k, n) for n in range(D // NT) for k in range(base.shape[0] // P)])
    router = np.concatenate([np.asarray(i["L0_ffn_A"]), np.asarray(i["L0_ffn_router_w"])], 0).T
    out["f_router"] = np.ascontiguousarray(router.reshape(KD, P, -1).transpose(1, 0, 2))
    out["f_bias"] = np.asarray(i["L0_ffn_base_b"]).reshape(1, D)

    half = 16
    inv = np.float32(1.0) / np.float32(10000.0) ** (np.arange(half, dtype=np.float32) / np.float32(half))
    out["x_inv"] = np.tile(inv.astype(np.float32), (P, 1))
    inv = (np.float32(1.0) / np.float32(10000.0) ** (np.arange(0, P, 2, dtype=np.float32) / np.float32(P))).astype(np.float32)
    ang = (np.arange(P, dtype=np.float32)[None, :] * inv[:, None]).astype(np.float64)
    cos, sin = np.cos(ang), np.sin(ang)
    out["g_rope"] = np.stack([np.concatenate([cos, cos]), np.concatenate([sin, -sin])], 1).astype(np.float32)
    out["causal"] = np.where(np.tril(np.ones((P, P))) > 0, 0.0, -3e38).astype(np.float32)
    out["iota"] = np.tile(np.arange(16, dtype=np.float32), (P, 1))
    out["ident"] = np.eye(P, dtype=np.float32)
    return {k: np.ascontiguousarray(v) for k, v in out.items()}


def perceiver_layer(nc, t, out):
    with ExitStack() as ctx:
        R = ctx.enter_context(nc.sbuf_tensor("residual", [P, B, D], F32))
        ident = ctx.enter_context(nc.sbuf_tensor("identity", [P, P], F32))
        ident_loaded = ctx.enter_context(nc.semaphore("ident_loaded"))
        with nc.Block() as block:
            @block.sync
            def _(sp):
                sp.dma_start(ident[:, :], t["ident"]).then_inc(ident_loaded, 16)
                sp.wait_ge(ident_loaded, 16)

        with nc.sbuf_tensor("hidden", [P, B, D], F32) as H:
            xattn_attention(nc, R, H, ident, t["x"], t["a_stream"], t["a_gamma"], t["a_beta"], t["pos"], t["x_inv"],
                            t["causal"], t["a_side_bias"], t["a_du"])
            xattn_mlp(nc, R, H, ident, t["m_stream"], t["m_gamma"], t["m_beta"], t["m_side_bias"], t["m_du"])
        grouped_query_attention(nc, R, ident, t["g_stream"], t["g_scales"], t["g_rope"], t["causal"])
        routed_ffn(nc, R, ident, t["f_stream"], t["f_router"], t["iota"], t["f_bias"], out)


def kernel(**inputs):
    import concourse.bacc as bacc
    from concourse.bass_utils import run_bass_kernel_spmd

    nc = bacc.Bacc("TRN2", target_bir_lowering=False, num_devices=1)
    arrays = _layouts(inputs)
    tensors = {n: nc.dram_tensor("in_" + n, a.shape, mybir.dt.from_np(a.dtype), kind="ExternalInput").ap() for n, a in arrays.items()}
    out = nc.dram_tensor("out", (B, P, D), F32, kind="ExternalOutput").ap()
    perceiver_layer(nc, tensors, out)
    r = run_bass_kernel_spmd(nc, [{"in_" + n: a for n, a in arrays.items()}], core_ids=[0])
    return r.results[0]["out"]
```

```python
import numpy as np
import concourse.bass as bass
from concourse import mybir
from contextlib import ExitStack

F32 = mybir.dt.float32
F32R = mybir.dt.float32r
I32 = mybir.dt.int32
ALU = mybir.AluOpType
ACT = mybir.ActivationFunctionType
AXX = mybir.AxisListType.X

P = 128
B = 4
D = 2048
TOK = B * P
NT = 512
KD = D // P
EPS = 1e-5
GROUP = 2
RAW_SLOTS = 4
SCALE_SLOTS = 2
PART_SLOTS = 4


class Chain:

    def __init__(self, eng, sem, base=0):
        self.eng, self.sem, self.base, self.n = eng, sem, base, 0

    def __call__(self, ins):
        self.n += 1
        ins.then_inc(self.sem, 1)
        self.eng.wait_ge(self.sem, self.base + self.n)
        return ins


class Scope:

    def __init__(self, nc, ctx, prefix):
        self.nc, self.ctx, self.prefix, self.at, self.sems = nc, ctx, prefix, {}, []
        ctx.callback(self.end)

    def sb(self, name, shape, dt=F32):
        self.at[name] = -(-self.nc.sbuf_base // 32) * 32
        return self.ctx.enter_context(self.nc.sbuf_tensor(self.prefix + name, shape, dt))

    def over(self, host, row, name, shape, dt=F32):
        return self.nc.alloc_sbuf_tensor_at(self.prefix + name, shape, dt, offset=self.at[host] + row * 4 * NT)

    def banks(self):
        return [self.ctx.enter_context(self.nc.psum_tensor(f"{self.prefix}bank{i}", [P, NT], F32)) for i in range(8)]

    def sem(self, name):
        self.sems.append(self.nc.alloc_semaphore(name=self.prefix + name))
        return self.sems[-1]

    def end(self):
        self.nc.clear_and_free_semaphores(self.sems)
        self.nc.all_engine_barrier()


def f32(ap):
    return ap.bitcast(F32)


ROUND = RAW_SLOTS * GROUP
LEAD = 2
SSM_EPS = 1e-5
ZERO = 8.0


class Turned:

    def __init__(self, s, rows, ident):
        self.rows, self.ident = rows, ident
        self.XH = s.sb("XH", [P, KD, TOK], F32R)
        self.XL = s.sb("XL", [P, KD, TOK], F32R)
        self.turned = s.sem("x_turned")
        self.hi_done = s.sem("x_hi_done")
        self.lo_done = s.sem("x_lo_done")

    def part(self, x, b, g):
        return x[:, 4 * g:4 * g + 4, b * P:(b + 1) * P]

    def free(self, eng, n):
        eng.wait_ge(self.lo_done, n + 1)

    def turn(self, eng, banks, b):
        for g in range(4):
            n = 4 * b + g
            bank = banks[n % len(banks)]
            if n >= len(banks):
                self.free(eng, n - len(banks))
            for c in range(4):
                last = eng.transpose(bank[:, c * P:(c + 1) * P],
                                     self.rows[b % len(self.rows)][:, (4 * g + c) * P:(4 * g + c + 1) * P], self.ident[:, :])
            last.then_inc(self.turned, 1)

    def high_parts(self, eng, banks, b):
        for g in range(4):
            n = 4 * b + g
            eng.wait_ge(self.turned, n + 1)
            eng.activation(self.part(self.XH, b, g), banks[n % len(banks)][:, :].rearrange("p (c t) -> p c t", c=4),
                           ACT.Copy).then_inc(self.hi_done, 1)

    def low_parts(self, eng, banks, b):
        for g in range(4):
            n = 4 * b + g
            eng.wait_ge(self.hi_done, n + 1)
            eng.tensor_tensor(self.part(self.XL, b, g), banks[n % len(banks)][:, :].rearrange("p (c t) -> p c t", c=4),
                              f32(self.part(self.XH, b, g)), ALU.subtract).then_inc(self.lo_done, 1)


class Copied(Turned):

    def __init__(self, s, rows, ident):
        Turned.__init__(self, s, rows, ident)
        self.XT = s.over("XH", 0, "XT", [P, KD, TOK])

    def free(self, eng, n):
        eng.wait_ge((self.hi_done, self.lo_done)[n % 2], n // 2 + 1)

    def copy(self, eng, banks, b, odd):
        for g in (odd, odd + 2):
            n = 4 * b + g
            src = banks[n % len(banks)][:, :].rearrange("p (c t) -> p c t", c=4)
            eng.wait_ge(self.turned, n + 1)
            if odd:
                eng.tensor_copy(self.part(self.XT, b, g), src).then_inc(self.lo_done, 1)
            else:
                eng.activation(self.part(self.XT, b, g), src, ACT.Copy).then_inc(self.hi_done, 1)


class Norm(Turned):

    def __init__(self, s, R, ident, rows):
        Turned.__init__(self, s, rows, ident)
        self.R = R
        self.stats = s.sb("ln_stats", [P, B, 4, 6])
        self.mv = s.sb("ln_mv", [P, B, 2])
        self.veps = s.sb("ln_veps", [P, B])
        self.rstd = s.sb("ln_rstd", [P, B])
        self.nhalf = s.sb("ln_nhalf", [P, 1])
        self.stats_done = s.sem("ln_stats_done")
        self.var_done = s.sem("ln_var_done")
        self.rstd_steps = s.sem("ln_rstd_steps")
        self.scaled = s.sem("ln_scaled")

    def pool(self, eng):
        eng.memset(self.nhalf[:, :], -0.5).then_inc(self.rstd_steps, 1)
        for b in range(B):
            one = slice(b, b + 1)
            eng.wait_ge(self.var_done, b + 1)
            eng.tensor_scalar(self.veps[:, one], self.mv[:, b, 1:2], EPS, None, ALU.add).then_inc(self.rstd_steps, 1)
            eng.wait_ge(self.rstd_steps, 2 * b + 2)
            eng.tensor_tensor(self.rstd[:, one], self.veps[:, one], self.nhalf[:, :], ALU.pow).then_inc(self.rstd_steps, 1)

    def moments(self, eng, b):
        for c in range(4):
            last = eng.bn_stats(self.stats[:, b, c, :], self.R[:, b, c * NT:(c + 1) * NT])
        last.then_inc(self.stats_done, 1)
        eng.wait_ge(self.stats_done, b + 1)
        eng.bn_aggr(self.mv[:, b, :], self.stats[:, b, :, :].rearrange("p c s -> p (c s)")).then_inc(self.var_done, 1)

    def scale(self, eng, b):
        eng.wait_ge(self.var_done, b + 1)
        eng.wait_ge(self.rstd_steps, 2 * b + 3)
        if b >= len(self.rows):
            eng.wait_ge(self.turned, 4 * (b + 1 - len(self.rows)))
        eng.tensor_scalar(self.rows[b % len(self.rows)], self.R[:, b, :], self.mv[:, b, 0:1], self.rstd[:, b:b + 1],
                          ALU.subtract, ALU.mult).then_inc(self.scaled, 1)

    def vector(self, eng, banks):
        self.moments(eng, 0)
        for b in range(B):
            if b + 1 < B:
                self.moments(eng, b + 1)
            self.scale(eng, b)
            if b >= 1:
                self.low_parts(eng, banks, b - 1)
        self.low_parts(eng, banks, B - 1)

    def tensor(self, eng, banks):
        for b in range(B):
            eng.wait_ge(self.scaled, b + 1)
            self.turn(eng, banks, b)

    def scalar(self, eng, banks):
        for b in range(B):
            self.high_parts(eng, banks, b)


class CopiedNorm(Copied, Norm):

    def __init__(self, s, R, ident, rows):
        Norm.__init__(self, s, R, ident, rows)
        self.XT = s.over("XH", 0, "XT", [P, KD, TOK])


class Stream:

    def __init__(self, s, tiles, dram, scales=None):
        self.tiles, self.dram, self.scales = tiles, dram, scales
        self.raw = [s.sb(f"raw{n}", [P, GROUP, NT], I32 if scales is not None else F32) for n in range(RAW_SLOTS)]
        if scales is not None:
            self.scale = [s.sb(f"scale{n}", [P, GROUP * NT]) for n in range(SCALE_SLOTS)]
            self.scale_loaded = [s.sem(f"scale_loaded{n}") for n in range(SCALE_SLOTS)]
            self.scaled = s.sem("tile_scaled")
        self.WH = [s.sb(f"WH{n}", [P, NT], F32R) for n in range(PART_SLOTS)]
        self.WL = [s.sb(f"WL{n}", [P, NT], F32R) for n in range(PART_SLOTS)]
        self.raw_loaded = [s.sem(f"raw_loaded{n}") for n in range(RAW_SLOTS)]
        self.hi_done = s.sem("tile_hi_done")
        self.lo_done = s.sem("tile_lo_done")
        self.used = s.sem("tile_used")

    def load_round(self, eng, r, first):
        for g in range(RAW_SLOTS):
            if not first:
                eng.wait_ge(self.lo_done, r * ROUND + (g + 1) * GROUP - ROUND)
            q = r * RAW_SLOTS + g
            eng.dma_start(self.raw[g][:, :, :], self.dram[bass.ds(q, 1), :, :, :].rearrange("a p t n -> (a p) t n"))\
               .then_inc(self.raw_loaded[g], 16)
            if self.scales is not None:
                if not first or g >= SCALE_SLOTS:
                    eng.wait_ge(self.scaled, r * ROUND + (g + 1 - SCALE_SLOTS) * GROUP)
                eng.dma_start(self.scale[g % SCALE_SLOTS][:, :],
                              self.scales[bass.ds(q, 1), :].broadcast_to([P, GROUP * NT]))\
                   .then_inc(self.scale_loaded[g % SCALE_SLOTS], 16)

    def loads(self, eng):
        self.load_round(eng, 0, True)
        rounds = -(-self.tiles // ROUND)
        with eng.Fori(1, rounds) as r:
            self.load_round(eng, r, False)
        for loaded in self.raw_loaded:
            eng.wait_ge(loaded, 16 * rounds)

    def w(self, t):
        raw = self.raw[t % ROUND // GROUP][:, t % GROUP, :]
        return raw.bitcast(F32) if self.scales is not None else raw

    def dequantise(self, eng, r, t):
        g = t % ROUND // GROUP
        if t % GROUP == 0:
            eng.wait_ge(self.raw_loaded[g], (r + t // ROUND) * 16 + 16)
            eng.wait_ge(self.scale_loaded[g % SCALE_SLOTS], (r + t // ROUND) * 32 + 16 * (g // SCALE_SLOTS + 1))
        eng.scalar_tensor_tensor(out=self.w(t), in0=self.raw[g][:, t % GROUP, :], scalar=-ZERO,
                                 in1=self.scale[g % SCALE_SLOTS][:, t % GROUP * NT:(t % GROUP + 1) * NT],
                                 op0=ALU.add, op1=ALU.mult).then_inc(self.scaled, 1)

    def high(self, eng, r, t):
        if self.scales is not None:
            eng.wait_ge(self.scaled, r * ROUND + t + 1)
        elif t % GROUP == 0:
            eng.wait_ge(self.raw_loaded[t % ROUND // GROUP], (r + t // ROUND) * 16 + 16)
        if not isinstance(r, int) or r * ROUND + t >= PART_SLOTS:
            eng.wait_ge(self.used, r * ROUND + t + 1 - PART_SLOTS)
        eng.activation(self.WH[t % PART_SLOTS][:, :], self.w(t), ACT.Copy).then_inc(self.hi_done, 1)

    def low(self, eng, r, t):
        eng.wait_ge(self.hi_done, r * ROUND + t + 1)
        eng.tensor_tensor(self.WL[t % PART_SLOTS][:, :], self.w(t), f32(self.WH[t % PART_SLOTS][:, :]),
                          ALU.subtract).then_inc(self.lo_done, 1)


    def begin_vector(self, eng):
        for t in range(LEAD + 1):
            if self.scales is not None:
                self.dequantise(eng, 0, t)
            if t:
                self.low(eng, 0, t - 1)

    def at_vector(self, eng, r, t):
        if not isinstance(r, int) or r * ROUND + t + LEAD + 1 < self.tiles:
            if self.scales is not None:
                self.dequantise(eng, r, t + LEAD + 1)
        if not isinstance(r, int) or r * ROUND + t + LEAD < self.tiles:
            self.low(eng, r, t + LEAD)

    def begin_scalar(self, eng):
        for t in range(LEAD):
            self.high(eng, 0, t)

    def at_scalar(self, eng, r, t):
        if not isinstance(r, int) or r * ROUND + t + LEAD < self.tiles:
            self.high(eng, r, t + LEAD)


    def product_features(self, eng, r, t, xh, xl, banks, first, last, free=None):
        eng.wait_ge(self.lo_done, r * ROUND + t + 1)
        wh, wl = self.WH[t % PART_SLOTS], self.WL[t % PART_SLOTS]
        for j, bank in enumerate(banks):
            if free:
                free(j)
            c = slice(j * P, (j + 1) * P)
            eng.matmul(bank[:, :], wh[:, c], xh, start=first, stop=False)
            eng.matmul(bank[:, :], wh[:, c], xl, start=False, stop=False)
            mm = eng.matmul(bank[:, :], wl[:, c], xh, start=False, stop=last)
        mm.then_inc(self.used, 1)

    def product_tokens(self, eng, r, t, xh, xl, banks, first, last, free=None):
        eng.wait_ge(self.lo_done, r * ROUND + t + 1)
        wh, wl = self.WH[t % PART_SLOTS], self.WL[t % PART_SLOTS]
        for b, bank in enumerate(banks):
            if free:
                free(b)
            c = slice(b * P, (b + 1) * P)
            eng.matmul(bank[:, :], xh[:, c], wh[:, :], start=first, stop=False)
            eng.matmul(bank[:, :], xh[:, c], wl[:, :], start=False, stop=False)
            mm = eng.matmul(bank[:, :], xl[:, c], wh[:, :], start=False, stop=last)
        mm.then_inc(self.used, 1)


def grouped_query_attention(nc, R, ident, wstream, scales, rope, causal):
    NKV = 8
    REP = 4
    STEPS = NKV
    QT_TILES = KD
    O_TILES = REP * D // NT
    TILES = 4 * KD + STEPS * (QT_TILES + O_TILES)
    SCALE = float(P) ** -0.5
    HALF = P // 2
    SCORES_AT = [1, 4, 7, 10]

    with ExitStack() as ctx:
        s = Scope(nc, ctx, "g_")
        banks = s.banks()
        KT = s.sb("KT", [P, NKV, TOK])
        V = s.sb("V", [P, B, NKV * P])
        xn = [KT[:, 0:4, :].rearrange("p a n -> p (a n)"), KT[:, 4:8, :].rearrange("p a n -> p (a n)")]
        norm = Norm(s, R, ident, xn)
        st = Stream(s, TILES, wstream, scales)
        QT = s.sb("QT", [P, REP, TOK])
        turn = [s.sb(f"turn{n}", [P, TOK]) for n in range(2)]
        rt = s.sb("rope", [P, 2, P])
        mask = s.sb("mask", [P, P])
        Vcur = s.sb("Vcur", [P, B, P])
        S = s.sb("S", [P, B, P])
        E = s.sb("E", [P, B, P])
        PT = s.sb("PT", [P, TOK])
        CH = s.sb("CH", [P, REP, TOK], F32R)
        CL = s.sb("CL", [P, REP, TOK], F32R)
        nmax = [s.sb(f"nmax{n}", [P, B]) for n in range(2)]
        rsum = [s.sb(f"rsum{n}", [P, B]) for n in range(2)]
        rinv = [s.sb(f"rinv{n}", [P, B]) for n in range(2)]

        tables_loaded = s.sem("tables_loaded")
        rope_multiplied = s.sem("rope_multiplied")
        rope_done = s.sem("rope_done")
        read_out = s.sem("read_out")
        v_staged = s.sem("v_staged")
        scores_done = s.sem("scores_done")
        masked = s.sem("masked")
        max_done = s.sem("max_done")
        exp_done = s.sem("exp_done")
        rinv_done = s.sem("rinv_done")
        prob_done = s.sem("prob_done")
        prob_turned = s.sem("prob_turned")
        prob_copied = s.sem("prob_copied")
        pv_done = s.sem("pv_done")
        ctx_high = s.sem("ctx_high")
        ctx_low = s.sem("ctx_low")
        block = ctx.enter_context(nc.Block())

        def before(i):
            return (4 * KD - O_TILES) // ROUND + (QT_TILES + O_TILES) // ROUND * i

        LAST = STEPS - 1
        CTX_LAST = (norm.XH[:, 0:REP, :], norm.XL[:, 0:REP, :])

        def context(i):
            return CTX_LAST if isinstance(i, int) and i == STEPS else (CH, CL)

        def output_banks(i, n):
            if isinstance(i, int) and i >= LAST:
                low = n > 0 if i == LAST else n % 2 == 0
            else:
                low = n % 2 == 1
            return banks[0:4] if low else banks[4:8]

        def outputs_read(i, n, b):
            return 2 * B + (i - 1) * 4 * B + n * B + b + 1

        def tile_end(r, t):
            return r * ROUND + t + 1

        bc = lambda ap: ap.unsqueeze(1).broadcast_to([ap.shape[0], B, P])

        @block.sync
        def _(sp):
            sp.dma_start(rt[:, :, :], rope).then_inc(tables_loaded, 16)
            sp.dma_start(mask[:, :], causal).then_inc(tables_loaded, 16)
            st.loads(sp)

        @block.gpsimd
        def _(pool):
            norm.pool(pool)

            def rope_add(h, dst):
                pool.wait_ge(rope_multiplied, h + 1)
                j = dst[1] % 2
                pool.tensor_tensor(dst[0], dst[0], turn[j][:, :], ALU.add).then_inc(rope_done, 1)

            for h in range(NKV):
                rope_add(h, (KT[:, h, :], h))
            with pool.Fori(0, STEPS) as i:
                for j in range(REP):
                    rope_add(NKV + i * REP + j, (QT[:, j, :], j))

        @block.vector
        def _(dve):
            st_r = st

            def rope_mult(r, t, h, j, bank, dst):
                dve.wait_ge(st_r.used, tile_end(r, t))
                if not isinstance(h, int) or h >= 2:
                    dve.wait_ge(rope_done, h - 1)
                v = lambda ap: ap.rearrange("p (b t) -> p b t", b=B)
                dve.tensor_tensor(v(dst), v(bank[:, :]), bc(rt[:, 0, :]), ALU.mult)
                dve.tensor_tensor(v(turn[j % 2][0:HALF, :]), v(bank[HALF:P, :]), bc(rt[HALF:P, 1, :]), ALU.mult)
                dve.tensor_tensor(v(turn[j % 2][HALF:P, :]), v(bank[0:HALF, :]), bc(rt[0:HALF, 1, :]),
                                  ALU.mult).then_inc(rope_multiplied, 1)

            def read_values(r, t, n, b):
                dve.wait_ge(st.used, tile_end(r, t))
                dve.tensor_copy(V[:, b, n * NT:(n + 1) * NT], banks[b][:, :]).then_inc(read_out, 1)

            def mask_max(i, j):
                h = (i - 1) * REP + j
                dve.wait_ge(scores_done, h + 1)
                if j:
                    dve.wait_ge(exp_done, h)
                dve.scalar_tensor_tensor(out=S[:, :, :], in0=banks[4][:, :].rearrange("p (b k) -> p b k", b=B),
                                         scalar=SCALE, in1=bc(mask[:, :]), op0=ALU.mult, op1=ALU.add)\
                   .then_inc(masked, 1)
                dve.wait_ge(masked, h + 1)
                dve.tensor_reduce(nmax[j % 2][:, :], S[:, :, :], AXX, ALU.max, negate=True).then_inc(max_done, 1)

            def normalise(i, j):
                h = (i - 1) * REP + j
                dve.wait_ge(exp_done, h + 1)
                dve.reciprocal(rinv[j % 2][:, :], rsum[j % 2][:, :]).then_inc(rinv_done, 1)
                dve.wait_ge(rinv_done, h + 1)
                dve.tensor_tensor(E[:, :, :], E[:, :, :], rinv[j % 2][:, :].unsqueeze(2).broadcast_to([P, B, P]),
                                  ALU.mult).then_inc(prob_done, 1)

            def context_low(i, j):
                dve.wait_ge(ctx_high, (i - 1) * REP + j + 1)
                high, low = context(i)
                dve.tensor_tensor(low[:, j, :], banks[6][:, :], f32(high[:, j, :]), ALU.subtract).then_inc(ctx_low, 1)

            def add_output(r, i, o, n, b):
                dve.wait_ge(st.used, tile_end(r, o + REP * n + REP - 1))
                out = R[:, b, n * NT:(n + 1) * NT]
                dve.tensor_tensor(out, output_banks(i, n)[b][:, :], out, ALU.add).then_inc(read_out, 1)

            def attention_at(i, k):
                for j, at in enumerate(SCORES_AT):
                    if k == at:
                        mask_max(i, j)
                    if k == at + 2:
                        normalise(i, j)
                    if k == at + 5:
                        context_low(i, j)

            def outputs(r, i, o):
                last = isinstance(i, int) and i == LAST
                for t in range(O_TILES):
                    st.at_vector(dve, r, o + t)
                    if o and t < REP:
                        rope_mult(r, o - 1, NKV + i * REP + t, t, banks[t], QT[:, t, :])
                    for n in range(3):
                        for b in range(B):
                            if t == 4 * n + 4 + (b // 2 if not last else 0):
                                add_output(r, i, o, n, b)
                    if last and t >= REP:
                        attention_at(STEPS, t - REP + 1)
                for b in range(B):
                    add_output(r, i, o, 3, b)
                if last:
                    for t in range(O_TILES, O_TILES + REP):
                        attention_at(STEPS, t - REP + 1)

            norm.vector(dve, banks)
            st.begin_vector(dve)
            dve.wait_ge(tables_loaded, 32)
            for k in range(2 * KD):
                st.at_vector(dve, 0, k)
                if KD <= k < KD + REP:
                    rope_mult(0, KD - 1, k - KD, k - KD, banks[k - KD], KT[:, k - KD, :])
            for k in range(KD):
                st.at_vector(dve, 2 * KD // ROUND, k)
                if k < REP:
                    rope_mult(0, 2 * KD - 1, REP + k, k, banks[4 + k], KT[:, REP + k, :])
            for k in range(QT_TILES):
                st.at_vector(dve, 3 * KD // ROUND, k)
                if k < B:
                    read_values(2 * KD // ROUND, KD - 1, 0, k)
            for k in range(KD):
                st.at_vector(dve, 4 * KD // ROUND, k)
                if k < REP:
                    rope_mult(3 * KD // ROUND, QT_TILES - 1, NKV + k, k, banks[4 + k], QT[:, k, :])
            for b in range(B):
                read_values(4 * KD // ROUND, KD - 1, 1, b)

            def step(i):
                r = before(i)
                for k in range(QT_TILES):
                    st.at_vector(dve, r, k)
                    attention_at(i, k)
                outputs(r, i, QT_TILES)

            with dve.Fori(1, LAST) as i:
                step(i)
            step(LAST)
            outputs(before(STEPS), STEPS, 0)

        @block.scalar
        def _(act):
            def stage_values(i):
                act.activation(Vcur[:, :, :], V[:, :, bass.ds(i * P, P)], ACT.Copy).then_inc(v_staged, 1)

            def exponent(i, j):
                h = (i - 1) * REP + j
                act.wait_ge(max_done, h + 1)
                if j:
                    act.wait_ge(prob_turned, h)
                for b in range(B):
                    last = act.activation(E[:, b, :], S[:, b, :], ACT.Exp, bias=nmax[j % 2][:, b:b + 1],
                                          accum_out=rsum[j % 2][:, b:b + 1])
                last.then_inc(exp_done, 1)

            def copy_turned(i, j):
                h = (i - 1) * REP + j
                act.wait_ge(prob_turned, h + 1)
                if j:
                    act.wait_ge(pv_done, h)
                act.activation(PT[:, :], banks[5][:, :], ACT.Copy).then_inc(prob_copied, 1)

            def context_high(r, i, j):
                act.wait_ge(pv_done, (i - 1) * REP + j + 1)
                if not j:
                    act.wait_ge(st.used, r * ROUND)
                act.activation(context(i)[0][:, j, :], banks[6][:, :], ACT.Copy).then_inc(ctx_high, 1)

            def attention_at(r, i, k):
                for j, at in enumerate(SCORES_AT):
                    if k == at:
                        exponent(i, j)
                    if k == at + 3:
                        copy_turned(i, j)
                    if k == at + 4:
                        context_high(r, i, j)

            norm.scalar(act, banks)
            st.begin_scalar(act)
            for r, n in ((0, 2 * KD), (2 * KD // ROUND, 2 * KD), (4 * KD // ROUND, QT_TILES)):
                for k in range(n):
                    st.at_scalar(act, r, k)
            act.wait_ge(read_out, 2 * B)
            stage_values(0)
            def step(i):
                r = before(i)
                for k in range(QT_TILES):
                    st.at_scalar(act, r, k)
                    attention_at(r, i, k)
                act.wait_ge(pv_done, i * REP)
                stage_values(i)
                for t in range(O_TILES):
                    st.at_scalar(act, r, QT_TILES + t)
                    if isinstance(i, int) and t >= REP:
                        attention_at(r + QT_TILES // ROUND, STEPS, t - REP + 1)

            with act.Fori(1, LAST) as i:
                step(i)
            step(LAST)
            for t in range(O_TILES, O_TILES + REP):
                attention_at(before(LAST) + QT_TILES // ROUND, STEPS, t - REP + 1)
            for t in range(O_TILES):
                st.at_scalar(act, before(STEPS), t)

        @block.tensor
        def _(pe):
            XH, XL = norm.XH, norm.XL

            def project_features(r, t0, use, free):
                for k in range(KD):
                    st.product_features(pe, r, t0 + k, XH[:, k, :], XL[:, k, :], use, k == 0, k == KD - 1,
                                        free if k == 0 else None)
                    yield k

            def project_tokens(r, t0, use, free):
                for k in range(KD):
                    st.product_tokens(pe, r, t0 + k, XH[:, k, :], XL[:, k, :], use, k == 0, k == KD - 1,
                                      free if k == 0 else None)

            def scores(i, j):
                h = (i - 1) * REP + j
                pe.wait_ge(rope_done, NKV + h + 1)
                if j:
                    pe.wait_ge(masked, h)
                for b in range(B):
                    c = slice(b * P, (b + 1) * P)
                    mm = pe.matmul(banks[4][:, c], QT[:, j, c], KT[:, bass.ds(i - 1, 1), c].rearrange("p a t -> p (a t)"),
                                   start=True, stop=True)
                mm.then_inc(scores_done, 1)

            def turn_probs(i, j):
                h = (i - 1) * REP + j
                pe.wait_ge(prob_done, h + 1)
                for b in range(B):
                    mm = pe.transpose(banks[5][:, b * P:(b + 1) * P], E[:, b, :], ident[:, :])
                mm.then_inc(prob_turned, 1)

            def values(i, j):
                h = (i - 1) * REP + j
                pe.wait_ge(prob_copied, h + 1)
                if j:
                    pe.wait_ge(ctx_low, h)
                else:
                    pe.wait_ge(v_staged, i)
                for b in range(B):
                    c = slice(b * P, (b + 1) * P)
                    mm = pe.matmul(banks[6][:, c], Vcur[:, b, :], PT[:, c], start=True, stop=True)
                mm.then_inc(pv_done, 1)

            def attention_at(i, k):
                for j, at in enumerate(SCORES_AT):
                    if k == at:
                        scores(i, j)
                    if k == at + 3:
                        turn_probs(i, j)
                    if k == at + 4:
                        values(i, j)

            def outputs(r, i, o):
                high, low = context(i)
                pe.wait_ge(ctx_low, i * REP)
                for t in range(O_TILES):
                    n, j = t // REP, t % REP

                    def free(b):
                        if isinstance(i, int) and i == STEPS:
                            if n == 0:
                                pe.wait_ge(read_out, outputs_read(LAST, 3, b))
                            if n >= 2:
                                pe.wait_ge(read_out, outputs_read(i, n - 2, b))
                        elif n == 1:
                            pe.wait_ge(rope_multiplied, NKV + i * REP + b + 1)
                        elif n >= 2:
                            same = n - 1 if isinstance(i, int) else n - 2
                            pe.wait_ge(read_out, outputs_read(i, same, b))

                    st.product_tokens(pe, r, o + t, high[:, j, :], low[:, j, :], output_banks(i, n), j == 0, j == REP - 1,
                                      free if j == 0 else None)
                    if isinstance(i, int) and i == LAST and t >= REP:
                        if t == REP:
                            pe.wait_ge(read_out, outputs_read(i, 0, B - 1))
                        attention_at(STEPS, t - REP + 1)

            norm.tensor(pe, banks)
            pe.wait_ge(norm.lo_done, 4 * B)
            for n in range(2):
                for _ in project_features(0, n * KD, banks[4 * n:4 * n + 4], None):
                    pass
            project_tokens(2 * KD // ROUND, 0, banks[0:4], lambda b: pe.wait_ge(rope_multiplied, b + 1))
            for _ in project_features(3 * KD // ROUND, 0, banks[4:8], lambda j: pe.wait_ge(rope_multiplied, REP + j + 1)):
                pass
            project_tokens(4 * KD // ROUND, 0, banks[0:4], lambda b: pe.wait_ge(read_out, b + 1))

            def step(i):
                r = before(i)
                pe.wait_ge(rope_multiplied, NKV + i * REP)
                for k in project_features(r, 0, banks[0:4], lambda j: pe.wait_ge(read_out, outputs_read(i, -1, j))):
                    attention_at(i, k)
                outputs(r, i, QT_TILES)

            with pe.Fori(1, LAST) as i:
                step(i)
            step(LAST)
            for t in range(O_TILES, O_TILES + REP):
                attention_at(STEPS, t - REP + 1)
            outputs(before(STEPS), STEPS, 0)


XH_ = 512
C = 4
RH = 16
HS = XH_ // RH
AC = C - 1
PIECE = 4
SIDE_SKIP = RH
SIDE_A = 2 * RH
SIDE_B = SIDE_A + RH * AC


class Read:

    def __init__(self, s, outs, turned, W, Y, YH, YL, F, gamma, beta, ident):
        self.outs, self.turned_x, self.W, self.Y = outs, turned, W, Y
        self.w_loaded = s.sem("read_w_loaded")
        self.YH, self.YL, self.F, self.gamma, self.beta, self.ident = YH, YL, F, gamma, beta, ident
        self.stats = s.sb("y_stats", [P, B, outs, 6])
        self.mv = s.sb("y_mv", [P, B, outs, 2])
        self.veps = s.sb("y_veps", [P, B, outs])
        self.rstd = s.sb("y_rstd", [P, B, outs])
        self.nhalf = s.sb("y_nhalf", [P, 1])
        self.summed = s.sem("y_summed")
        self.y_read = s.sem("y_read")
        self.stats_done = s.sem("y_stats_done")
        self.var_done = s.sem("y_var_done")
        self.rstd_steps = s.sem("y_rstd_steps")
        self.scaled = s.sem("y_scaled")
        self.turned = s.sem("y_turned")
        self.affine_done = s.sem("y_affine_done")
        self.hi_done = s.sem("y_hi_done")
        self.lo_done = s.sem("y_lo_done")

    def load(self, eng, weights):
        eng.dma_start(self.W[:, :, :], weights).then_inc(self.w_loaded, 16)

    def sums(self, eng, banks, b):
        x, tok = self.turned_x, slice(b * P, (b + 1) * P)
        eng.wait_ge(self.w_loaded, 16)
        eng.wait_ge(x.hi_done, 2 * (b + 1))
        eng.wait_ge(x.lo_done, 2 * (b + 1))
        for t in range(KD // PIECE):
            if b:
                eng.wait_ge(self.y_read, 4 * (b - 1) + t + 1)
            for j in range(PIECE):
                w = slice(j * P, j * P + 32 * self.outs)
                mm = eng.matmul(banks[t][:, w], x.XT[:, PIECE * t + j, tok], self.W[:, t, w], start=True, stop=True)
            mm.then_inc(self.summed, 1)

    def read_sums(self, eng, banks, b):
        for t in range(KD // PIECE):
            eng.wait_ge(self.summed, 4 * b + t + 1)
            src = banks[t][:, :].rearrange("p (j o h) -> p j o h", j=PIECE, h=32)
            for o in range(self.outs):
                last = eng.activation(self.Y[:, b, o, t * P:(t + 1) * P].rearrange("p (j h) -> p j h", j=PIECE),
                                      src[:, :, o, :], ACT.Copy)
            last.then_inc(self.y_read, 1)

    def norm(self, eng, b):
        eng.wait_ge(self.y_read, 4 * (b + 1))
        for o in range(self.outs):
            last = eng.bn_stats(self.stats[:, b, o, :], self.Y[:, b, o, :])
        last.then_inc(self.stats_done, 1)
        eng.wait_ge(self.stats_done, b + 1)
        for o in range(self.outs):
            last = eng.bn_aggr(self.mv[:, b, o, :], self.stats[:, b, o, :])
        last.then_inc(self.var_done, 1)
        eng.wait_ge(self.var_done, b + 1)
        eng.wait_ge(self.rstd_steps, 2 * b + 3)
        for o in range(self.outs):
            eng.tensor_scalar(self.Y[:, b, o, :], self.Y[:, b, o, :], self.mv[:, b, o, 0:1], self.rstd[:, b, o:o + 1],
                              ALU.subtract, ALU.mult).then_inc(self.scaled, 1)

    def pool(self, eng):
        eng.memset(self.nhalf[:, :], -0.5).then_inc(self.rstd_steps, 1)
        for b in range(B):
            eng.wait_ge(self.var_done, b + 1)
            eng.tensor_scalar(self.veps[:, b, :], self.mv[:, b, :, 1], EPS, None, ALU.add).then_inc(self.rstd_steps, 1)
            eng.wait_ge(self.rstd_steps, 2 * b + 2)
            eng.tensor_tensor(self.rstd[:, b, :], self.veps[:, b, :], self.nhalf[:, :].broadcast_to([P, self.outs]),
                              ALU.pow).then_inc(self.rstd_steps, 1)


    def turn(self, eng, banks, n):
        o, c = n // 4, n % 4
        eng.wait_ge(self.scaled, (B - 1) * self.outs + o + 1)
        if n >= len(banks):
            eng.wait_ge(self.affine_done, n + 1 - len(banks))
        for b in range(B):
            mm = eng.transpose(banks[n % len(banks)][:, b * P:(b + 1) * P], self.Y[:, b, o, c * P:(c + 1) * P],
                               self.ident[:, :])
        mm.then_inc(self.turned, 1)

    def affine(self, eng, banks, n, first=1):
        eng.wait_ge(self.turned, max(n + 1, first))
        if n >= 2:
            eng.wait_ge(self.lo_done, n - 1)
        eng.activation(self.F[n % 2][:, :], banks[n % len(banks)][:, :], ACT.Identity, bias=self.beta[:, n:n + 1],
                       scale=self.gamma[:, n:n + 1]).then_inc(self.affine_done, 1)
        eng.wait_ge(self.affine_done, n + 1)
        eng.activation(self.YH[:, n, :], self.F[n % 2][:, :], ACT.Copy).then_inc(self.hi_done, 1)

    def low_part(self, eng, n):
        eng.wait_ge(self.hi_done, n + 1)
        eng.tensor_tensor(self.YL[:, n, :], self.F[n % 2][:, :], f32(self.YH[:, n, :]), ALU.subtract)\
           .then_inc(self.lo_done, 1)


class Write:

    def __init__(self, s, H, R, G, side, sideT, ident, side_bias, DU):
        self.H, self.R, self.G = H, R, G
        self.log = [g[:, 0, :] for g in G]
        self.side, self.sideT = side, sideT
        self.ident, self.side_bias, self.DU = ident, side_bias, DU
        self.decay = s.sb("decay", [P, B, RH * AC])
        self.spl = s.sb("decay_log", [P, B, RH * AC])
        self.cn = s.sb("coef", [P, B, RH * AC])
        self.biased = s.sem("w_side_biased")
        self.side_turned = s.sem("w_side_turned")
        self.side_done = s.sem("w_side")
        self.pre_done = s.sem("w_pre")
        self.abs_done = s.sem("w_abs")
        self.exp_done = s.sem("w_exp")
        self.decay_log = s.sem("w_decay_log")
        self.delta_log = s.sem("w_delta_log")
        self.delta_done = s.sem("w_delta")
        self.coef_steps = s.sem("w_coef_steps")
        self.coef_done = s.sem("w_coef")
        self.arg_done = s.sem("w_arg")
        self.skip_done = s.sem("w_skip")
        self.a_done = s.sem("w_a")
        self.folded = s.sem("w_folded")
        self.factors_done = s.sem("w_factors")
        self.multiplied = s.sem("w_multiplied")


    def turn_side(self, eng, dst, b):
        eng.wait_ge(self.biased, b + 1)
        eng.transpose(dst, self.sideT[:, b * P:(b + 1) * P], self.ident[:, :]).then_inc(self.side_turned, 1)

    def expand_delta(self, eng, dst, b):
        eng.wait_ge(self.biased, b + 1)
        eng.matmul(dst[:, :], self.sideT[0:9, b * P:(b + 1) * P], self.DU[0:9, :], start=True, stop=True)\
           .then_inc(self.pre_done, 1)


    def add_bias(self, eng, src, b):
        eng.activation(self.sideT[:, b * P:(b + 1) * P], src, ACT.Identity, bias=self.side_bias[:, 0:1])\
           .then_inc(self.biased, 1)


    def exponents(self, eng, pre, b):
        eng.wait_ge(self.side_done, b + 1)
        eng.activation(self.spl[:, b, :], self.side[:, b, SIDE_A:SIDE_B], ACT.Abs).then_inc(self.abs_done, 1)
        eng.wait_ge(self.pre_done, b + 1)
        eng.activation(self.log[b], pre[:, :], ACT.Abs).then_inc(self.abs_done, 1)
        eng.wait_ge(self.abs_done, 2 * b + 1)
        eng.activation(self.spl[:, b, :], self.spl[:, b, :], ACT.Exp, scale=-1.0).then_inc(self.exp_done, 1)
        eng.wait_ge(self.abs_done, 2 * b + 2)
        eng.activation(self.log[b], self.log[b], ACT.Exp, scale=-1.0).then_inc(self.exp_done, 1)

    def logs(self, eng, b):
        eng.wait_ge(self.exp_done, 2 * b + 1)
        eng.activation(self.spl[:, b, :], self.spl[:, b, :], ACT.Ln, bias=1.0).then_inc(self.decay_log, 1)
        eng.wait_ge(self.exp_done, 2 * b + 2)
        eng.activation(self.log[b], self.log[b], ACT.Ln, bias=1.0).then_inc(self.delta_log, 1)

    def decays(self, eng, b):
        eng.wait_ge(self.arg_done, b + 1)
        eng.activation(self.G[b][:, 0:AC, :], self.G[b][:, 0:AC, :], ACT.Exp, scale=-1.0).then_inc(self.a_done, 1)


    def per_group(self, x):
        return x.unsqueeze(1).broadcast_to([P, HS, RH])

    def of_channel(self, x, b, c):
        return self.per_group(x[:, b, :].rearrange("p (r c) -> p r c", c=AC)[:, :, c])

    def grouped(self, x):
        return x.rearrange("p (s r) -> p s r", r=RH)

    def pool(self, eng):
        for b in range(B):
            d = self.grouped(self.G[b][:, AC, :])
            eng.wait_ge(self.coef_done, b + 1)
            eng.wait_ge(self.delta_done, b + 1)
            for c in range(AC):
                last = eng.tensor_tensor(self.grouped(self.G[b][:, c, :]), d, self.of_channel(self.decay, b, c), ALU.mult)
            last.then_inc(self.arg_done, 1)
            eng.wait_ge(self.arg_done, b + 1)
            eng.tensor_tensor(d, d, self.per_group(self.side[:, b, SIDE_SKIP:SIDE_SKIP + RH]), ALU.mult)\
               .then_inc(self.skip_done, 1)


    def copy_turned(self, eng, src, b, turned):
        eng.wait_ge(self.side_turned, turned)
        eng.tensor_copy(self.side[:, b, :], src).then_inc(self.side_done, 1)

    def softplus(self, eng, pre, b):
        eng.wait_ge(self.side_done, b + 1)
        eng.wait_ge(self.decay_log, b + 1)
        eng.scalar_tensor_tensor(out=self.decay[:, b, :], in0=self.side[:, b, SIDE_A:SIDE_B], scalar=0.0,
                                 in1=self.spl[:, b, :], op0=ALU.max, op1=ALU.add).then_inc(self.coef_steps, 1)
        eng.wait_ge(self.delta_log, b + 1)
        eng.scalar_tensor_tensor(out=self.G[b][:, AC, :], in0=pre[:, :], scalar=0.0, in1=self.log[b],
                                 op0=ALU.max, op1=ALU.add).then_inc(self.delta_done, 1)
        eng.wait_ge(self.coef_steps, 3 * b + 1)
        eng.tensor_scalar(self.spl[:, b, :], self.decay[:, b, :], SSM_EPS, None, ALU.add).then_inc(self.coef_steps, 1)
        eng.wait_ge(self.coef_steps, 3 * b + 2)
        eng.reciprocal(self.cn[:, b, :], self.spl[:, b, :]).then_inc(self.coef_steps, 1)
        eng.wait_ge(self.coef_steps, 3 * b + 3)
        eng.scalar_tensor_tensor(out=self.cn[:, b, :], in0=self.cn[:, b, :], scalar=-1.0, in1=self.side[:, b, SIDE_B:P],
                                 op0=ALU.mult, op1=ALU.mult).then_inc(self.coef_done, 1)

    def channels(self, x, b):
        return x[:, b, :].rearrange("p (n c) -> p c n", c=C)

    def fold(self, eng, b):
        G = self.G[b]
        eng.wait_ge(self.a_done, b + 1)
        h = self.channels(self.H, b)[:, 0:AC, :]
        eng.tensor_tensor(h, h, G[:, 0:AC, :], ALU.mult).then_inc(self.folded, 1)
        eng.wait_ge(self.folded, b + 1)
        eng.wait_ge(self.coef_done, b + 1)
        for c in range(AC):
            last = eng.scalar_tensor_tensor(out=self.grouped(G[:, c, :]), in0=self.grouped(G[:, c, :]), scalar=-1.0,
                                            in1=self.of_channel(self.cn, b, c), op0=ALU.add, op1=ALU.mult)
        if self.R is not None:
            last = eng.tensor_tensor(self.R[:, b, :], self.R[:, b, :], self.H[:, b, :], ALU.add)
        last.then_inc(self.factors_done, 1)

    POOL_ADDS = 1

    def update(self, eng, banks):
        target = self.H if self.R is None else self.R
        for b in range(B):
            G = self.G[b]
            eng.wait_ge(self.skip_done, b + 1)
            eng.wait_ge(self.factors_done, b + 1)
            eng.tensor_tensor(G[:, :, :], G[:, :, :], banks[b][:, :].unsqueeze(1).broadcast_to([P, C, XH_]), ALU.mult)\
               .then_inc(self.multiplied, 1)
            if b >= self.POOL_ADDS:
                x = self.channels(target, b)
                eng.wait_ge(self.multiplied, b + 1)
                eng.tensor_tensor(x, x, G[:, :, :], ALU.add)

    def pool_update(self, eng):
        target = self.H if self.R is None else self.R
        for b in range(self.POOL_ADDS):
            x = self.channels(target, b)
            eng.wait_ge(self.multiplied, b + 1)
            eng.tensor_tensor(x, x, self.G[b][:, :, :], ALU.add)


def side_products(pe, st, t0, pieces, xh, xl, dst, tok, last, done=None, ready=None):
    for t in range(pieces // 4):
        pe.wait_ge(st.lo_done, t0 + t + 1)
        if ready:
            ready(t)
        wh, wl = st.WH[(t0 + t) % PART_SLOTS], st.WL[(t0 + t) % PART_SLOTS]
        for j in range(4):
            k, w = 4 * t + j, slice(j * P, (j + 1) * P)
            pe.matmul(dst, wh[:, w], xh[:, k, tok], start=k == 0, stop=False)
            pe.matmul(dst, wh[:, w], xl[:, k, tok], start=False, stop=False)
            mm = pe.matmul(dst, wl[:, w], xh[:, k, tok], start=False, stop=k == pieces - 1)
        mm.then_inc(st.used if last else done, 1)


def xattn_attention(nc, R, H, ident, x, read_w, wstream, gamma_d, beta_d, pos_d, inv_d, causal, side_bias_d, du_d):
    NH = 16
    HD = XH_ // NH
    HALF = HD // 2
    OUTS = 3
    TILES = OUTS * 4 + 1 + 4
    SCALE = 1.0 / float(np.sqrt(HD))
    PROJ = 0
    SIDE = PROJ + OUTS * 4
    TWO_PI = 2.0 * np.pi
    C1 = 6.28125
    C2 = float(np.round((TWO_PI - C1) * 2.0 ** 17) / 2.0 ** 17)
    C3 = float(np.float32(TWO_PI - C1 - C2))
    MAGIC = 1.5 * 2.0 ** 23
    LIMIT = 3.1415925

    with ExitStack() as ctx:
        s = Scope(nc, ctx, "a_")
        banks = s.banks()
        norm = CopiedNorm(s, R, ident, [H[:, b, :] for b in range(B)])
        st = Stream(s, TILES, wstream)
        YH = norm.XH[:, 0:12, :]
        YL = norm.XL[:, 0:12, :]
        QT = s.over("XH", 12, "QT", [P, 4, TOK])
        KT = s.over("XL", 12, "KT", [P, 4, TOK])
        PT = s.over("XH", 0, "PT", [P, NH, P])
        OH = norm.XH[:, 4:8, :]
        OL = norm.XL[:, 4:8, :]
        Y = s.sb("Y", [P, B, OUTS, XH_])
        q_tok = Y[:, :, 0, :]
        k_tok = Y[:, :, 1, :]
        V = Y[:, :, 2, :]
        S = s.sb("S", [P, NH, P])
        F = [s.sb(f"F{n}", [P, TOK]) for n in range(2)]
        gamma = s.sb("gamma", [P, 4 * OUTS])
        beta = s.sb("beta", [P, 4 * OUTS])
        read = Read(s, OUTS, norm, s.over("XL", 12, "read_w", [P, KD // PIECE, NT]), Y, YH, YL, F, gamma, beta, ident)
        posi = s.sb("pos", [P, B], I32)
        posf = s.sb("posf", [P, B])
        inv = s.sb("inv", [P, HALF])
        ang = s.sb("ang", [P, B, HALF])
        kk = s.sb("kk", [P, B, HALF])
        sc = s.sb("sincos", [P, 3, B, HALF])
        mask = s.sb("mask", [P, P])
        nmax = s.sb("nmax", [P, NH])
        rsum = s.sb("rsum", [P, NH])
        rinv = s.sb("rinv", [P, NH])
        side_bias = s.sb("side_bias", [P, 1])
        DU = s.sb("DU", [9, XH_])
        side_product_done = s.sem("side_product_done")
        write = Write(s, H, None, [s.over(x, row, f"G{n}", [P, C, XH_]) for n, (x, row) in
                                   enumerate((("XH", 8), ("XL", 0), ("XL", 8), ("XH", 0)))],
                      q_tok[:, 1, :].rearrange("p (b n) -> p b n", b=B), k_tok[:, 1, :], ident, side_bias, DU)

        x_loaded = [s.sem(f"x_loaded{b}") for b in range(B)]
        small_loaded = s.sem("small_loaded")
        table_steps = s.sem("table_steps")
        sin_done = s.sem("sin_done")
        tables_done = s.sem("tables_done")
        rope_mult = s.sem("rope_mult")
        rope_done = s.sem("rope_done")
        v_read = s.sem("v_read")
        qk_turned = s.sem("qk_turned")
        qk_copied = s.sem("qk_copied")
        scores_done = s.sem("scores_done")
        masked = s.sem("masked")
        max_done = s.sem("max_done")
        exp_done = s.sem("exp_done")
        prob_turned = s.sem("prob_turned")
        prob_copied = s.sem("prob_copied")
        pv_done = s.sem("pv_done")
        rinv_done = s.sem("rinv_done")
        normalised = s.sem("normalised")
        o_high = s.sem("o_high")
        o_low = s.sem("o_low")
        block = ctx.enter_context(nc.Block())
        pieces4 = lambda ap: ap.rearrange("p (c t) -> p c t", c=4)

        @block.sync
        def _(sp):
            for b in range(2):
                sp.dma_start(R[:, b, :], x[b, :, :]).then_inc(x_loaded[b], 16)
            for dst, src in ((gamma[:, :], gamma_d), (beta[:, :], beta_d), (posi[:, :], pos_d), (inv[:, :], inv_d),
                             (mask[:, :], causal), (side_bias[:, :], side_bias_d), (DU[:, :], du_d)):
                sp.dma_start(dst, src).then_inc(small_loaded, 16)
            read.load(sp, read_w)
            st.loads(sp)

        SMALL = 7 * 16

        @block.gpsimd
        def _(pool):
            norm.pool(pool)
            read.pool(pool)
            for n in range(2 * B):
                dst = (q_tok, k_tok)[n // B][:, n % B, :]
                pool.wait_ge(rope_mult, n + 1)
                pool.tensor_tensor(dst, dst, F[n % 2][:, :], ALU.add).then_inc(rope_done, 1)
            write.pool(pool)
            write.pool_update(pool)

        @block.vector
        def _(dve):
            def moments(b):
                dve.wait_ge(x_loaded[b], 16)
                norm.moments(dve, b)

            moments(0)
            moments(1)
            norm.scale(dve, 0)
            norm.copy(dve, banks[0:4], 0, 1)
            moments(2)
            norm.scale(dve, 1)
            norm.copy(dve, banks[0:4], 1, 1)
            moments(3)
            norm.scale(dve, 2)
            norm.scale(dve, 3)
            norm.copy(dve, banks[0:4], 2, 1)
            read.norm(dve, 0)
            norm.copy(dve, banks[0:4], 3, 1)

            for b in range(1, B):
                read.norm(dve, b)
            st.begin_vector(dve)
            for n in range(4 * OUTS):
                read.low_part(dve, n)
                if n == 3 or n == 7:
                    st.at_vector(dve, 0, PROJ + n // 4 * 2)
                    st.at_vector(dve, 0, PROJ + n // 4 * 2 + 1)

            link = Chain(dve, table_steps)
            dve.wait_ge(small_loaded, SMALL)
            link(dve.tensor_copy(posf[:, :], posi[:, :]))
            link(dve.tensor_tensor(ang[:, :, :], posf[:, :].unsqueeze(2).broadcast_to([P, B, HALF]),
                                   inv[:, :].unsqueeze(1).broadcast_to([P, B, HALF]), ALU.mult))
            link(dve.tensor_scalar(kk[:, :, :], ang[:, :, :], 1.0 / TWO_PI, MAGIC, ALU.mult, ALU.add))
            link(dve.tensor_scalar(kk[:, :, :], kk[:, :, :], MAGIC, None, ALU.subtract))
            for part in (C1, C2, C3):
                link(dve.scalar_tensor_tensor(out=ang[:, :, :], in0=kk[:, :, :], scalar=-part, in1=ang[:, :, :],
                                              op0=ALU.mult, op1=ALU.add))
            link(dve.tensor_scalar(sc[:, 1, :, :], ang[:, :, :], np.pi / 2, None, ALU.add))
            link(dve.tensor_scalar(kk[:, :, :], sc[:, 1, :, :], LIMIT, -TWO_PI, ALU.is_gt, ALU.mult))
            link(dve.tensor_tensor(sc[:, 1, :, :], sc[:, 1, :, :], kk[:, :, :], ALU.add))
            link(dve.tensor_copy(sc[:, 0, :, :], ang[:, :, :]))
            link(dve.tensor_scalar(sc[:, 0:2, :, :], sc[:, 0:2, :, :], LIMIT, -LIMIT, ALU.min, ALU.max))
            dve.wait_ge(sin_done, 1)
            link(dve.tensor_scalar(sc[:, 2, :, :], sc[:, 0, :, :], -1.0, None, ALU.mult))

            heads = lambda ap: ap.rearrange("p (h d) -> p h d", d=HALF)
            halves = lambda ap: ap.rearrange("p (h two d) -> p h two d", two=2, d=HALF)

            def rope(n):
                which, b = n // B, n % B
                bank, dst, turn = banks[4 * which + b], (q_tok, k_tok)[which][:, b, :], F[n % 2][:, :]
                dve.wait_ge(st.used, PROJ + 4 * (which + 1))
                if n < 2:
                    dve.wait_ge(read.lo_done, 11 + n)
                if n >= 2:
                    dve.wait_ge(rope_done, n - 1)
                dve.tensor_tensor(heads(dst), heads(bank[:, :]),
                                  sc[:, 1, b, :].unsqueeze(1).broadcast_to([P, 2 * NH, HALF]), ALU.mult)
                dve.tensor_tensor(halves(turn)[:, :, 0, :], halves(bank[:, :])[:, :, 1, :],
                                  sc[:, 2, b, :].unsqueeze(1).broadcast_to([P, NH, HALF]), ALU.mult)
                dve.tensor_tensor(halves(turn)[:, :, 1, :], halves(bank[:, :])[:, :, 0, :],
                                  sc[:, 0, b, :].unsqueeze(1).broadcast_to([P, NH, HALF]), ALU.mult)\
                   .then_inc(rope_mult, 1)

            for n in range(2 * B):
                st.at_vector(dve, 0, PROJ + 4 + n)
                rope(n)
            for t in range(PROJ + 12, SIDE + 2):
                st.at_vector(dve, 0, t)

            def masked_scores(b, r):
                n = 4 * b + r + 1
                dve.wait_ge(scores_done, n)
                if b:
                    dve.wait_ge(prob_turned, n - 4)
                dve.scalar_tensor_tensor(
                    out=S[:, 4 * r:4 * r + 4, :], in0=banks[r][:, :].rearrange("p (c k) -> p c k", c=4),
                    scalar=SCALE, in1=mask[:, :].unsqueeze(1).broadcast_to([P, 4, P]), op0=ALU.mult, op1=ALU.add)\
                   .then_inc(masked, 1)
                dve.wait_ge(masked, n)
                dve.tensor_reduce(nmax[:, 4 * r:4 * r + 4], S[:, 4 * r:4 * r + 4, :], AXX, ALU.max, negate=True)\
                   .then_inc(max_done, 1)

            def normalise(b, r):
                n = 4 * b + r + 1
                heads = slice(4 * r, 4 * r + 4)
                dve.wait_ge(exp_done, n)
                dve.reciprocal(rinv[:, heads], rsum[:, heads]).then_inc(rinv_done, 1)
                dve.wait_ge(rinv_done, n)
                dve.tensor_tensor(S[:, heads, :], S[:, heads, :], rinv[:, heads].unsqueeze(2).broadcast_to([P, 4, P]),
                                  ALU.mult).then_inc(normalised, 1)

            for r in range(4):
                masked_scores(0, r)
            for r in range(4):
                normalise(0, r)
            for b in range(B):
                more = b + 1 < B
                if more:
                    for r in range(4):
                        masked_scores(b + 1, r)
                    normalise(b + 1, 0)
                    normalise(b + 1, 1)
                dve.wait_ge(o_high, b + 1)
                tok = slice(b * P, (b + 1) * P)
                dve.tensor_tensor(OL[:, :, tok], pieces4(banks[4][:, :]), f32(OH[:, :, tok]), ALU.subtract).then_inc(o_low, 1)
                if more:
                    normalise(b + 1, 2)
                write.copy_turned(dve, banks[6][:, P:2 * P], b, b + 1)
                if more:
                    normalise(b + 1, 3)
                write.softplus(dve, banks[7], b)
                if b:
                    write.fold(dve, b - 1)
            st.at_vector(dve, 0, SIDE + 2)
            write.fold(dve, B - 1)
            dve.wait_ge(st.used, TILES)
            write.update(dve, banks)

        @block.scalar
        def _(act):
            act.wait_ge(x_loaded[0], 16)
            for b in range(2, B):
                act.dma_start(R[:, b, :], x[b, :, :]).then_inc(x_loaded[b], 16)
            norm.copy(act, banks[0:4], 0, 0)
            norm.copy(act, banks[0:4], 1, 0)
            for b in range(B):
                read.read_sums(act, banks[4:8], b)
                if b + 2 < B:
                    norm.copy(act, banks[0:4], b + 2, 0)
            st.begin_scalar(act)
            act.wait_ge(small_loaded, SMALL)
            for n in range(4 * OUTS):
                read.affine(act, banks[4:8], n)
                if n == 3 or n == 7:
                    st.at_scalar(act, 0, PROJ + n // 4 * 2)
                    st.at_scalar(act, 0, PROJ + n // 4 * 2 + 1)
            act.wait_ge(table_steps, 12)
            act.activation(sc[:, 0:2, :, :], sc[:, 0:2, :, :], ACT.Sin).then_inc(sin_done, 1)
            for t in range(PROJ + 4, SIDE + 2):
                st.at_scalar(act, 0, t)
            for b in range(B):
                act.activation(V[:, b, :], banks[b][:, :], ACT.Copy).then_inc(v_read, 1)
            for n in range(2 * B):
                act.wait_ge(qk_turned, n + 1)
                act.activation((QT, KT)[n % 2][:, :, n // 2 * P:(n // 2 + 1) * P], pieces4(banks[4 + n % 4][:, :]), ACT.Copy)\
                   .then_inc(qk_copied, 1)

            def exponents(b, r):
                n = 4 * b + r + 1
                act.wait_ge(max_done, n)
                if b and r == 0:
                    act.wait_ge(rinv_done, 4 * b)
                for h in range(4 * r, 4 * r + 4):
                    last = act.activation(S[:, h, :], S[:, h, :], ACT.Exp, bias=nmax[:, h:h + 1],
                                          accum_out=rsum[:, h:h + 1])
                last.then_inc(exp_done, 1)

            for r in range(4):
                exponents(0, r)
            for b in range(B):
                for r in range(4):
                    act.wait_ge(prob_turned, 4 * b + r + 1)
                    if b:
                        act.wait_ge(pv_done, b)
                    act.activation(PT[:, 4 * r:4 * r + 4, :], banks[4 + r][:, :].rearrange("p (c q) -> p c q", c=4),
                                   ACT.Copy).then_inc(prob_copied, 1)
                if b + 1 < B:
                    exponents(b + 1, 0)
                    exponents(b + 1, 1)
                act.wait_ge(pv_done, b + 1)
                act.activation(OH[:, :, b * P:(b + 1) * P], pieces4(banks[4][:, :]), ACT.Copy).then_inc(o_high, 1)
                if b + 1 < B:
                    exponents(b + 1, 2)
                act.wait_ge(*((side_product_done, b + 1) if b + 1 < B else (st.used, SIDE + 1)))
                write.add_bias(act, banks[6][:, 0:P], b)
                if b + 1 < B:
                    exponents(b + 1, 3)
                write.exponents(act, banks[7], b)
                if b:
                    write.decays(act, b - 1)
                write.logs(act, b)
            st.at_scalar(act, 0, SIDE + 2)
            write.decays(act, B - 1)

        @block.tensor
        def _(pe):
            def turn(b):
                pe.wait_ge(norm.scaled, b + 1)
                norm.turn(pe, banks[0:4], b)

            turn(0)
            turn(1)
            for b in range(B):
                read.sums(pe, banks[4:8], b)
                if b + 2 < B:
                    turn(b + 2)

            def project(o, use, free):
                for k in range(4):
                    pe.wait_ge(read.lo_done, 4 * o + k + 1)
                    st.product_tokens(pe, 0, PROJ + 4 * o + k, YH[:, 4 * o + k, :], YL[:, 4 * o + k, :], use, k == 0, k == 3,
                                      free if k == 0 else None)

            for n in range(8):
                read.turn(pe, banks[4:8], n)
            project(0, banks[0:4], None)
            for n in range(8, 12):
                read.turn(pe, banks[4:8], n)
            project(1, banks[4:8], lambda b: pe.wait_ge(read.affine_done, 9 + b))
            project(2, banks[0:4], lambda b: pe.wait_ge(rope_mult, b + 1))
            for n in range(2 * B):
                which, b = n % 2, n // 2
                pe.wait_ge(rope_done, which * B + b + 1)
                if n < 4:
                    pe.wait_ge(rope_mult, B + n + 1)
                else:
                    pe.wait_ge(qk_copied, n - 3)
                for c in range(4):
                    mm = pe.transpose(banks[4 + n % 4][:, c * P:(c + 1) * P], (q_tok, k_tok)[which][:, b, c * P:(c + 1) * P],
                                      ident[:, :])
                mm.then_inc(qk_turned, 1)

            def scores(b):
                pe.wait_ge(qk_copied, 2 * b + 2)
                t = slice(b * P, (b + 1) * P)
                for r in range(4):
                    if b:
                        pe.wait_ge(masked, 4 * (b - 1) + r + 1)
                    f = slice(HD * r, HD * (r + 1))
                    for c in range(4):
                        mm = pe.matmul(banks[r][:, c * P:(c + 1) * P], QT[f, c, t], KT[f, c, t], start=True, stop=True)
                    mm.then_inc(scores_done, 1)

            pe.wait_ge(v_read, B)
            scores(0)
            pe.wait_ge(qk_copied, 2 * B)
            for b in range(B):
                for r in range(4):
                    pe.wait_ge(normalised, 4 * b + r + 1)
                    if b and r != 1:
                        pe.wait_ge({0: o_low, 2: write.side_done, 3: write.delta_done}[r], b)
                    for c in range(4):
                        mm = pe.transpose(banks[4 + r][:, c * P:(c + 1) * P], S[:, 4 * r + c, :], ident[:, :])
                    mm.then_inc(prob_turned, 1)
                if b + 1 < B:
                    scores(b + 1)
                pe.wait_ge(prob_copied, 4 * (b + 1))
                for c in range(4):
                    for r in range(4):
                        f = slice(HD * (4 * c + r), HD * (4 * c + r + 1))
                        mm = pe.matmul(banks[4][HD * r:HD * (r + 1), c * P:(c + 1) * P], V[:, b, f], PT[:, 4 * r + c, :],
                                       start=True, stop=True)
                mm.then_inc(pv_done, 1)
                pe.wait_ge(o_low, b + 1)
                side_products(pe, st, SIDE, 4, OH, OL, banks[6][:, 0:P], slice(b * P, (b + 1) * P), b == B - 1,
                              side_product_done)
                write.turn_side(pe, banks[6][:, P:2 * P], b)
                write.expand_delta(pe, banks[7], b)
            for k in range(4):
                st.product_tokens(pe, 0, SIDE + 1 + k, OH[:, k, :], OL[:, k, :], banks[0:4], k == 0, k == 3)


def xattn_mlp(nc, R, H, ident, read_w, wstream, gamma_d, beta_d, side_bias_d, du_d):
    OUTS = 2
    M = 2048
    MB = M // NT
    GATE = 0
    WOD = GATE + 8 * MB
    TILES = WOD + M // P + M // P // 4

    with ExitStack() as ctx:
        s = Scope(nc, ctx, "m_")
        banks = s.banks()
        turned = Copied(s, [H[:, b, :] for b in range(B)], ident)
        XH, XL = turned.XH, turned.XL
        gate = turned.XT
        st = Stream(s, TILES, wstream)
        YH = s.sb("YH", [P, 4 * OUTS, TOK], F32R)
        YL = s.sb("YL", [P, 4 * OUTS, TOK], F32R)
        Y = s.over("YH", 0, "Y", [P, B, OUTS, XH_])
        F = [s.sb(f"F{n}", [P, TOK]) for n in range(2)]
        gamma = s.sb("gamma", [P, 4 * OUTS])
        beta = s.sb("beta", [P, 4 * OUTS])
        read = Read(s, OUTS, turned, s.over("XL", 12, "read_w", [P, KD // PIECE, NT]), Y, YH, YL, F, gamma, beta, ident)
        side_bias = s.sb("side_bias", [P, 1])
        DU = s.sb("DU", [9, XH_])
        write = Write(s, H, R, [s.over(x, row, f"G{n}", [P, C, XH_]) for n, (x, row) in
                                enumerate((("YH", 0), ("YH", 4), ("YL", 0), ("YL", 4)))],
                      F[1][:, :].rearrange("p (b n) -> p b n", b=B), F[0], ident, side_bias, DU)
        small_loaded = s.sem("small_loaded")
        silu_done = s.sem("silu_done")
        unit_done = s.sem("unit_done")
        unit_high = s.sem("unit_high")
        unit_low = s.sem("unit_low")
        block = ctx.enter_context(nc.Block())
        OUT = WOD + M // P // 4
        PRE = (banks[2], banks[3], banks[0], banks[1])

        @block.sync
        def _(sp):
            for dst, src in ((gamma[:, :], gamma_d), (beta[:, :], beta_d),
                             (side_bias[:, :], side_bias_d), (DU[:, :], du_d)):
                sp.dma_start(dst, src).then_inc(small_loaded, 16)
            read.load(sp, read_w)
            st.loads(sp)

        @block.gpsimd
        def _(pool):
            read.pool(pool)
            write.pool(pool)
            write.pool_update(pool)

        def piece(x, m, c):
            return x[:, bass.ds(4 * m + c, 1), :].rearrange("p a n -> p (a n)")

        @block.vector
        def _(dve):
            turned.copy(dve, banks[0:4], 0, 1)
            turned.copy(dve, banks[0:4], 1, 1)
            for b in range(2, B):
                turned.copy(dve, banks[0:4], b, 1)
                read.norm(dve, b - 2)
            read.norm(dve, 2)
            read.norm(dve, 3)
            st.begin_vector(dve)
            for n in range(4 * OUTS):
                read.low_part(dve, n)

            def unit(m, c):
                if c == 0:
                    dve.wait_ge(st.used, m * ROUND + GATE + 8)
                dve.wait_ge(silu_done, 4 * m + c + 1)
                if c >= 2:
                    dve.wait_ge(unit_low, 4 * m + c - 1)
                dve.tensor_tensor(F[c % 2][:, :], banks[4 + c][:, :], piece(gate, m, c), ALU.mult).then_inc(unit_done, 1)

            def low_of_unit(m, c):
                dve.wait_ge(unit_high, 4 * m + c + 1)
                dve.tensor_tensor(piece(XL, m, c), F[c % 2][:, :], f32(piece(XH, m, c)), ALU.subtract).then_inc(unit_low, 1)

            def units_at(m, t):
                if t < 4:
                    unit(m, t)
                if 1 <= t < 5:
                    low_of_unit(m, t - 1)
                if t == 4:
                    dve.wait_ge(unit_low, 4 * m + 4)

            for t in range(8):
                st.at_vector(dve, 0, GATE + t)
            with dve.Fori(1, MB) as m:
                for t in range(8):
                    st.at_vector(dve, m, GATE + t)
                    units_at(m - 1, t)
            for t in range(5):
                st.at_vector(dve, 0, WOD + t)
                units_at(MB - 1, t)
            for n, t in enumerate(range(OUT + 1, TILES)):
                st.at_vector(dve, 0, t)
                if n == 0:
                    for b in range(B):
                        write.copy_turned(dve, banks[1][:, b * P:(b + 1) * P], b, B)
                if n in (4, 5):
                    for b in (2 * n - 8, 2 * n - 7):
                        write.softplus(dve, PRE[b], b)
                if n in (7, 9, 11, 13):
                    write.fold(dve, (n - 7) // 2)
            dve.wait_ge(st.used, TILES)
            write.update(dve, banks[4:8])

        @block.scalar
        def _(act):
            turned.copy(act, banks[0:4], 0, 0)
            turned.copy(act, banks[0:4], 1, 0)
            for b in range(B):
                read.read_sums(act, banks[4:8], b)
                if b + 2 < B:
                    turned.copy(act, banks[0:4], b + 2, 0)
            act.wait_ge(small_loaded, 64)
            st.begin_scalar(act)
            for n in range(4 * OUTS):
                read.affine(act, banks, n, first=4 * OUTS)

            def silu(m, c):
                if c == 0:
                    act.wait_ge(st.used, m * ROUND + GATE + 4)
                act.activation(piece(gate, m, c), banks[c][:, :], ACT.Silu).then_inc(silu_done, 1)

            def high_of_unit(m, c):
                act.wait_ge(unit_done, 4 * m + c + 1)
                act.activation(piece(XH, m, c), F[c % 2][:, :], ACT.Copy).then_inc(unit_high, 1)

            def block_of(m, first):
                for t in range(8):
                    st.at_scalar(act, m, GATE + t)
                    if t < 4 and not first:
                        high_of_unit(m - 1, t)
                    if t >= 4:
                        silu(m, t - 4)

            block_of(0, True)
            with act.Fori(1, MB) as m:
                block_of(m, False)
            for t in range(4):
                st.at_scalar(act, 0, WOD + t)
                high_of_unit(MB - 1, t)
            for n, t in enumerate(range(OUT, TILES)):
                st.at_scalar(act, 0, t)
                if n == 0:
                    act.wait_ge(st.used, OUT)
                    for b in range(B):
                        write.add_bias(act, banks[0][:, b * P:(b + 1) * P], b)
                if n in (2, 3):
                    for b in (2 * n - 4, 2 * n - 3):
                        write.exponents(act, PRE[b], b)
                if n == 4:
                    for b in range(B):
                        write.logs(act, b)
                if 8 <= n < 8 + B:
                    write.decays(act, n - 8)

        @block.tensor
        def _(pe):
            turned.turn(pe, banks[0:4], 0)
            turned.turn(pe, banks[0:4], 1)
            for b in range(B):
                read.sums(pe, banks[4:8], b)
                if b + 2 < B:
                    turned.turn(pe, banks[0:4], b + 2)
            for n in range(4 * OUTS):
                if n >= 4 and n < 8:
                    pe.wait_ge(read.y_read, 4 * (B - 1) + n - 3)
                read.turn(pe, banks, n)

            def block_of(m, first):
                for o in range(2):
                    def free(c):
                        if first:
                            pe.wait_ge(read.affine_done, 4 * o + c + 1)
                        else:
                            pe.wait_ge((silu_done, unit_done)[o], 4 * m - 4 + c + 1)
                    for k in range(4):
                        if first:
                            pe.wait_ge(read.lo_done, 4 * o + k + 1)
                        st.product_features(pe, m, GATE + 4 * o + k, YH[:, 4 * o + k, :], YL[:, 4 * o + k, :],
                                            banks[4 * o:4 * o + 4], k == 0, k == 3, free if k == 0 else None)

            block_of(0, True)
            with pe.Fori(1, MB) as m:
                block_of(m, False)

            pe.wait_ge(silu_done, 4 * MB)
            side_products(pe, st, WOD, M // P, XH, XL, banks[0][:, :], slice(0, TOK), True,
                          ready=lambda t: pe.wait_ge(unit_low, 4 * t + 4))
            for k in range(M // P):
                st.product_tokens(pe, 0, OUT + k, XH[:, k, :], XL[:, k, :], banks[4:8], k == 0, k == M // P - 1)
                if k == 0:
                    for b in range(B):
                        write.turn_side(pe, banks[1][:, b * P:(b + 1) * P], b)
                        if b < 2:
                            write.expand_delta(pe, PRE[b], b)
                if k == 1:
                    pe.wait_ge(write.side_done, B)
                    for b in (2, 3):
                        write.expand_delta(pe, PRE[b], b)


def routed_ffn(nc, R, ident, wstream, router, iota, bias, out):
    EXPERTS = 16
    RANK = 64
    SCALING = 0.5
    AR = RANK + EXPERTS
    KE = EXPERTS * RANK // P
    NB = D // NT
    PER = KD + KE
    TILES = NB * PER
    BIG = 1024.0

    with ExitStack() as ctx:
        s = Scope(nc, ctx, "f_")
        banks = s.banks()
        EH = s.sb("EH", [P, KE, TOK], F32R)
        EL = s.sb("EL", [P, KE, TOK], F32R)
        xn = [s.sb(f"xn{n}", [P, D]) for n in range(2)]
        ET = [xn[n][:, 0:EXPERTS * RANK] for n in range(2)]
        norm = Norm(s, R, ident, [x[:, :] for x in xn])
        st = Stream(s, TILES, wstream)
        A = s.sb("A", [P, KD, AR])
        AH = s.sb("AH", [P, KD, AR], F32R)
        AL = s.sb("AL", [P, KD, AR], F32R)
        bias_all = s.sb("bias", [P, D])
        io = s.sb("iota", [P, EXPERTS])
        sideT = s.sb("sideT", [AR, TOK])
        res = s.sb("res", [P, B, AR])
        pr = s.sb("probs", [P, B, EXPERTS])
        one = [s.sb(f"one{n}", [P, B, EXPERTS]) for n in range(2)]
        key = s.sb("key", [P, B, EXPERTS])
        wt = s.sb("weights", [P, B, EXPERTS])
        small = s.sb("small", [P, 8, B])

        small_loaded = s.sem("small_loaded")
        a_high = s.sem("a_high")
        a_low = s.sem("a_low")
        bias_added = s.sem("bias_added")
        side_done = s.sem("side_done")
        side_copied = s.sem("side_copied")
        res_done = s.sem("res_done")
        steps = s.sem("routing_steps")
        shifted = s.sem("logits_shifted")
        exp_done = s.sem("exp_done")
        rows_done = s.sem("rows_done")
        rows_turned = s.sem("rows_turned")
        rows_high = s.sem("rows_high")
        rows_low = s.sem("rows_low")
        out_added = s.sem("out_added")
        out_stored = s.sem("out_stored")
        block = ctx.enter_context(nc.Block())

        ROWS_AT = 4
        ROUNDS = PER // ROUND
        bce = lambda ap: ap.unsqueeze(2).broadcast_to([P, B, EXPERTS])

        @block.sync
        def _(sp):
            sp.dma_start(A[:, :, :], router).then_inc(small_loaded, 16)
            sp.dma_start(io[:, :], iota).then_inc(small_loaded, 16)
            sp.dma_start(bias_all[:, :], bias.broadcast_to([P, D])).then_inc(small_loaded, 16)
            st.loads(sp)

        @block.gpsimd
        def _(pool):
            norm.pool(pool)
            pool.wait_ge(small_loaded, 48)
            for b in range(B):
                pool.wait_ge(norm.scaled, b + 1)
                pool.tensor_tensor(R[:, b, :], R[:, b, :], bias_all[:, :], ALU.add).then_inc(bias_added, 1)

        @block.vector
        def _(dve):
            link = Chain(dve, steps)
            norm.vector(dve, banks)
            dve.wait_ge(a_high, 1)
            dve.tensor_tensor(AL[:, :, :], A[:, :, :], f32(AH[:, :, :]), ALU.subtract).then_inc(a_low, 1)
            st.begin_vector(dve)
            for t in range(2):
                st.at_vector(dve, 0, t)

            dve.wait_ge(res_done, 1)
            link(dve.tensor_copy(res[:, :, :], banks[5][:, 0:B * AR].rearrange("p (b n) -> p b n", b=B)))
            logits = res[:, :, RANK:AR]
            link(dve.tensor_reduce(small[:, 0, :], logits, AXX, ALU.max))
            dve.tensor_tensor(pr[:, :, :], logits, bce(small[:, 0, :]), ALU.subtract).then_inc(shifted, 1)
            dve.wait_ge(exp_done, 1)
            link(dve.tensor_reduce(small[:, 1, :], pr[:, :, :], AXX, ALU.add))
            link(dve.reciprocal(small[:, 2, :], small[:, 1, :]))
            link(dve.tensor_tensor(pr[:, :, :], pr[:, :, :], bce(small[:, 2, :]), ALU.mult))
            for n in range(2):
                top = small[:, 3 + n, :]
                link(dve.tensor_reduce(top, pr[:, :, :], AXX, ALU.max))
                link(dve.tensor_tensor(key[:, :, :], pr[:, :, :], bce(top), ALU.is_lt))
                link(dve.scalar_tensor_tensor(out=key[:, :, :], in0=key[:, :, :], scalar=BIG,
                                              in1=io[:, :].unsqueeze(1).broadcast_to([P, B, EXPERTS]),
                                              op0=ALU.mult, op1=ALU.add))
                link(dve.tensor_reduce(small[:, 5, :], key[:, :, :], AXX, ALU.min))
                link(dve.tensor_tensor(one[n][:, :, :], key[:, :, :], bce(small[:, 5, :]), ALU.is_equal))
                if n == 0:
                    link(dve.scalar_tensor_tensor(out=pr[:, :, :], in0=one[0][:, :, :], scalar=-2.0,
                                                  in1=pr[:, :, :], op0=ALU.mult, op1=ALU.add))
            link(dve.tensor_tensor(small[:, 6, :], small[:, 3, :], small[:, 4, :], ALU.add))
            link(dve.tensor_scalar(small[:, 6, :], small[:, 6, :], 1e-6, None, ALU.add))
            link(dve.reciprocal(small[:, 7, :], small[:, 6, :]))
            link(dve.tensor_scalar(small[:, 7, :], small[:, 7, :], SCALING, None, ALU.mult))
            for n in range(2):
                link(dve.tensor_tensor(small[:, 3 + n, :], small[:, 3 + n, :], small[:, 7, :], ALU.mult))
                link(dve.tensor_tensor(one[n][:, :, :], one[n][:, :, :], bce(small[:, 3 + n, :]), ALU.mult))
            link(dve.tensor_tensor(wt[:, :, :], one[0][:, :, :], one[1][:, :, :], ALU.add))

            def rows(b):
                if b >= 2:
                    dve.wait_ge(rows_turned, 2 * (b - 1))
                dve.tensor_tensor(ET[b % 2].rearrange("p (e r) -> p e r", e=EXPERTS),
                                  wt[:, b, :].unsqueeze(2).broadcast_to([P, EXPERTS, RANK]),
                                  res[:, b, 0:RANK].unsqueeze(1).broadcast_to([P, EXPERTS, RANK]),
                                  ALU.mult).then_inc(rows_done, 1)

            def rows_low_parts(n):
                b, g = n // 2, n % 2
                dve.wait_ge(rows_high, n + 1)
                part = (slice(None), slice(4 * g, 4 * g + 4), slice(b * P, (b + 1) * P))
                dve.tensor_tensor(EL[part], banks[4 + n % 4][:, :].rearrange("p (c t) -> p c t", c=4), f32(EH[part]),
                                  ALU.subtract).then_inc(rows_low, 1)

            def add_output(r, t, n, b):
                dve.wait_ge(st.used, r * ROUND + t + 1)
                o = R[:, b, bass.ds(n * NT, NT)]
                dve.tensor_tensor(o, banks[b][:, :], o, ALU.add).then_inc(out_added, 1)

            for t in range(2, PER):
                st.at_vector(dve, 0, t)
                if ROWS_AT - 2 <= t < ROWS_AT - 2 + B:
                    rows(t - ROWS_AT + 2)
                if ROWS_AT <= t < ROWS_AT + 2 * B:
                    rows_low_parts(t - ROWS_AT)
            dve.wait_ge(bias_added, B)
            for b in range(B):
                add_output(0, PER - 1, 0, b)

            def block_of(n):
                for t in range(PER):
                    st.at_vector(dve, n * ROUNDS, t)
                for b in range(B):
                    add_output(n * ROUNDS, PER - 1, n, b)

            with dve.Fori(1, NB - 1) as n:
                block_of(n)
            block_of(NB - 1)

        @block.scalar
        def _(act):
            norm.scalar(act, banks)
            act.wait_ge(small_loaded, 48)
            act.activation(AH[:, :, :], A[:, :, :], ACT.Copy).then_inc(a_high, 1)
            st.begin_scalar(act)

            def rows_high_parts(n):
                b, g = n // 2, n % 2
                act.wait_ge(rows_turned, n + 1)
                act.activation(EH[:, 4 * g:4 * g + 4, b * P:(b + 1) * P],
                               banks[4 + n % 4][:, :].rearrange("p (c t) -> p c t", c=4), ACT.Copy).then_inc(rows_high, 1)

            def store(n):
                act.wait_ge(out_added, (n + 1) * B)
                act.dma_start(out[:, :, bass.ds(n * NT, NT)].rearrange("b p d -> p b d"),
                              R[:, :, bass.ds(n * NT, NT)]).then_inc(out_stored, 16)

            for t in range(PER):
                st.at_scalar(act, 0, t)
                if t == 0:
                    act.wait_ge(side_done, 1)
                    act.activation(sideT[:, :], banks[4][0:AR, :], ACT.Copy).then_inc(side_copied, 1)
                if t == 2:
                    act.wait_ge(shifted, 1)
                    act.activation(pr[:, :, :], pr[:, :, :], ACT.Exp).then_inc(exp_done, 1)
                if ROWS_AT <= t < ROWS_AT + 2 * B:
                    rows_high_parts(t - ROWS_AT)

            def block_of(n):
                for t in range(PER):
                    st.at_scalar(act, n * ROUNDS, t)
                    if t == 4:
                        store(n - 1)

            with act.Fori(1, NB - 1) as n:
                block_of(n)
            block_of(NB - 1)
            store(NB - 1)
            act.wait_ge(out_stored, 16 * NB)

        @block.tensor
        def _(pe):
            XH, XL = norm.XH, norm.XL
            norm.tensor(pe, banks)
            pe.wait_ge(norm.lo_done, 4 * B)
            pe.wait_ge(a_low, 1)
            for k in range(KD):
                pe.matmul(banks[4][0:AR, :], AH[:, k, :], XH[:, k, :], start=k == 0, stop=False)
                pe.matmul(banks[4][0:AR, :], AL[:, k, :], XH[:, k, :], start=False, stop=False)
                mm = pe.matmul(banks[4][0:AR, :], AH[:, k, :], XL[:, k, :], start=False, stop=k == KD - 1)
            mm.then_inc(side_done, 1)

            def turn_side():
                pe.wait_ge(side_copied, 1)
                for b in range(B):
                    mm = pe.transpose(banks[5][:, b * AR:(b + 1) * AR], sideT[:, b * P:(b + 1) * P], ident[0:AR, 0:AR])
                mm.then_inc(res_done, 1)

            def turn_rows(n):
                b, g = n // 2, n % 2
                pe.wait_ge(rows_done, b + 1)
                if n >= 4:
                    pe.wait_ge(rows_low, n - 3)
                elif n == 0:
                    pe.wait_ge(steps, 1)
                for c in range(4):
                    mm = pe.transpose(banks[4 + n % 4][:, c * P:(c + 1) * P], ET[b % 2][:, (4 * g + c) * P:(4 * g + c + 1) * P],
                                      ident[:, :])
                mm.then_inc(rows_turned, 1)

            def products(r, t, free):
                xh, xl = (XH[:, t, :], XL[:, t, :]) if t < KD else (EH[:, t - KD, :], EL[:, t - KD, :])
                st.product_tokens(pe, r, t, xh, xl, banks[0:4], t == 0, t == PER - 1, free if t == 0 else None)

            for t in range(PER):
                if t == 1:
                    turn_side()
                if ROWS_AT <= t < ROWS_AT + 2 * B:
                    turn_rows(t - ROWS_AT)
                if t == KD:
                    pe.wait_ge(rows_low, 2 * B)
                products(0, t, None)
            with pe.Fori(1, NB) as n:
                for t in range(PER):
                    products(n * ROUNDS, t, lambda b: pe.wait_ge(out_added, (n - 1) * B + b + 1))


def _tiles(w, k, n):
    t = w[k * P:(k + 1) * P, n * NT:(n + 1) * NT]
    return t if t.shape[1] == NT else np.pad(t, ((0, 0), (0, NT - t.shape[1])))


def _stream(tiles):
    tiles = list(tiles) + [np.zeros_like(tiles[0])] * (-len(tiles) % ROUND)
    return np.ascontiguousarray(np.stack(tiles).reshape(-1, GROUP, P, NT).transpose(0, 2, 1, 3))


def _read_tiles(w):
    h, outs, c = w.shape
    full = np.zeros((h // 32, 32, c, P // 32, 32), w.dtype)
    for i in range(32):
        full[:, i, :, :outs, i] = w.reshape(h // 32, 32, outs, c)[:, i].transpose(0, 2, 1)
    pieces = full.reshape(KD, P, P)
    return pieces.reshape(KD // PIECE, PIECE, P, P).transpose(2, 0, 1, 3).reshape(P, -1, NT)


def _side(wod, wab):
    n = wod.shape[1]
    A = wab[:RH * AC]
    Bp = wab[RH * AC:2 * RH * AC]
    skip = wab[2 * RH * AC:]
    low = wod[XH_:]
    return np.concatenate([low, np.zeros((RH - low.shape[0], n), wod.dtype), skip, A, Bp], 0).T


def _side_tiles(wod, wab):
    w = _side(wod, wab)
    k = w.shape[0] // P
    return list(w.reshape(k // 4, 4, P, P).transpose(0, 2, 1, 3).reshape(k // 4, P, NT))


def _side_bias(b):
    one = np.zeros(RH, b.dtype)
    one[8] = 1.0
    return np.concatenate([one, b[2 * RH * AC:], b[:2 * RH * AC]]).reshape(P, 1)


def _columns(g):
    return np.ascontiguousarray(g.reshape(-1, P).T)


def _layouts(i):
    x = lambda name: np.asarray(i["L0_xattn_" + name])
    out = {"x": np.asarray(i["x"]), "pos": np.ascontiguousarray(np.asarray(i["pos_BxS"]).T)}
    wod = x("attn_wod_w")
    out["a_stream"] = _stream([_tiles(x("qkv_w")[o].T, k, 0) for o in range(3) for k in range(4)]
                              + _side_tiles(wod, x("attn_wab_w")) + [_tiles(wod[:XH_].T, k, 0) for k in range(4)])
    ctx = np.asarray(i["ctx_1024"])
    wod = x("mlp_wod_w")
    out["m_stream"] = _stream([_tiles(ctx[o].T, k, n) for n in range(4) for o in range(2) for k in range(4)]
                              + _side_tiles(wod, x("mlp_wab_w")) + [_tiles(wod[:XH_].T, k, 0) for k in range(16)])
    for p, q in (("a", "attn"), ("m", "mlp")):
        out[p + "_read"] = _read_tiles(x(q + "_read_w"))
        out[p + "_gamma"] = _columns(x(q + "_read_g"))
        out[p + "_beta"] = _columns(x(q + "_read_b"))
        out[p + "_side_bias"] = _side_bias(x(q + "_wab_b"))
        out[p + "_du"] = np.concatenate([x(q + "_du_w").T, x(q + "_du_b")[None]], 0)
    order = [(m, k, n) for m, n in (("k", 0), ("k", 1), ("v", 0), ("q", 0), ("v", 1)) for k in range(KD)]
    for step in range(1, 9):
        order += [("q", k, step) for k in range(KD) if step < 8]
        order += [("o", 4 * step - 4 + j, n) for n in range(4) for j in range(4)]
    w = {m: np.asarray(i["L0_attn_qw_" + m]) for m in "qkvo"}
    sc = {m: np.asarray(i["L0_attn_scales_" + m]) for m in "qkvo"}
    out["g_stream"] = _stream([_tiles(w[m], k, n) for m, k, n in order])
    out["g_scales"] = np.stack([sc[m][k, n * NT:(n + 1) * NT] for m, k, n in order]).reshape(-1, GROUP * NT)
    base = np.concatenate([np.asarray(i["L0_ffn_base_w"]).T, np.asarray(i["L0_ffn_B"]).transpose(0, 2, 1).reshape(-1, D)], 0)
    out["f_stream"] = _stream([_tiles(base, k, n) for n in range(D // NT) for k in range(base.shape[0] // P)])
    router = np.concatenate([np.asarray(i["L0_ffn_A"]), np.asarray(i["L0_ffn_router_w"])], 0).T
    out["f_router"] = np.ascontiguousarray(router.reshape(KD, P, -1).transpose(1, 0, 2))
    out["f_bias"] = np.asarray(i["L0_ffn_base_b"]).reshape(1, D)

    half = 16
    inv = np.float32(1.0) / np.float32(10000.0) ** (np.arange(half, dtype=np.float32) / np.float32(half))
    out["x_inv"] = np.tile(inv.astype(np.float32), (P, 1))
    inv = (np.float32(1.0) / np.float32(10000.0) ** (np.arange(0, P, 2, dtype=np.float32) / np.float32(P))).astype(np.float32)
    ang = (np.arange(P, dtype=np.float32)[None, :] * inv[:, None]).astype(np.float64)
    cos, sin = np.cos(ang), np.sin(ang)
    out["g_rope"] = np.stack([np.concatenate([cos, cos]), np.concatenate([sin, -sin])], 1).astype(np.float32)
    out["causal"] = np.where(np.tril(np.ones((P, P))) > 0, 0.0, -3e38).astype(np.float32)
    out["iota"] = np.tile(np.arange(16, dtype=np.float32), (P, 1))
    out["ident"] = np.eye(P, dtype=np.float32)
    return {k: np.ascontiguousarray(v) for k, v in out.items()}


def perceiver_layer(nc, t, out):
    with ExitStack() as ctx:
        R = ctx.enter_context(nc.sbuf_tensor("residual", [P, B, D], F32))
        ident = ctx.enter_context(nc.sbuf_tensor("identity", [P, P], F32))
        ident_loaded = ctx.enter_context(nc.semaphore("ident_loaded"))
        with nc.Block() as block:
            @block.sync
            def _(sp):
                sp.dma_start(ident[:, :], t["ident"]).then_inc(ident_loaded, 16)
                sp.wait_ge(ident_loaded, 16)

        with nc.sbuf_tensor("hidden", [P, B, D], F32) as H:
            xattn_attention(nc, R, H, ident, t["x"], t["a_read"], t["a_stream"], t["a_gamma"], t["a_beta"], t["pos"], t["x_inv"],
                            t["causal"], t["a_side_bias"], t["a_du"])
            xattn_mlp(nc, R, H, ident, t["m_read"], t["m_stream"], t["m_gamma"], t["m_beta"], t["m_side_bias"], t["m_du"])
        grouped_query_attention(nc, R, ident, t["g_stream"], t["g_scales"], t["g_rope"], t["causal"])
        routed_ffn(nc, R, ident, t["f_stream"], t["f_router"], t["iota"], t["f_bias"], out)


def kernel(**inputs):
    import concourse.bacc as bacc
    from concourse.bass_utils import run_bass_kernel_spmd

    nc = bacc.Bacc("TRN2", target_bir_lowering=False, num_devices=1)
    arrays = _layouts(inputs)
    tensors = {n: nc.dram_tensor("in_" + n, a.shape, mybir.dt.from_np(a.dtype), kind="ExternalInput").ap() for n, a in arrays.items()}
    out = nc.dram_tensor("out", (B, P, D), F32, kind="ExternalOutput").ap()
    perceiver_layer(nc, tensors, out)
    r = run_bass_kernel_spmd(nc, [{"in_" + n: a for n, a in arrays.items()}], core_ids=[0])
    return r.results[0]["out"]
```

```python
import numpy as np
import concourse.bass as bass
from concourse import mybir
from contextlib import ExitStack

F32 = mybir.dt.float32
F32R = mybir.dt.float32r
I32 = mybir.dt.int32
ALU = mybir.AluOpType
ACT = mybir.ActivationFunctionType
AXX = mybir.AxisListType.X

P = 128
B = 4
D = 2048
TOK = B * P
NT = 512
KD = D // P
EPS = 1e-5
GROUP = 2
RAW_SLOTS = 4
SCALE_SLOTS = 2
PART_SLOTS = 4


class Chain:

    def __init__(self, eng, sem, base=0):
        self.eng, self.sem, self.base, self.n = eng, sem, base, 0

    def __call__(self, ins):
        self.n += 1
        ins.then_inc(self.sem, 1)
        self.eng.wait_ge(self.sem, self.base + self.n)
        return ins


class Scope:

    def __init__(self, nc, ctx, prefix):
        self.nc, self.ctx, self.prefix, self.at, self.sems = nc, ctx, prefix, {}, []
        ctx.callback(self.end)

    def sb(self, name, shape, dt=F32):
        self.at[name] = -(-self.nc.sbuf_base // 32) * 32
        return self.ctx.enter_context(self.nc.sbuf_tensor(self.prefix + name, shape, dt))

    def over(self, host, row, name, shape, dt=F32):
        return self.nc.alloc_sbuf_tensor_at(self.prefix + name, shape, dt, offset=self.at[host] + row * 4 * NT)

    def banks(self):
        return [self.ctx.enter_context(self.nc.psum_tensor(f"{self.prefix}bank{i}", [P, NT], F32)) for i in range(8)]

    def sem(self, name):
        self.sems.append(self.nc.alloc_semaphore(name=self.prefix + name))
        return self.sems[-1]

    def end(self):
        self.nc.clear_and_free_semaphores(self.sems)
        self.nc.all_engine_barrier()


def f32(ap):
    return ap.bitcast(F32)


ROUND = RAW_SLOTS * GROUP
LEAD = 3
SSM_EPS = 1e-5
ZERO = 8.0


class Turned:

    def __init__(self, s, rows, ident):
        self.rows, self.ident = rows, ident
        self.XH = s.sb("XH", [P, KD, TOK], F32R)
        self.XL = s.sb("XL", [P, KD, TOK], F32R)
        self.turned = s.sem("x_turned")
        self.hi_done = s.sem("x_hi_done")
        self.lo_done = s.sem("x_lo_done")

    def part(self, x, b, g):
        return x[:, 4 * g:4 * g + 4, b * P:(b + 1) * P]

    def free(self, eng, n):
        eng.wait_ge(self.lo_done, n + 1)

    def turn(self, eng, banks, b):
        for g in range(4):
            n = 4 * b + g
            bank = banks[n % len(banks)]
            if n >= len(banks):
                self.free(eng, n - len(banks))
            for c in range(4):
                last = eng.transpose(bank[:, c * P:(c + 1) * P],
                                     self.rows[b % len(self.rows)][:, (4 * g + c) * P:(4 * g + c + 1) * P], self.ident[:, :])
            last.then_inc(self.turned, 1)

    def high_parts(self, eng, banks, b):
        for g in range(4):
            n = 4 * b + g
            eng.wait_ge(self.turned, n + 1)
            eng.activation(self.part(self.XH, b, g), banks[n % len(banks)][:, :].rearrange("p (c t) -> p c t", c=4),
                           ACT.Copy).then_inc(self.hi_done, 1)

    def low_parts(self, eng, banks, b):
        for g in range(4):
            n = 4 * b + g
            eng.wait_ge(self.hi_done, n + 1)
            eng.tensor_tensor(self.part(self.XL, b, g), banks[n % len(banks)][:, :].rearrange("p (c t) -> p c t", c=4),
                              f32(self.part(self.XH, b, g)), ALU.subtract).then_inc(self.lo_done, 1)


class Copied(Turned):

    def __init__(self, s, rows, ident):
        Turned.__init__(self, s, rows, ident)
        self.XT = s.over("XH", 0, "XT", [P, KD, TOK])

    def free(self, eng, n):
        eng.wait_ge((self.hi_done, self.lo_done)[n % 2], n // 2 + 1)

    def copy(self, eng, banks, b, odd):
        for g in (odd, odd + 2):
            n = 4 * b + g
            src = banks[n % len(banks)][:, :].rearrange("p (c t) -> p c t", c=4)
            eng.wait_ge(self.turned, n + 1)
            if odd:
                eng.tensor_copy(self.part(self.XT, b, g), src).then_inc(self.lo_done, 1)
            else:
                eng.activation(self.part(self.XT, b, g), src, ACT.Copy).then_inc(self.hi_done, 1)


class Norm(Turned):

    def __init__(self, s, R, ident, rows):
        Turned.__init__(self, s, rows, ident)
        self.R = R
        self.stats = s.sb("ln_stats", [P, B, 4, 6])
        self.mv = s.sb("ln_mv", [P, B, 2])
        self.veps = s.sb("ln_veps", [P, B])
        self.rstd = s.sb("ln_rstd", [P, B])
        self.nhalf = s.sb("ln_nhalf", [P, 1])
        self.stats_done = s.sem("ln_stats_done")
        self.var_done = s.sem("ln_var_done")
        self.rstd_steps = s.sem("ln_rstd_steps")
        self.scaled = s.sem("ln_scaled")

    def pool(self, eng):
        eng.memset(self.nhalf[:, :], -0.5).then_inc(self.rstd_steps, 1)
        for b in range(B):
            one = slice(b, b + 1)
            eng.wait_ge(self.var_done, b + 1)
            eng.tensor_scalar(self.veps[:, one], self.mv[:, b, 1:2], EPS, None, ALU.add).then_inc(self.rstd_steps, 1)
            eng.wait_ge(self.rstd_steps, 2 * b + 2)
            eng.tensor_tensor(self.rstd[:, one], self.veps[:, one], self.nhalf[:, :], ALU.pow).then_inc(self.rstd_steps, 1)

    def moments(self, eng, b):
        for c in range(4):
            last = eng.bn_stats(self.stats[:, b, c, :], self.R[:, b, c * NT:(c + 1) * NT])
        last.then_inc(self.stats_done, 1)
        eng.wait_ge(self.stats_done, b + 1)
        eng.bn_aggr(self.mv[:, b, :], self.stats[:, b, :, :].rearrange("p c s -> p (c s)")).then_inc(self.var_done, 1)

    def scale(self, eng, b):
        eng.wait_ge(self.var_done, b + 1)
        eng.wait_ge(self.rstd_steps, 2 * b + 3)
        if b >= len(self.rows):
            eng.wait_ge(self.turned, 4 * (b + 1 - len(self.rows)))
        eng.tensor_scalar(self.rows[b % len(self.rows)], self.R[:, b, :], self.mv[:, b, 0:1], self.rstd[:, b:b + 1],
                          ALU.subtract, ALU.mult).then_inc(self.scaled, 1)


    def vector(self, eng, banks, st):
        self.moments(eng, 0)
        for b in range(B):
            if b + 1 < B:
                self.moments(eng, b + 1)
            self.scale(eng, b)
            if b == 0:
                st.begin_vector(eng)
                for t in range(PART_SLOTS - LEAD):
                    st.at_vector(eng, 0, t)
            else:
                self.low_parts(eng, banks, b - 1)
        self.low_parts(eng, banks, B - 1)

    def scalar(self, eng, banks, st):
        st.begin_scalar(eng)
        for t in range(PART_SLOTS - LEAD):
            st.at_scalar(eng, 0, t)
        for b in range(B):
            self.high_parts(eng, banks, b)

    def tensor(self, eng, banks, st, use):
        def turn(b):
            eng.wait_ge(self.scaled, b + 1)
            self.turn(eng, banks, b)

        def ready(b):
            if b + 1 < B:
                turn(b + 1)
            eng.wait_ge(self.lo_done, 4 * (b + 1))

        turn(0)
        st.products_by_batch(eng, 0, 0, self.XH, self.XL, use, True, False, ready=ready)


class CopiedNorm(Copied, Norm):

    def __init__(self, s, R, ident, rows):
        Norm.__init__(self, s, R, ident, rows)
        self.XT = s.over("XH", 0, "XT", [P, KD, TOK])


class Stream:

    def __init__(self, s, tiles, dram, scales=None):
        self.tiles, self.dram, self.scales = tiles, dram, scales
        self.raw = [s.sb(f"raw{n}", [P, GROUP, NT], I32 if scales is not None else F32) for n in range(RAW_SLOTS)]
        if scales is not None:
            self.scale = [s.sb(f"scale{n}", [P, GROUP * NT]) for n in range(SCALE_SLOTS)]
            self.scale_loaded = [s.sem(f"scale_loaded{n}") for n in range(SCALE_SLOTS)]
            self.scaled = s.sem("tile_scaled")
        self.WH = [s.sb(f"WH{n}", [P, NT], F32R) for n in range(PART_SLOTS)]
        self.WL = [s.sb(f"WL{n}", [P, NT], F32R) for n in range(PART_SLOTS)]
        self.raw_loaded = [s.sem(f"raw_loaded{n}") for n in range(RAW_SLOTS)]
        self.hi_done = s.sem("tile_hi_done")
        self.lo_done = s.sem("tile_lo_done")
        self.used = s.sem("tile_used")

    def load_round(self, eng, r, first):
        for g in range(RAW_SLOTS):
            if not first:
                eng.wait_ge(self.lo_done, r * ROUND + (g + 1) * GROUP - ROUND)
            q = r * RAW_SLOTS + g
            eng.dma_start(self.raw[g][:, :, :], self.dram[bass.ds(q, 1), :, :, :].rearrange("a p t n -> (a p) t n"))\
               .then_inc(self.raw_loaded[g], 16)
            if self.scales is not None:
                if not first or g >= SCALE_SLOTS:
                    eng.wait_ge(self.scaled, r * ROUND + (g + 1 - SCALE_SLOTS) * GROUP)
                eng.dma_start(self.scale[g % SCALE_SLOTS][:, :],
                              self.scales[bass.ds(q, 1), :].broadcast_to([P, GROUP * NT]))\
                   .then_inc(self.scale_loaded[g % SCALE_SLOTS], 16)

    def loads(self, eng):
        self.load_round(eng, 0, True)
        rounds = -(-self.tiles // ROUND)
        with eng.Fori(1, rounds) as r:
            self.load_round(eng, r, False)
        for loaded in self.raw_loaded:
            eng.wait_ge(loaded, 16 * rounds)

    def w(self, t):
        raw = self.raw[t % ROUND // GROUP][:, t % GROUP, :]
        return raw.bitcast(F32) if self.scales is not None else raw

    def dequantise(self, eng, r, t):
        g = t % ROUND // GROUP
        if t % GROUP == 0:
            eng.wait_ge(self.raw_loaded[g], (r + t // ROUND) * 16 + 16)
            eng.wait_ge(self.scale_loaded[g % SCALE_SLOTS], (r + t // ROUND) * 32 + 16 * (g // SCALE_SLOTS + 1))
        eng.scalar_tensor_tensor(out=self.w(t), in0=self.raw[g][:, t % GROUP, :], scalar=-ZERO,
                                 in1=self.scale[g % SCALE_SLOTS][:, t % GROUP * NT:(t % GROUP + 1) * NT],
                                 op0=ALU.add, op1=ALU.mult).then_inc(self.scaled, 1)

    def high(self, eng, r, t):
        if self.scales is not None:
            eng.wait_ge(self.scaled, r * ROUND + t + 1)
        elif t % GROUP == 0:
            eng.wait_ge(self.raw_loaded[t % ROUND // GROUP], (r + t // ROUND) * 16 + 16)
        if not isinstance(r, int) or r * ROUND + t >= PART_SLOTS:
            eng.wait_ge(self.used, r * ROUND + t + 1 - PART_SLOTS)
        eng.activation(self.WH[t % PART_SLOTS][:, :], self.w(t), ACT.Copy).then_inc(self.hi_done, 1)

    def low(self, eng, r, t):
        eng.wait_ge(self.hi_done, r * ROUND + t + 1)
        eng.tensor_tensor(self.WL[t % PART_SLOTS][:, :], self.w(t), f32(self.WH[t % PART_SLOTS][:, :]),
                          ALU.subtract).then_inc(self.lo_done, 1)


    def begin_vector(self, eng):
        for t in range(LEAD + 1):
            if self.scales is not None:
                self.dequantise(eng, 0, t)
            if t:
                self.low(eng, 0, t - 1)

    def at_vector(self, eng, r, t):
        if not isinstance(r, int) or r * ROUND + t + LEAD + 1 < self.tiles:
            if self.scales is not None:
                self.dequantise(eng, r, t + LEAD + 1)
        if not isinstance(r, int) or r * ROUND + t + LEAD < self.tiles:
            self.low(eng, r, t + LEAD)

    def begin_scalar(self, eng):
        for t in range(LEAD):
            self.high(eng, 0, t)

    def at_scalar(self, eng, r, t):
        if not isinstance(r, int) or r * ROUND + t + LEAD < self.tiles:
            self.high(eng, r, t + LEAD)


    def product_features(self, eng, r, t, xh, xl, banks, first, last, free=None):
        eng.wait_ge(self.lo_done, r * ROUND + t + 1)
        wh, wl = self.WH[t % PART_SLOTS], self.WL[t % PART_SLOTS]
        for j, bank in enumerate(banks):
            if free:
                free(j)
            c = slice(j * P, (j + 1) * P)
            eng.matmul(bank[:, :], wh[:, c], xh, start=first, stop=False)
            eng.matmul(bank[:, :], wh[:, c], xl, start=False, stop=False)
            mm = eng.matmul(bank[:, :], wl[:, c], xh, start=False, stop=last)
        mm.then_inc(self.used, 1)

    def product_tokens(self, eng, r, t, xh, xl, banks, first, last, free=None):
        eng.wait_ge(self.lo_done, r * ROUND + t + 1)
        wh, wl = self.WH[t % PART_SLOTS], self.WL[t % PART_SLOTS]
        for b, bank in enumerate(banks):
            if free:
                free(b)
            c = slice(b * P, (b + 1) * P)
            eng.matmul(bank[:, :], xh[:, c], wh[:, :], start=first, stop=False)
            eng.matmul(bank[:, :], xh[:, c], wl[:, :], start=False, stop=False)
            mm = eng.matmul(bank[:, :], xl[:, c], wh[:, :], start=False, stop=last)
        mm.then_inc(self.used, 1)

    def products_by_batch(self, eng, r, t, xh, xl, banks, first, last, ready=None, done=None):
        for b, bank in enumerate(banks):
            if ready:
                ready(b)
            c = slice(b * P, (b + 1) * P)
            for j in range(PART_SLOTS):
                eng.wait_ge(self.lo_done, r * ROUND + t + j + 1)
                wh, wl = self.WH[(t + j) % PART_SLOTS], self.WL[(t + j) % PART_SLOTS]
                eng.matmul(bank[:, :], xh[:, j, c], wh[:, :], start=first and j == 0, stop=False)
                eng.matmul(bank[:, :], xh[:, j, c], wl[:, :], start=False, stop=False)
                mm = eng.matmul(bank[:, :], xl[:, j, c], wh[:, :], start=False, stop=last and j == PART_SLOTS - 1)
                if b == B - 1 and done is None:
                    mm.then_inc(self.used, 1)
            if done is not None:
                mm.then_inc(done, 1)


def grouped_query_attention(nc, R, ident, wstream, scales, rope, causal):
    NKV = 8
    REP = 4
    STEPS = NKV
    QT_TILES = KD
    O_TILES = REP * D // NT
    TILES = 4 * KD + STEPS * (QT_TILES + O_TILES)
    SCALE = float(P) ** -0.5
    HALF = P // 2
    SCORES_AT = [1, 4, 7, 10]

    with ExitStack() as ctx:
        s = Scope(nc, ctx, "g_")
        banks = s.banks()
        KT = s.sb("KT", [P, NKV, TOK])
        V = s.sb("V", [P, B, NKV * P])
        xn = [KT[:, 0:4, :].rearrange("p a n -> p (a n)"), KT[:, 4:8, :].rearrange("p a n -> p (a n)")]
        norm = Norm(s, R, ident, xn)
        st = Stream(s, TILES, wstream, scales)
        QT = s.sb("QT", [P, REP, TOK])
        turn = [s.sb(f"turn{n}", [P, TOK]) for n in range(2)]
        rt = s.sb("rope", [P, 2, P])
        mask = s.sb("mask", [P, P])
        Vcur = s.sb("Vcur", [P, B, P])
        S = s.sb("S", [P, B, P])
        E = s.sb("E", [P, B, P])
        PT = s.sb("PT", [P, TOK])
        CH = s.sb("CH", [P, REP, TOK], F32R)
        CL = s.sb("CL", [P, REP, TOK], F32R)
        nmax = [s.sb(f"nmax{n}", [P, B]) for n in range(2)]
        rsum = [s.sb(f"rsum{n}", [P, B]) for n in range(2)]
        rinv = [s.sb(f"rinv{n}", [P, B]) for n in range(2)]

        tables_loaded = s.sem("tables_loaded")
        rope_multiplied = s.sem("rope_multiplied")
        rope_done = s.sem("rope_done")
        read_out = s.sem("read_out")
        v_staged = s.sem("v_staged")
        scores_done = s.sem("scores_done")
        masked = s.sem("masked")
        max_done = s.sem("max_done")
        exp_done = s.sem("exp_done")
        rinv_done = s.sem("rinv_done")
        prob_done = s.sem("prob_done")
        prob_turned = s.sem("prob_turned")
        prob_copied = s.sem("prob_copied")
        pv_done = s.sem("pv_done")
        ctx_high = s.sem("ctx_high")
        ctx_low = s.sem("ctx_low")
        last_done = s.sem("last_done")
        block = ctx.enter_context(nc.Block())

        def before(i):
            return (4 * KD - O_TILES) // ROUND + (QT_TILES + O_TILES) // ROUND * i

        LAST = STEPS - 1
        CTX_LAST = (norm.XH[:, 0:REP, :], norm.XL[:, 0:REP, :])

        def context(i):
            return CTX_LAST if isinstance(i, int) and i == STEPS else (CH, CL)

        def output_banks(i, n):
            if isinstance(i, int) and i >= LAST:
                low = n > 0 if i == LAST else n % 2 == 0
            else:
                low = n % 2 == 1
            return banks[0:4] if low else banks[4:8]

        def outputs_read(i, n, b):
            return 2 * B + (i - 1) * 4 * B + n * B + b + 1

        def tile_end(r, t):
            return r * ROUND + t + 1

        bc = lambda ap: ap.unsqueeze(1).broadcast_to([ap.shape[0], B, P])

        @block.sync
        def _(sp):
            sp.dma_start(rt[:, :, :], rope).then_inc(tables_loaded, 16)
            sp.dma_start(mask[:, :], causal).then_inc(tables_loaded, 16)
            st.loads(sp)

        @block.gpsimd
        def _(pool):
            norm.pool(pool)

            def rope_add(h, dst):
                pool.wait_ge(rope_multiplied, h + 1)
                j = dst[1] % 2
                pool.tensor_tensor(dst[0], dst[0], turn[j][:, :], ALU.add).then_inc(rope_done, 1)

            for h in range(NKV):
                rope_add(h, (KT[:, h, :], h))
            with pool.Fori(0, STEPS) as i:
                for j in range(REP):
                    rope_add(NKV + i * REP + j, (QT[:, j, :], j))

        @block.vector
        def _(dve):
            def rope_mult(r, t, h, j, bank, dst):
                dve.wait_ge(st.used, tile_end(r, t))
                if not isinstance(h, int) or h >= 2:
                    dve.wait_ge(rope_done, h - 1)
                v = lambda ap: ap.rearrange("p (b t) -> p b t", b=B)
                dve.tensor_tensor(v(dst), v(bank[:, :]), bc(rt[:, 0, :]), ALU.mult)
                dve.tensor_tensor(v(turn[j % 2][0:HALF, :]), v(bank[HALF:P, :]), bc(rt[HALF:P, 1, :]), ALU.mult)
                dve.tensor_tensor(v(turn[j % 2][HALF:P, :]), v(bank[0:HALF, :]), bc(rt[0:HALF, 1, :]),
                                  ALU.mult).then_inc(rope_multiplied, 1)

            def read_values(r, t, n, b):
                dve.wait_ge(st.used, tile_end(r, t))
                dve.tensor_copy(V[:, b, n * NT:(n + 1) * NT], banks[b][:, :]).then_inc(read_out, 1)

            def mask_max(i, j):
                h = (i - 1) * REP + j
                dve.wait_ge(scores_done, h + 1)
                if j:
                    dve.wait_ge(exp_done, h)
                dve.scalar_tensor_tensor(out=S[:, :, :], in0=banks[4][:, :].rearrange("p (b k) -> p b k", b=B),
                                         scalar=SCALE, in1=bc(mask[:, :]), op0=ALU.mult, op1=ALU.add)\
                   .then_inc(masked, 1)
                dve.wait_ge(masked, h + 1)
                dve.tensor_reduce(nmax[j % 2][:, :], S[:, :, :], AXX, ALU.max, negate=True).then_inc(max_done, 1)

            def normalise(i, j):
                h = (i - 1) * REP + j
                dve.wait_ge(exp_done, h + 1)
                dve.reciprocal(rinv[j % 2][:, :], rsum[j % 2][:, :]).then_inc(rinv_done, 1)
                dve.wait_ge(rinv_done, h + 1)
                dve.tensor_tensor(E[:, :, :], E[:, :, :], rinv[j % 2][:, :].unsqueeze(2).broadcast_to([P, B, P]),
                                  ALU.mult).then_inc(prob_done, 1)

            def context_low(i, j):
                dve.wait_ge(ctx_high, (i - 1) * REP + j + 1)
                high, low = context(i)
                dve.tensor_tensor(low[:, j, :], banks[6][:, :], f32(high[:, j, :]), ALU.subtract).then_inc(ctx_low, 1)

            def add_output(r, i, o, n, b):
                if isinstance(i, int) and i == STEPS and n == 3:
                    dve.wait_ge(last_done, b + 1)
                else:
                    dve.wait_ge(st.used, tile_end(r, o + REP * n + REP - 1))
                out = R[:, b, n * NT:(n + 1) * NT]
                dve.tensor_tensor(out, output_banks(i, n)[b][:, :], out, ALU.add).then_inc(read_out, 1)

            def attention_at(i, k):
                for j, at in enumerate(SCORES_AT):
                    if k == at:
                        mask_max(i, j)
                    if k == at + 2:
                        normalise(i, j)
                    if k == at + 5:
                        context_low(i, j)

            def outputs(r, i, o):
                last = isinstance(i, int) and i == LAST
                for t in range(O_TILES):
                    n = t // REP - 1
                    if last and n >= 0 and t % REP == 0:
                        for b in range(B):
                            add_output(r, i, o, n, b)
                    st.at_vector(dve, r, o + t)
                    if o and t < REP:
                        rope_mult(r, o - 1, NKV + i * REP + t, t, banks[t], QT[:, t, :])
                    if not last and n >= 0 and t % REP < 2:
                        for b in (t % REP * 2, t % REP * 2 + 1):
                            add_output(r, i, o, n, b)
                    if last and t >= REP:
                        attention_at(STEPS, t - REP + 1)
                for b in range(B):
                    add_output(r, i, o, 3, b)
                if last:
                    for t in range(O_TILES, O_TILES + REP):
                        attention_at(STEPS, t - REP + 1)

            norm.vector(dve, banks[4:8], st)
            dve.wait_ge(tables_loaded, 32)
            for k in range(PART_SLOTS - LEAD, KD):
                st.at_vector(dve, 0, k)
            for k in range(KD):
                st.at_vector(dve, KD // ROUND, k)
                if k < B:
                    read_values(0, KD - 1, 0, k)
            for k in range(KD):
                st.at_vector(dve, 2 * KD // ROUND, k)
                if k < REP:
                    rope_mult(KD // ROUND, KD - 1, k, k, banks[4 + k], KT[:, k, :])
            for k in range(QT_TILES):
                st.at_vector(dve, 3 * KD // ROUND, k)
                if k < REP:
                    rope_mult(2 * KD // ROUND, KD - 1, REP + k, k, banks[k], KT[:, REP + k, :])
            for k in range(KD):
                st.at_vector(dve, 4 * KD // ROUND, k)
                if k < REP:
                    rope_mult(3 * KD // ROUND, QT_TILES - 1, NKV + k, k, banks[4 + k], QT[:, k, :])
            for b in range(B):
                read_values(4 * KD // ROUND, KD - 1, 1, b)

            def step(i):
                r = before(i)
                for k in range(QT_TILES):
                    st.at_vector(dve, r, k)
                    attention_at(i, k)
                outputs(r, i, QT_TILES)

            with dve.Fori(1, LAST) as i:
                step(i)
            step(LAST)
            outputs(before(STEPS), STEPS, 0)

        @block.scalar
        def _(act):
            def stage_values(i):
                act.activation(Vcur[:, :, :], V[:, :, bass.ds(i * P, P)], ACT.Copy).then_inc(v_staged, 1)

            def exponent(i, j):
                h = (i - 1) * REP + j
                act.wait_ge(max_done, h + 1)
                if j:
                    act.wait_ge(prob_turned, h)
                for b in range(B):
                    last = act.activation(E[:, b, :], S[:, b, :], ACT.Exp, bias=nmax[j % 2][:, b:b + 1],
                                          accum_out=rsum[j % 2][:, b:b + 1])
                last.then_inc(exp_done, 1)

            def copy_turned(i, j):
                h = (i - 1) * REP + j
                act.wait_ge(prob_turned, h + 1)
                if j:
                    act.wait_ge(pv_done, h)
                act.activation(PT[:, :], banks[5][:, :], ACT.Copy).then_inc(prob_copied, 1)

            def context_high(r, i, j):
                act.wait_ge(pv_done, (i - 1) * REP + j + 1)
                if not j:
                    act.wait_ge(st.used, r * ROUND)
                act.activation(context(i)[0][:, j, :], banks[6][:, :], ACT.Copy).then_inc(ctx_high, 1)

            def attention_at(r, i, k):
                for j, at in enumerate(SCORES_AT):
                    if k == at:
                        exponent(i, j)
                    if k == at + 3:
                        copy_turned(i, j)
                    if k == at + 4:
                        context_high(r, i, j)

            norm.scalar(act, banks[4:8], st)
            for k in range(PART_SLOTS - LEAD, 5 * KD):
                st.at_scalar(act, 0, k)
            act.wait_ge(read_out, 2 * B)
            stage_values(0)
            def step(i):
                r = before(i)
                for k in range(QT_TILES):
                    st.at_scalar(act, r, k)
                    attention_at(r, i, k)
                act.wait_ge(pv_done, i * REP)
                stage_values(i)
                for t in range(O_TILES):
                    st.at_scalar(act, r, QT_TILES + t)
                    if isinstance(i, int) and t >= REP:
                        attention_at(r + QT_TILES // ROUND, STEPS, t - REP + 1)

            with act.Fori(1, LAST) as i:
                step(i)
            step(LAST)
            for t in range(O_TILES, O_TILES + REP):
                attention_at(before(LAST) + QT_TILES // ROUND, STEPS, t - REP + 1)
            for t in range(O_TILES):
                st.at_scalar(act, before(STEPS), t)

        @block.tensor
        def _(pe):
            XH, XL = norm.XH, norm.XL

            def project_features(r, t0, use, free):
                for k in range(KD):
                    st.product_features(pe, r, t0 + k, XH[:, k, :], XL[:, k, :], use, k == 0, k == KD - 1,
                                        free if k == 0 else None)
                    yield k

            def project_tokens(r, t0, use, free):
                for k in range(KD):
                    st.product_tokens(pe, r, t0 + k, XH[:, k, :], XL[:, k, :], use, k == 0, k == KD - 1,
                                      free if k == 0 else None)

            def scores(i, j):
                h = (i - 1) * REP + j
                pe.wait_ge(rope_done, NKV + h + 1)
                if j:
                    pe.wait_ge(masked, h)
                for b in range(B):
                    c = slice(b * P, (b + 1) * P)
                    mm = pe.matmul(banks[4][:, c], QT[:, j, c], KT[:, bass.ds(i - 1, 1), c].rearrange("p a t -> p (a t)"),
                                   start=True, stop=True)
                mm.then_inc(scores_done, 1)

            def turn_probs(i, j):
                h = (i - 1) * REP + j
                pe.wait_ge(prob_done, h + 1)
                for b in range(B):
                    mm = pe.transpose(banks[5][:, b * P:(b + 1) * P], E[:, b, :], ident[:, :])
                mm.then_inc(prob_turned, 1)

            def values(i, j):
                h = (i - 1) * REP + j
                pe.wait_ge(prob_copied, h + 1)
                if j:
                    pe.wait_ge(ctx_low, h)
                else:
                    pe.wait_ge(v_staged, i)
                for b in range(B):
                    c = slice(b * P, (b + 1) * P)
                    mm = pe.matmul(banks[6][:, c], Vcur[:, b, :], PT[:, c], start=True, stop=True)
                mm.then_inc(pv_done, 1)

            def attention_at(i, k):
                for j, at in enumerate(SCORES_AT):
                    if k == at:
                        scores(i, j)
                    if k == at + 3:
                        turn_probs(i, j)
                    if k == at + 4:
                        values(i, j)

            def outputs(r, i, o):
                high, low = context(i)
                pe.wait_ge(ctx_low, i * REP)
                end = isinstance(i, int) and i == STEPS
                for t in range(O_TILES - (REP if end else 0)):
                    n, j = t // REP, t % REP

                    def free(b):
                        if end:
                            if n == 0:
                                pe.wait_ge(read_out, outputs_read(LAST, 3, b))
                            if n >= 2:
                                pe.wait_ge(read_out, outputs_read(i, n - 2, b))
                        elif n == 1:
                            pe.wait_ge(rope_multiplied, NKV + i * REP + b + 1)
                        elif n >= 2:
                            same = n - 1 if isinstance(i, int) else n - 2
                            pe.wait_ge(read_out, outputs_read(i, same, b))

                    st.product_tokens(pe, r, o + t, high[:, j, :], low[:, j, :], output_banks(i, n), j == 0, j == REP - 1,
                                      free if j == 0 else None)
                    if isinstance(i, int) and i == LAST and t >= REP:
                        if t == REP:
                            pe.wait_ge(read_out, outputs_read(i, 0, B - 1))
                        attention_at(STEPS, t - REP + 1)
                if end:
                    st.products_by_batch(pe, r, o + O_TILES - REP, high, low, output_banks(i, 3), True, True,
                                         ready=lambda b: pe.wait_ge(read_out, outputs_read(i, 1, b)), done=last_done)

            norm.tensor(pe, banks[4:8], st, banks[0:4])
            for k in range(PART_SLOTS, KD):
                st.product_tokens(pe, 0, k, XH[:, k, :], XL[:, k, :], banks[0:4], False, k == KD - 1)
            for _ in project_features(KD // ROUND, 0, banks[4:8], None):
                pass
            for _ in project_features(2 * KD // ROUND, 0, banks[0:4], lambda j: pe.wait_ge(read_out, j + 1)):
                pass
            for _ in project_features(3 * KD // ROUND, 0, banks[4:8], lambda j: pe.wait_ge(rope_multiplied, j + 1)):
                pass
            project_tokens(4 * KD // ROUND, 0, banks[0:4], lambda b: pe.wait_ge(rope_multiplied, REP + b + 1))

            def step(i):
                r = before(i)
                pe.wait_ge(rope_multiplied, NKV + i * REP)
                for k in project_features(r, 0, banks[0:4], lambda j: pe.wait_ge(read_out, outputs_read(i, -1, j))):
                    attention_at(i, k)
                outputs(r, i, QT_TILES)

            with pe.Fori(1, LAST) as i:
                step(i)
            step(LAST)
            for t in range(O_TILES, O_TILES + REP):
                attention_at(STEPS, t - REP + 1)
            outputs(before(STEPS), STEPS, 0)


FEAT = 512
C = 4
RH = 16
HS = FEAT // RH
AC = C - 1
PIECE = 4
SIDE_SKIP = RH
SIDE_A = 2 * RH
SIDE_B = SIDE_A + RH * AC


class Read:

    def __init__(self, s, outs, turned, W, Y, YH, YL, F, gamma, beta, ident):
        self.outs, self.turned_x, self.W, self.Y = outs, turned, W, Y
        self.w_loaded = s.sem("read_w_loaded")
        self.YH, self.YL, self.F, self.gamma, self.beta, self.ident = YH, YL, F, gamma, beta, ident
        self.stats = s.sb("y_stats", [P, B, outs, 6])
        self.mv = s.sb("y_mv", [P, B, outs, 2])
        self.veps = s.sb("y_veps", [P, B, outs])
        self.rstd = s.sb("y_rstd", [P, B, outs])
        self.nhalf = s.sb("y_nhalf", [P, 1])
        self.summed = s.sem("y_summed")
        self.y_read = s.sem("y_read")
        self.stats_done = s.sem("y_stats_done")
        self.var_done = s.sem("y_var_done")
        self.rstd_steps = s.sem("y_rstd_steps")
        self.scaled = s.sem("y_scaled")
        self.turned = s.sem("y_turned")
        self.affine_done = s.sem("y_affine_done")
        self.hi_done = s.sem("y_hi_done")
        self.lo_done = s.sem("y_lo_done")

    def load(self, eng, weights):
        eng.dma_start(self.W[:, :, :], weights).then_inc(self.w_loaded, 16)

    def sums(self, eng, banks, b):
        x, tok = self.turned_x, slice(b * P, (b + 1) * P)
        eng.wait_ge(self.w_loaded, 16)
        eng.wait_ge(x.hi_done, 2 * (b + 1))
        eng.wait_ge(x.lo_done, 2 * (b + 1))
        for t in range(KD // PIECE):
            if b:
                eng.wait_ge(self.y_read, 4 * (b - 1) + t + 1)
            for j in range(PIECE):
                w = slice(j * P, j * P + 32 * self.outs)
                mm = eng.matmul(banks[t][:, w], x.XT[:, PIECE * t + j, tok], self.W[:, t, w], start=True, stop=True)
            mm.then_inc(self.summed, 1)

    def read_sums(self, eng, banks, b):
        for t in range(KD // PIECE):
            eng.wait_ge(self.summed, 4 * b + t + 1)
            src = banks[t][:, :].rearrange("p (j o h) -> p j o h", j=PIECE, h=32)
            for o in range(self.outs):
                last = eng.activation(self.Y[:, b, o, t * P:(t + 1) * P].rearrange("p (j h) -> p j h", j=PIECE),
                                      src[:, :, o, :], ACT.Copy)
            last.then_inc(self.y_read, 1)


    def moments(self, eng, b):
        eng.wait_ge(self.y_read, 4 * (b + 1))
        for o in range(self.outs):
            last = eng.bn_stats(self.stats[:, b, o, :], self.Y[:, b, o, :])
        last.then_inc(self.stats_done, 1)
        eng.wait_ge(self.stats_done, b + 1)
        for o in range(self.outs):
            last = eng.bn_aggr(self.mv[:, b, o, :], self.stats[:, b, o, :])
        last.then_inc(self.var_done, 1)

    def scale(self, eng, b):
        eng.wait_ge(self.var_done, b + 1)
        eng.wait_ge(self.rstd_steps, 2 * b + 3)
        for o in range(self.outs):
            eng.tensor_scalar(self.Y[:, b, o, :], self.Y[:, b, o, :], self.mv[:, b, o, 0:1], self.rstd[:, b, o:o + 1],
                              ALU.subtract, ALU.mult).then_inc(self.scaled, 1)

    def pool(self, eng):
        eng.memset(self.nhalf[:, :], -0.5).then_inc(self.rstd_steps, 1)
        for b in range(B):
            eng.wait_ge(self.var_done, b + 1)
            eng.tensor_scalar(self.veps[:, b, :], self.mv[:, b, :, 1], EPS, None, ALU.add).then_inc(self.rstd_steps, 1)
            eng.wait_ge(self.rstd_steps, 2 * b + 2)
            eng.tensor_tensor(self.rstd[:, b, :], self.veps[:, b, :], self.nhalf[:, :].broadcast_to([P, self.outs]),
                              ALU.pow).then_inc(self.rstd_steps, 1)


    def turn(self, eng, banks, n):
        o, c = n // 4, n % 4
        eng.wait_ge(self.scaled, (B - 1) * self.outs + o + 1)
        if n >= len(banks):
            eng.wait_ge(self.affine_done, n + 1 - len(banks))
        for b in range(B):
            mm = eng.transpose(banks[n % len(banks)][:, b * P:(b + 1) * P], self.Y[:, b, o, c * P:(c + 1) * P],
                               self.ident[:, :])
        mm.then_inc(self.turned, 1)

    def affine(self, eng, banks, n, first=1):
        eng.wait_ge(self.turned, max(n + 1, first))
        if n >= 2:
            eng.wait_ge(self.lo_done, n - 1)
        eng.activation(self.F[n % 2][:, :], banks[n % len(banks)][:, :], ACT.Identity, bias=self.beta[:, n:n + 1],
                       scale=self.gamma[:, n:n + 1]).then_inc(self.affine_done, 1)
        eng.wait_ge(self.affine_done, n + 1)
        eng.activation(self.YH[:, n, :], self.F[n % 2][:, :], ACT.Copy).then_inc(self.hi_done, 1)

    def low_part(self, eng, n):
        eng.wait_ge(self.hi_done, n + 1)
        eng.tensor_tensor(self.YL[:, n, :], self.F[n % 2][:, :], f32(self.YH[:, n, :]), ALU.subtract)\
           .then_inc(self.lo_done, 1)


class Write:

    def __init__(self, s, H, R, G, side, sideT, ident, side_bias, DU):
        self.H, self.R, self.G = H, R, G
        self.log = [g[:, 0, :] for g in G]
        self.side, self.sideT = side, sideT
        self.ident, self.side_bias, self.DU = ident, side_bias, DU
        self.decay = s.sb("decay", [P, B, RH * AC])
        self.spl = s.sb("decay_log", [P, B, RH * AC])
        self.cn = s.sb("coef", [P, B, RH * AC])
        self.biased = s.sem("w_side_biased")
        self.side_turned = s.sem("w_side_turned")
        self.side_done = s.sem("w_side")
        self.pre_done = s.sem("w_pre")
        self.abs_done = s.sem("w_abs")
        self.exp_done = s.sem("w_exp")
        self.decay_log = s.sem("w_decay_log")
        self.delta_log = s.sem("w_delta_log")
        self.delta_done = s.sem("w_delta")
        self.coef_steps = s.sem("w_coef_steps")
        self.coef_done = s.sem("w_coef")
        self.arg_done = [s.sem(f"w_arg{b}") for b in range(B)]
        self.skip_done = [s.sem(f"w_skip{b}") for b in range(B)]
        self.a_done = s.sem("w_a")
        self.folded = s.sem("w_folded")
        self.factors_done = s.sem("w_factors")
        self.multiplied = s.sem("w_multiplied")
        if R is not None:
            self.old_added = [s.sem(f"w_old_added{b}") for b in range(B)]


    def turn_side(self, eng, dst, b):
        eng.wait_ge(self.biased, b + 1)
        eng.transpose(dst, self.sideT[:, b * P:(b + 1) * P], self.ident[:, :]).then_inc(self.side_turned, 1)

    def expand_delta(self, eng, dst, b):
        eng.wait_ge(self.biased, b + 1)
        eng.matmul(dst[:, :], self.sideT[0:9, b * P:(b + 1) * P], self.DU[0:9, :], start=True, stop=True)\
           .then_inc(self.pre_done, 1)


    def add_bias(self, eng, src, b):
        eng.activation(self.sideT[:, b * P:(b + 1) * P], src, ACT.Identity, bias=self.side_bias[:, 0:1])\
           .then_inc(self.biased, 1)


    def exponents(self, eng, pre, b):
        eng.wait_ge(self.side_done, b + 1)
        eng.activation(self.spl[:, b, :], self.side[:, b, SIDE_A:SIDE_B], ACT.Abs).then_inc(self.abs_done, 1)
        eng.wait_ge(self.pre_done, b + 1)
        eng.activation(self.log[b], pre[:, :], ACT.Abs).then_inc(self.abs_done, 1)
        eng.wait_ge(self.abs_done, 2 * b + 1)
        eng.activation(self.spl[:, b, :], self.spl[:, b, :], ACT.Exp, scale=-1.0).then_inc(self.exp_done, 1)
        eng.wait_ge(self.abs_done, 2 * b + 2)
        eng.activation(self.log[b], self.log[b], ACT.Exp, scale=-1.0).then_inc(self.exp_done, 1)

    def logs(self, eng, b):
        eng.wait_ge(self.exp_done, 2 * b + 1)
        eng.activation(self.spl[:, b, :], self.spl[:, b, :], ACT.Ln, bias=1.0).then_inc(self.decay_log, 1)
        eng.wait_ge(self.exp_done, 2 * b + 2)
        eng.activation(self.log[b], self.log[b], ACT.Ln, bias=1.0).then_inc(self.delta_log, 1)

    def decays(self, eng, b):
        eng.wait_ge(self.arg_done[b], 1)
        eng.activation(self.G[b][:, 0:AC, :], self.G[b][:, 0:AC, :], ACT.Exp, scale=-1.0).then_inc(self.a_done, 1)


    def per_group(self, x):
        return x.unsqueeze(1).broadcast_to([P, HS, RH])

    def of_channel(self, x, b, c):
        return self.per_group(x[:, b, :].rearrange("p (r c) -> p r c", c=AC)[:, :, c])

    def grouped(self, x):
        return x.rearrange("p (s r) -> p s r", r=RH)

    def arguments(self, eng, b):
        d = self.grouped(self.G[b][:, AC, :])
        eng.wait_ge(self.coef_done, b + 1)
        eng.wait_ge(self.delta_done, b + 1)
        for c in range(AC):
            last = eng.tensor_tensor(self.grouped(self.G[b][:, c, :]), d, self.of_channel(self.decay, b, c), ALU.mult)
        last.then_inc(self.arg_done[b], 1)
        eng.wait_ge(self.arg_done[b], 1)
        eng.tensor_tensor(d, d, self.per_group(self.side[:, b, SIDE_SKIP:SIDE_SKIP + RH]), ALU.mult)\
           .then_inc(self.skip_done[b], 1)


    def copy_turned(self, eng, src, b, turned):
        eng.wait_ge(self.side_turned, turned)
        eng.tensor_copy(self.side[:, b, :], src).then_inc(self.side_done, 1)

    def softplus(self, eng, pre, b):
        eng.wait_ge(self.side_done, b + 1)
        eng.wait_ge(self.decay_log, b + 1)
        eng.scalar_tensor_tensor(out=self.decay[:, b, :], in0=self.side[:, b, SIDE_A:SIDE_B], scalar=0.0,
                                 in1=self.spl[:, b, :], op0=ALU.max, op1=ALU.add).then_inc(self.coef_steps, 1)
        eng.wait_ge(self.delta_log, b + 1)
        eng.scalar_tensor_tensor(out=self.G[b][:, AC, :], in0=pre[:, :], scalar=0.0, in1=self.log[b],
                                 op0=ALU.max, op1=ALU.add).then_inc(self.delta_done, 1)
        eng.wait_ge(self.coef_steps, 3 * b + 1)
        eng.tensor_scalar(self.spl[:, b, :], self.decay[:, b, :], SSM_EPS, None, ALU.add).then_inc(self.coef_steps, 1)
        eng.wait_ge(self.coef_steps, 3 * b + 2)
        eng.reciprocal(self.cn[:, b, :], self.spl[:, b, :]).then_inc(self.coef_steps, 1)
        eng.wait_ge(self.coef_steps, 3 * b + 3)
        eng.scalar_tensor_tensor(out=self.cn[:, b, :], in0=self.cn[:, b, :], scalar=-1.0, in1=self.side[:, b, SIDE_B:P],
                                 op0=ALU.mult, op1=ALU.mult).then_inc(self.coef_done, 1)

    def channels(self, x, b):
        return x[:, b, :].rearrange("p (n c) -> p c n", c=C)

    def fold(self, eng, b):
        G = self.G[b]
        eng.wait_ge(self.a_done, b + 1)
        h = self.channels(self.H, b)[:, 0:AC, :]
        eng.tensor_tensor(h, h, G[:, 0:AC, :], ALU.mult).then_inc(self.folded, 1)
        eng.wait_ge(self.folded, b + 1)
        eng.wait_ge(self.coef_done, b + 1)
        for c in range(AC):
            last = eng.scalar_tensor_tensor(out=self.grouped(G[:, c, :]), in0=self.grouped(G[:, c, :]), scalar=-1.0,
                                            in1=self.of_channel(self.cn, b, c), op0=ALU.add, op1=ALU.mult)
        last.then_inc(self.factors_done, 1)

    def add_old(self, eng, b):
        eng.wait_ge(self.folded, b + 1)
        eng.tensor_tensor(self.R[:, b, :], self.R[:, b, :], self.H[:, b, :], ALU.add).then_inc(self.old_added[b], 1)

    def multiply(self, eng, out, b):
        G = self.G[b]
        eng.wait_ge(self.skip_done[b], 1)
        eng.wait_ge(self.factors_done, b + 1)
        eng.tensor_tensor(G[:, :, :], G[:, :, :], out.unsqueeze(1).broadcast_to([P, C, FEAT]), ALU.mult)\
           .then_inc(self.multiplied, 1)

    def add(self, eng, b):
        x = self.channels(self.H if self.R is None else self.R, b)
        eng.wait_ge(self.multiplied, b + 1)
        if self.R is not None:
            eng.wait_ge(self.old_added[b], 1)
        eng.tensor_tensor(x, x, self.G[b][:, :, :], ALU.add)


def xattn_attention(nc, R, H, ident, ident_d, x, read_w, wstream, gamma_d, beta_d, pos_d, inv_d, causal, side_w_d, side_bias_d, du_d):
    NH = 16
    HD = FEAT // NH
    HALF = HD // 2
    OUTS = 3
    TILES = OUTS * 4 + 4
    SCALE = 1.0 / float(np.sqrt(HD))
    PROJ = 0
    OUT = PROJ + OUTS * 4
    TWO_PI = 2.0 * np.pi
    C1 = 6.28125
    C2 = float(np.round((TWO_PI - C1) * 2.0 ** 17) / 2.0 ** 17)
    C3 = float(np.float32(TWO_PI - C1 - C2))
    MAGIC = 1.5 * 2.0 ** 23
    LIMIT = 3.1415925

    with ExitStack() as ctx:
        s = Scope(nc, ctx, "a_")
        banks = s.banks()
        norm = CopiedNorm(s, R, ident, [H[:, b, :] for b in range(B)])
        st = Stream(s, TILES, wstream)
        YH = norm.XH[:, 0:12, :]
        YL = norm.XL[:, 0:12, :]
        QT = s.over("XH", 12, "QT", [P, 4, TOK])
        KT = s.over("XL", 12, "KT", [P, 4, TOK])
        PT = s.over("XH", 0, "PT", [P, NH, P])
        OH = norm.XH[:, 4:8, :]
        OL = norm.XL[:, 4:8, :]
        Y = s.sb("Y", [P, B, OUTS, FEAT])
        q_tok = Y[:, :, 0, :]
        k_tok = Y[:, :, 1, :]
        V = Y[:, :, 2, :]
        S = s.sb("S", [P, NH, P])
        F = [s.sb(f"F{n}", [P, TOK]) for n in range(2)]
        gamma = s.sb("gamma", [P, 4 * OUTS])
        beta = s.sb("beta", [P, 4 * OUTS])
        read = Read(s, OUTS, norm, s.over("XL", 12, "read_w", [P, KD // PIECE, NT]), Y, YH, YL, F, gamma, beta, ident)
        posi = s.sb("pos", [P, B], I32)
        posf = s.sb("posf", [P, B])
        inv = s.sb("inv", [P, HALF])
        ang = s.sb("ang", [P, B, HALF])
        kk = s.sb("kk", [P, B, HALF])
        sc = s.sb("sincos", [P, 3, B, HALF])
        mask = s.sb("mask", [P, P])
        nmax = s.sb("nmax", [P, NH])
        rsum = s.sb("rsum", [P, NH])
        rinv = s.sb("rinv", [P, NH])
        side_bias = s.sb("side_bias", [P, 1])
        DU = s.sb("DU", [9, FEAT])
        side_w = s.sb("side_w", [P, NT])
        OT = F[0]
        ident_loaded = s.sem("ident_loaded")
        side_product_done = s.sem("side_product_done")
        out_done = s.sem("out_done")
        out_copied = s.sem("out_copied")
        write = Write(s, H, None, [s.over(x, row, f"G{n}", [P, C, FEAT]) for n, (x, row) in
                                   enumerate((("XH", 8), ("XL", 0), ("XL", 8), ("XH", 0)))],
                      q_tok[:, 1, :].rearrange("p (b n) -> p b n", b=B), k_tok[:, 1, :], ident, side_bias, DU)
        out_tok = [q_tok[:, 0, :], k_tok[:, 0, :]]

        x_loaded = [s.sem(f"x_loaded{b}") for b in range(B)]
        small_loaded = s.sem("small_loaded")
        table_steps = s.sem("table_steps")
        sin_done = s.sem("sin_done")
        rope_mult = s.sem("rope_mult")
        rope_done = s.sem("rope_done")
        v_read = s.sem("v_read")
        qk_turned = s.sem("qk_turned")
        qk_copied = s.sem("qk_copied")
        scores_done = s.sem("scores_done")
        masked = s.sem("masked")
        max_done = s.sem("max_done")
        exp_done = s.sem("exp_done")
        prob_turned = s.sem("prob_turned")
        prob_copied = s.sem("prob_copied")
        pv_done = s.sem("pv_done")
        rinv_done = s.sem("rinv_done")
        normalised = s.sem("normalised")
        o_copied = s.sem("o_copied")
        o_high = s.sem("o_high")
        o_low = s.sem("o_low")
        block = ctx.enter_context(nc.Block())
        pieces4 = lambda ap: ap.rearrange("p (c t) -> p c t", c=4)

        @block.sync
        def _(sp):
            sp.dma_start(R[:, 0, :], x[0, :, :]).then_inc(x_loaded[0], 16)
            sp.dma_start(ident[:, :], ident_d).then_inc(ident_loaded, 16)
            sp.dma_start(R[:, 1, :], x[1, :, :]).then_inc(x_loaded[1], 16)
            for dst, src in ((gamma[:, :], gamma_d), (beta[:, :], beta_d), (posi[:, :], pos_d), (inv[:, :], inv_d),
                             (mask[:, :], causal), (side_w[:, :], side_w_d), (side_bias[:, :], side_bias_d), (DU[:, :], du_d)):
                sp.dma_start(dst, src).then_inc(small_loaded, 16)
            read.load(sp, read_w)
            st.loads(sp)

        SMALL = 8 * 16

        @block.gpsimd
        def _(pool):
            norm.pool(pool)
            read.pool(pool)
            for n in range(2 * B):
                dst = (q_tok, k_tok)[n // B][:, n % B, :]
                pool.wait_ge(rope_mult, n + 1)
                pool.tensor_tensor(dst, dst, F[n % 2][:, :], ALU.add).then_inc(rope_done, 1)
            for b in range(B - 1):
                write.arguments(pool, b)
                if b:
                    write.add(pool, b - 1)
            write.add(pool, B - 2)

        @block.vector
        def _(dve):
            def moments(b):
                dve.wait_ge(x_loaded[b], 16)
                norm.moments(dve, b)

            moments(0)
            moments(1)
            norm.scale(dve, 0)
            norm.copy(dve, banks[0:4], 0, 1)
            moments(2)
            norm.scale(dve, 1)
            norm.copy(dve, banks[0:4], 1, 1)
            moments(3)
            norm.scale(dve, 2)
            norm.scale(dve, 3)
            norm.copy(dve, banks[0:4], 2, 1)
            read.moments(dve, 0)
            norm.copy(dve, banks[0:4], 3, 1)
            read.scale(dve, 0)

            read.moments(dve, 1)
            read.moments(dve, 2)
            read.scale(dve, 1)
            read.moments(dve, 3)
            read.scale(dve, 2)
            read.scale(dve, 3)
            st.begin_vector(dve)
            for n in range(4 * OUTS):
                read.low_part(dve, n)
                if n == 3 or n == 7:
                    st.at_vector(dve, 0, PROJ + n // 4 * 2)
                    st.at_vector(dve, 0, PROJ + n // 4 * 2 + 1)

            link = Chain(dve, table_steps)
            dve.wait_ge(small_loaded, SMALL)
            link(dve.tensor_copy(posf[:, :], posi[:, :]))
            link(dve.tensor_tensor(ang[:, :, :], posf[:, :].unsqueeze(2).broadcast_to([P, B, HALF]),
                                   inv[:, :].unsqueeze(1).broadcast_to([P, B, HALF]), ALU.mult))
            link(dve.tensor_scalar(kk[:, :, :], ang[:, :, :], 1.0 / TWO_PI, MAGIC, ALU.mult, ALU.add))
            link(dve.tensor_scalar(kk[:, :, :], kk[:, :, :], MAGIC, None, ALU.subtract))
            for part in (C1, C2, C3):
                link(dve.scalar_tensor_tensor(out=ang[:, :, :], in0=kk[:, :, :], scalar=-part, in1=ang[:, :, :],
                                              op0=ALU.mult, op1=ALU.add))
            link(dve.tensor_scalar(sc[:, 1, :, :], ang[:, :, :], np.pi / 2, None, ALU.add))
            link(dve.tensor_scalar(kk[:, :, :], sc[:, 1, :, :], LIMIT, -TWO_PI, ALU.is_gt, ALU.mult))
            link(dve.tensor_tensor(sc[:, 1, :, :], sc[:, 1, :, :], kk[:, :, :], ALU.add))
            link(dve.tensor_copy(sc[:, 0, :, :], ang[:, :, :]))
            link(dve.tensor_scalar(sc[:, 0:2, :, :], sc[:, 0:2, :, :], LIMIT, -LIMIT, ALU.min, ALU.max))
            dve.wait_ge(sin_done, 1)
            link(dve.tensor_scalar(sc[:, 2, :, :], sc[:, 0, :, :], -1.0, None, ALU.mult))

            heads = lambda ap: ap.rearrange("p (h d) -> p h d", d=HALF)
            halves = lambda ap: ap.rearrange("p (h two d) -> p h two d", two=2, d=HALF)

            def rope(n):
                which, b = n // B, n % B
                bank, dst, turn = banks[4 * which + b], (q_tok, k_tok)[which][:, b, :], F[n % 2][:, :]
                dve.wait_ge(st.used, PROJ + 4 * (which + 1))
                if n < 2:
                    dve.wait_ge(read.lo_done, 11 + n)
                if n >= 2:
                    dve.wait_ge(rope_done, n - 1)
                dve.tensor_tensor(heads(dst), heads(bank[:, :]),
                                  sc[:, 1, b, :].unsqueeze(1).broadcast_to([P, 2 * NH, HALF]), ALU.mult)
                dve.tensor_tensor(halves(turn)[:, :, 0, :], halves(bank[:, :])[:, :, 1, :],
                                  sc[:, 2, b, :].unsqueeze(1).broadcast_to([P, NH, HALF]), ALU.mult)
                dve.tensor_tensor(halves(turn)[:, :, 1, :], halves(bank[:, :])[:, :, 0, :],
                                  sc[:, 0, b, :].unsqueeze(1).broadcast_to([P, NH, HALF]), ALU.mult)\
                   .then_inc(rope_mult, 1)

            for n in range(2 * B):
                st.at_vector(dve, 0, PROJ + 4 + n)
                rope(n)
            for t in range(PROJ + 12, OUT + 2):
                st.at_vector(dve, 0, t)

            def masked_scores(b, r):
                n = 4 * b + r + 1
                dve.wait_ge(scores_done, n)
                if b:
                    dve.wait_ge(prob_turned, n - 4)
                dve.scalar_tensor_tensor(
                    out=S[:, 4 * r:4 * r + 4, :], in0=banks[r][:, :].rearrange("p (c k) -> p c k", c=4),
                    scalar=SCALE, in1=mask[:, :].unsqueeze(1).broadcast_to([P, 4, P]), op0=ALU.mult, op1=ALU.add)\
                   .then_inc(masked, 1)
                dve.wait_ge(masked, n)
                dve.tensor_reduce(nmax[:, 4 * r:4 * r + 4], S[:, 4 * r:4 * r + 4, :], AXX, ALU.max, negate=True)\
                   .then_inc(max_done, 1)

            def normalise(b, r):
                n = 4 * b + r + 1
                heads = slice(4 * r, 4 * r + 4)
                dve.wait_ge(exp_done, n)
                dve.reciprocal(rinv[:, heads], rsum[:, heads]).then_inc(rinv_done, 1)
                dve.wait_ge(rinv_done, n)
                dve.tensor_tensor(S[:, heads, :], S[:, heads, :], rinv[:, heads].unsqueeze(2).broadcast_to([P, 4, P]),
                                  ALU.mult).then_inc(normalised, 1)

            for r in range(4):
                masked_scores(0, r)
            for r in range(4):
                normalise(0, r)
            for b in range(B):
                more = b + 1 < B
                if more:
                    for r in range(4):
                        masked_scores(b + 1, r)
                    normalise(b + 1, 0)
                    normalise(b + 1, 1)
                dve.wait_ge(o_high, b + 1)
                tok = slice(b * P, (b + 1) * P)
                dve.tensor_tensor(OL[:, :, tok], pieces4(banks[4][:, :]), f32(OH[:, :, tok]), ALU.subtract).then_inc(o_low, 1)
                if more:
                    normalise(b + 1, 2)
                write.copy_turned(dve, banks[6][:, P:2 * P], b, b + 1)
                if more:
                    normalise(b + 1, 3)
                if b:
                    write.fold(dve, b - 1)
                write.softplus(dve, banks[7], b)
                if not more:
                    write.arguments(dve, b)
                if b:
                    dve.wait_ge(out_copied, b)
                    write.multiply(dve, out_tok[(b - 1) % 2], b - 1)
            write.fold(dve, B - 1)
            dve.wait_ge(out_copied, B)
            write.multiply(dve, out_tok[(B - 1) % 2], B - 1)
            write.add(dve, B - 1)

        @block.scalar
        def _(act):
            act.wait_ge(x_loaded[0], 16)
            for b in range(2, B):
                act.dma_start(R[:, b, :], x[b, :, :]).then_inc(x_loaded[b], 16)
            norm.copy(act, banks[0:4], 0, 0)
            norm.copy(act, banks[0:4], 1, 0)
            for b in range(B):
                read.read_sums(act, banks[4:8], b)
                if b + 2 < B:
                    norm.copy(act, banks[0:4], b + 2, 0)
            st.begin_scalar(act)
            act.wait_ge(small_loaded, SMALL)
            for n in range(4 * OUTS):
                read.affine(act, banks[4:8], n)
                if n == 3 or n == 7:
                    st.at_scalar(act, 0, PROJ + n // 4 * 2)
                    st.at_scalar(act, 0, PROJ + n // 4 * 2 + 1)
            act.wait_ge(table_steps, 12)
            act.activation(sc[:, 0:2, :, :], sc[:, 0:2, :, :], ACT.Sin).then_inc(sin_done, 1)
            for t in range(PROJ + 4, OUT + 2):
                st.at_scalar(act, 0, t)
            for b in range(B):
                act.activation(V[:, b, :], banks[b][:, :], ACT.Copy).then_inc(v_read, 1)
            for n in range(2 * B):
                act.wait_ge(qk_turned, n + 1)
                act.activation((QT, KT)[n % 2][:, :, n // 2 * P:(n // 2 + 1) * P], pieces4(banks[4 + n % 4][:, :]), ACT.Copy)\
                   .then_inc(qk_copied, 1)

            def exponents(b, r):
                n = 4 * b + r + 1
                act.wait_ge(max_done, n)
                if b and r == 0:
                    act.wait_ge(rinv_done, 4 * b)
                for h in range(4 * r, 4 * r + 4):
                    last = act.activation(S[:, h, :], S[:, h, :], ACT.Exp, bias=nmax[:, h:h + 1],
                                          accum_out=rsum[:, h:h + 1])
                last.then_inc(exp_done, 1)

            for r in range(4):
                exponents(0, r)
            for b in range(B):
                for r in range(4):
                    act.wait_ge(prob_turned, 4 * b + r + 1)
                    if b:
                        act.wait_ge(pv_done, b)
                    act.activation(PT[:, 4 * r:4 * r + 4, :], banks[4 + r][:, :].rearrange("p (c q) -> p c q", c=4),
                                   ACT.Copy).then_inc(prob_copied, 1)
                if b + 1 < B:
                    exponents(b + 1, 0)
                    exponents(b + 1, 1)
                act.wait_ge(pv_done, b + 1)
                act.activation(OT[:, :], banks[4][:, :], ACT.Copy).then_inc(o_copied, 1)
                act.activation(OH[:, :, b * P:(b + 1) * P], pieces4(banks[4][:, :]), ACT.Copy).then_inc(o_high, 1)
                if b + 1 < B:
                    exponents(b + 1, 2)
                act.wait_ge(side_product_done, b + 1)
                write.add_bias(act, banks[6][:, 0:P], b)
                if b + 1 < B:
                    exponents(b + 1, 3)
                if b:
                    write.decays(act, b - 1)
                write.exponents(act, banks[7], b)
                write.logs(act, b)
                act.wait_ge(out_done, b + 1)
                if b >= 2:
                    act.wait_ge(write.multiplied, b - 1)
                act.activation(out_tok[b % 2], banks[5][:, :], ACT.Copy).then_inc(out_copied, 1)
            write.decays(act, B - 1)

        @block.tensor
        def _(pe):
            def turn(b):
                pe.wait_ge(norm.scaled, b + 1)
                norm.turn(pe, banks[0:4], b)

            pe.wait_ge(ident_loaded, 16)
            turn(0)
            turn(1)
            for b in range(B):
                read.sums(pe, banks[4:8], b)
                if b + 2 < B:
                    turn(b + 2)

            def project(o, use, free):
                for k in range(4):
                    pe.wait_ge(read.lo_done, 4 * o + k + 1)
                    st.product_tokens(pe, 0, PROJ + 4 * o + k, YH[:, 4 * o + k, :], YL[:, 4 * o + k, :], use, k == 0, k == 3,
                                      free if k == 0 else None)

            for n in range(8):
                read.turn(pe, banks[4:8], n)
            project(0, banks[0:4], None)
            for n in range(8, 12):
                read.turn(pe, banks[4:8], n)
            project(1, banks[4:8], lambda b: pe.wait_ge(read.affine_done, 9 + b))
            project(2, banks[0:4], lambda b: pe.wait_ge(rope_mult, b + 1))
            for n in range(2 * B):
                which, b = n % 2, n // 2
                pe.wait_ge(rope_done, which * B + b + 1)
                if n < 4:
                    pe.wait_ge(rope_mult, B + n + 1)
                else:
                    pe.wait_ge(qk_copied, n - 3)
                for c in range(4):
                    mm = pe.transpose(banks[4 + n % 4][:, c * P:(c + 1) * P], (q_tok, k_tok)[which][:, b, c * P:(c + 1) * P],
                                      ident[:, :])
                mm.then_inc(qk_turned, 1)

            def scores(b):
                pe.wait_ge(qk_copied, 2 * b + 2)
                t = slice(b * P, (b + 1) * P)
                for r in range(4):
                    if b:
                        pe.wait_ge(masked, 4 * (b - 1) + r + 1)
                    f = slice(HD * r, HD * (r + 1))
                    for c in range(4):
                        mm = pe.matmul(banks[r][:, c * P:(c + 1) * P], QT[f, c, t], KT[f, c, t], start=True, stop=True)
                    mm.then_inc(scores_done, 1)

            pe.wait_ge(v_read, B)
            scores(0)
            pe.wait_ge(qk_copied, 2 * B)
            for b in range(B):
                for r in range(4):
                    pe.wait_ge(normalised, 4 * b + r + 1)
                    if b:
                        pe.wait_ge((o_low, out_copied, write.side_done, write.delta_done)[r], b)
                    for c in range(4):
                        mm = pe.transpose(banks[4 + r][:, c * P:(c + 1) * P], S[:, 4 * r + c, :], ident[:, :])
                    mm.then_inc(prob_turned, 1)
                if b + 1 < B:
                    scores(b + 1)
                pe.wait_ge(prob_copied, 4 * (b + 1))
                for c in range(4):
                    for r in range(4):
                        f = slice(HD * (4 * c + r), HD * (4 * c + r + 1))
                        mm = pe.matmul(banks[4][HD * r:HD * (r + 1), c * P:(c + 1) * P], V[:, b, f], PT[:, 4 * r + c, :],
                                       start=True, stop=True)
                mm.then_inc(pv_done, 1)
                pe.wait_ge(o_copied, b + 1)
                for k in range(4):
                    w = slice(k * P, (k + 1) * P)
                    mm = pe.matmul(banks[6][:, 0:P], side_w[:, w], OT[:, w], start=k == 0, stop=k == 3)
                mm.then_inc(side_product_done, 1)
                pe.wait_ge(o_low, b + 1)
                tok = slice(b * P, (b + 1) * P)

                def project_out(k):
                    pe.wait_ge(st.lo_done, OUT + k + 1)
                    wh, wl = st.WH[(OUT + k) % PART_SLOTS][:, :], st.WL[(OUT + k) % PART_SLOTS][:, :]
                    pe.matmul(banks[5][:, :], OH[:, k, tok], wh, start=k == 0, stop=False)
                    pe.matmul(banks[5][:, :], OH[:, k, tok], wl, start=False, stop=False)
                    return pe.matmul(banks[5][:, :], OL[:, k, tok], wh, start=False, stop=k == 3)

                project_out(0)
                project_out(1)
                write.turn_side(pe, banks[6][:, P:2 * P], b)
                write.expand_delta(pe, banks[7], b)
                project_out(2)
                project_out(3).then_inc(out_done, 1)


def xattn_mlp(nc, R, H, ident, read_w, wstream, gamma_d, beta_d, side_bias_d, du_d):
    OUTS = 2
    M = 2048
    MB = M // NT
    GATE = 0
    WOD = GATE + 8 * MB
    TILES = WOD + M // P + M // P // 4

    with ExitStack() as ctx:
        s = Scope(nc, ctx, "m_")
        banks = s.banks()
        turned = Copied(s, [H[:, b, :] for b in range(B)], ident)
        XH, XL = turned.XH, turned.XL
        gate = turned.XT
        st = Stream(s, TILES, wstream)
        YH = s.sb("YH", [P, 4 * OUTS, TOK], F32R)
        YL = s.sb("YL", [P, 4 * OUTS, TOK], F32R)
        Y = s.over("YH", 0, "Y", [P, B, OUTS, FEAT])
        F = [s.sb(f"F{n}", [P, TOK]) for n in range(2)]
        gamma = s.sb("gamma", [P, 4 * OUTS])
        beta = s.sb("beta", [P, 4 * OUTS])
        read = Read(s, OUTS, turned, s.over("XL", 12, "read_w", [P, KD // PIECE, NT]), Y, YH, YL, F, gamma, beta, ident)
        side_bias = s.sb("side_bias", [P, 1])
        DU = s.sb("DU", [9, FEAT])
        write = Write(s, H, R, [s.over(x, row, f"G{n}", [P, C, FEAT]) for n, (x, row) in
                                enumerate((("YH", 0), ("YH", 4), ("YL", 0), ("YL", 4)))],
                      F[1][:, :].rearrange("p (b n) -> p b n", b=B), F[0], ident, side_bias, DU)
        small_loaded = s.sem("small_loaded")
        silu_done = s.sem("silu_done")
        unit_done = s.sem("unit_done")
        unit_high = s.sem("unit_high")
        unit_low = s.sem("unit_low")
        out_done = s.sem("out_done")
        block = ctx.enter_context(nc.Block())
        POOL_ADDS = 2
        OUT = WOD + M // P // 4
        PRE = (banks[2], banks[3], banks[0], banks[1])

        @block.sync
        def _(sp):
            for dst, src in ((gamma[:, :], gamma_d), (beta[:, :], beta_d),
                             (side_bias[:, :], side_bias_d), (DU[:, :], du_d)):
                sp.dma_start(dst, src).then_inc(small_loaded, 16)
            read.load(sp, read_w)
            st.loads(sp)

        @block.gpsimd
        def _(pool):
            read.pool(pool)
            for b in range(B):
                write.arguments(pool, b)
            for b in range(B - POOL_ADDS, B):
                write.add_old(pool, b)
            for b in range(POOL_ADDS):
                write.add(pool, b)

        def piece(x, m, c):
            return x[:, bass.ds(4 * m + c, 1), :].rearrange("p a n -> p (a n)")

        @block.vector
        def _(dve):
            turned.copy(dve, banks[0:4], 0, 1)
            turned.copy(dve, banks[0:4], 1, 1)
            for b in range(2, B):
                turned.copy(dve, banks[0:4], b, 1)
                read.moments(dve, b - 2)
                read.scale(dve, b - 2)
            for b in range(B - 2, B):
                read.moments(dve, b)
                read.scale(dve, b)
            st.begin_vector(dve)
            for n in range(4 * OUTS):
                read.low_part(dve, n)

            def unit(m, c):
                if c == 0:
                    dve.wait_ge(st.used, m * ROUND + GATE + 8)
                dve.wait_ge(silu_done, 4 * m + c + 1)
                if c >= 2:
                    dve.wait_ge(unit_low, 4 * m + c - 1)
                dve.tensor_tensor(F[c % 2][:, :], banks[4 + c][:, :], piece(gate, m, c), ALU.mult).then_inc(unit_done, 1)

            def low_of_unit(m, c):
                dve.wait_ge(unit_high, 4 * m + c + 1)
                dve.tensor_tensor(piece(XL, m, c), F[c % 2][:, :], f32(piece(XH, m, c)), ALU.subtract).then_inc(unit_low, 1)

            def units_at(m, t):
                if t < 4:
                    unit(m, t)
                if 1 <= t < 5:
                    low_of_unit(m, t - 1)
                if t == 4:
                    dve.wait_ge(unit_low, 4 * m + 4)

            for t in range(8):
                st.at_vector(dve, 0, GATE + t)
            with dve.Fori(1, MB) as m:
                for t in range(8):
                    st.at_vector(dve, m, GATE + t)
                    units_at(m - 1, t)
            for t in range(5):
                units_at(MB - 1, t)
                st.at_vector(dve, 0, WOD + t)
            for n, t in enumerate(range(OUT + 1, TILES)):
                st.at_vector(dve, 0, t)
                if n == 0:
                    for b in range(B):
                        write.copy_turned(dve, banks[1][:, b * P:(b + 1) * P], b, B)
                if n in (3, 4):
                    for b in (2 * n - 6, 2 * n - 5):
                        write.softplus(dve, PRE[b], b)
                if n in (6, 8, 10, 12):
                    b = (n - 6) // 2
                    write.fold(dve, b)
                    if b < B - POOL_ADDS:
                        write.add_old(dve, b)
            for b in range(B):
                dve.wait_ge(out_done, b + 1)
                write.multiply(dve, banks[4 + b][:, :], b)
                if b >= POOL_ADDS:
                    write.add(dve, b)

        @block.scalar
        def _(act):
            turned.copy(act, banks[0:4], 0, 0)
            turned.copy(act, banks[0:4], 1, 0)
            for b in range(B):
                read.read_sums(act, banks[4:8], b)
                if b + 2 < B:
                    turned.copy(act, banks[0:4], b + 2, 0)
            act.wait_ge(small_loaded, 64)
            st.begin_scalar(act)
            for n in range(4 * OUTS):
                read.affine(act, banks, n, first=4 * OUTS)

            def silu(m, c):
                if c == 0:
                    act.wait_ge(st.used, m * ROUND + GATE + 4)
                act.activation(piece(gate, m, c), banks[c][:, :], ACT.Silu).then_inc(silu_done, 1)

            def high_of_unit(m, c):
                act.wait_ge(unit_done, 4 * m + c + 1)
                act.activation(piece(XH, m, c), F[c % 2][:, :], ACT.Copy).then_inc(unit_high, 1)

            def block_of(m, first):
                for t in range(8):
                    st.at_scalar(act, m, GATE + t)
                    if t < 4 and not first:
                        high_of_unit(m - 1, t)
                    if t >= 4:
                        silu(m, t - 4)

            block_of(0, True)
            with act.Fori(1, MB) as m:
                block_of(m, False)
            for t in range(4):
                st.at_scalar(act, 0, WOD + t)
                high_of_unit(MB - 1, t)
            for n, t in enumerate(range(OUT, TILES)):
                st.at_scalar(act, 0, t)
                if n == 0:
                    act.wait_ge(st.used, OUT)
                    for b in range(B):
                        write.add_bias(act, banks[0][:, b * P:(b + 1) * P], b)
                if n in (1, 2):
                    for b in (2 * n - 2, 2 * n - 1):
                        write.exponents(act, PRE[b], b)
                if n == 3:
                    for b in range(B):
                        write.logs(act, b)
                if 7 <= n < 7 + B:
                    write.decays(act, n - 7)

        @block.tensor
        def _(pe):
            turned.turn(pe, banks[0:4], 0)
            turned.turn(pe, banks[0:4], 1)
            for b in range(B):
                read.sums(pe, banks[4:8], b)
                if b + 2 < B:
                    turned.turn(pe, banks[0:4], b + 2)
            for n in range(4 * OUTS):
                if n >= 4 and n < 8:
                    pe.wait_ge(read.y_read, 4 * (B - 1) + n - 3)
                read.turn(pe, banks, n)

            def block_of(m, first):
                for o in range(2):
                    def free(c):
                        if first:
                            pe.wait_ge(read.affine_done, 4 * o + c + 1)
                        else:
                            pe.wait_ge((silu_done, unit_done)[o], 4 * m - 4 + c + 1)
                    for k in range(4):
                        if first:
                            pe.wait_ge(read.lo_done, 4 * o + k + 1)
                        st.product_features(pe, m, GATE + 4 * o + k, YH[:, 4 * o + k, :], YL[:, 4 * o + k, :],
                                            banks[4 * o:4 * o + 4], k == 0, k == 3, free if k == 0 else None)

            block_of(0, True)
            with pe.Fori(1, MB) as m:
                block_of(m, False)

            pe.wait_ge(silu_done, 4 * MB)
            for t in range(M // P // 4):
                pe.wait_ge(st.lo_done, WOD + t + 1)
                pe.wait_ge(unit_low, 4 * t + 4)
                wh, wl = st.WH[(WOD + t) % PART_SLOTS], st.WL[(WOD + t) % PART_SLOTS]
                for k in range(4 * t, 4 * t + 4):
                    w = slice(k % 4 * P, (k % 4 + 1) * P)
                    pe.matmul(banks[0][:, :], wh[:, w], XH[:, k, :], start=k == 0, stop=False)
                    pe.matmul(banks[0][:, :], wh[:, w], XL[:, k, :], start=False, stop=False)
                    mm = pe.matmul(banks[0][:, :], wl[:, w], XH[:, k, :], start=False, stop=k == M // P - 1)
                mm.then_inc(st.used, 1)
            for k in range(M // P - PART_SLOTS):
                st.product_tokens(pe, 0, OUT + k, XH[:, k, :], XL[:, k, :], banks[4:8], k == 0, False)
                if k == 0:
                    for b in range(B):
                        write.turn_side(pe, banks[1][:, b * P:(b + 1) * P], b)
                        if b < 2:
                            write.expand_delta(pe, PRE[b], b)
                if k == 1:
                    pe.wait_ge(write.side_done, B)
                    for b in (2, 3):
                        write.expand_delta(pe, PRE[b], b)
            k = M // P - PART_SLOTS
            st.products_by_batch(pe, 0, OUT + k, XH[:, k:, :], XL[:, k:, :], banks[4:8], False, True, done=out_done)


def routed_ffn(nc, R, ident, wstream, router, iota, bias, out):
    EXPERTS = 16
    RANK = 64
    SCALING = 0.5
    AR = RANK + EXPERTS
    KE = EXPERTS * RANK // P
    NB = D // NT
    PER = KD + KE
    TILES = NB * PER
    BIG = 1024.0

    with ExitStack() as ctx:
        s = Scope(nc, ctx, "f_")
        banks = s.banks()
        EH = s.sb("EH", [P, KE, TOK], F32R)
        EL = s.sb("EL", [P, KE, TOK], F32R)
        xn = [s.sb(f"xn{n}", [P, D]) for n in range(2)]
        ET = [xn[n][:, 0:EXPERTS * RANK] for n in range(2)]
        norm = Norm(s, R, ident, [x[:, :] for x in xn])
        st = Stream(s, TILES, wstream)
        A = s.sb("A", [P, KD, AR])
        AH = s.sb("AH", [P, KD, AR], F32R)
        AL = s.sb("AL", [P, KD, AR], F32R)
        bias_all = s.sb("bias", [P, D])
        io = s.sb("iota", [P, EXPERTS])
        sideT = s.sb("sideT", [AR, TOK])
        res = s.sb("res", [P, B, AR])
        pr = s.sb("probs", [P, B, EXPERTS])
        one = [s.sb(f"one{n}", [P, B, EXPERTS]) for n in range(2)]
        key = s.sb("key", [P, B, EXPERTS])
        wt = s.sb("weights", [P, B, EXPERTS])
        small = s.sb("small", [P, 8, B])

        small_loaded = s.sem("small_loaded")
        a_high = s.sem("a_high")
        a_low = s.sem("a_low")
        bias_added = s.sem("bias_added")
        side_done = s.sem("side_done")
        side_copied = s.sem("side_copied")
        res_done = s.sem("res_done")
        steps = s.sem("routing_steps")
        shifted = s.sem("logits_shifted")
        exp_done = s.sem("exp_done")
        rows_done = s.sem("rows_done")
        rows_turned = s.sem("rows_turned")
        rows_high = s.sem("rows_high")
        rows_low = s.sem("rows_low")
        out_added = s.sem("out_added")
        out_stored = s.sem("out_stored")
        last_done = s.sem("last_done")
        block = ctx.enter_context(nc.Block())

        SIDE_AT = PART_SLOTS
        ROWS_AT = SIDE_AT + 4
        ROUNDS = PER // ROUND
        bce = lambda ap: ap.unsqueeze(2).broadcast_to([P, B, EXPERTS])

        @block.sync
        def _(sp):
            sp.dma_start(A[:, :, :], router).then_inc(small_loaded, 16)
            sp.dma_start(io[:, :], iota).then_inc(small_loaded, 16)
            sp.dma_start(bias_all[:, :], bias.broadcast_to([P, D])).then_inc(small_loaded, 16)
            st.loads(sp)

        @block.gpsimd
        def _(pool):
            norm.pool(pool)
            pool.wait_ge(small_loaded, 48)
            for b in range(B):
                pool.wait_ge(norm.scaled, b + 1)
                pool.tensor_tensor(R[:, b, :], R[:, b, :], bias_all[:, :], ALU.add).then_inc(bias_added, 1)

        @block.vector
        def _(dve):
            link = Chain(dve, steps)
            norm.vector(dve, banks[4:8], st)
            dve.wait_ge(a_high, 1)
            dve.tensor_tensor(AL[:, :, :], A[:, :, :], f32(AH[:, :, :]), ALU.subtract).then_inc(a_low, 1)
            for t in range(SIDE_AT - LEAD, SIDE_AT + 4 - LEAD):
                st.at_vector(dve, 0, t)

            dve.wait_ge(res_done, 1)
            link(dve.tensor_copy(res[:, :, :], banks[5][:, 0:B * AR].rearrange("p (b n) -> p b n", b=B)))
            logits = res[:, :, RANK:AR]
            link(dve.tensor_reduce(small[:, 0, :], logits, AXX, ALU.max))
            dve.tensor_tensor(pr[:, :, :], logits, bce(small[:, 0, :]), ALU.subtract).then_inc(shifted, 1)
            dve.wait_ge(exp_done, 1)
            link(dve.tensor_reduce(small[:, 1, :], pr[:, :, :], AXX, ALU.add))
            link(dve.reciprocal(small[:, 2, :], small[:, 1, :]))
            link(dve.tensor_tensor(pr[:, :, :], pr[:, :, :], bce(small[:, 2, :]), ALU.mult))
            for n in range(2):
                top = small[:, 3 + n, :]
                link(dve.tensor_reduce(top, pr[:, :, :], AXX, ALU.max))
                link(dve.tensor_tensor(key[:, :, :], pr[:, :, :], bce(top), ALU.is_lt))
                link(dve.scalar_tensor_tensor(out=key[:, :, :], in0=key[:, :, :], scalar=BIG,
                                              in1=io[:, :].unsqueeze(1).broadcast_to([P, B, EXPERTS]),
                                              op0=ALU.mult, op1=ALU.add))
                link(dve.tensor_reduce(small[:, 5, :], key[:, :, :], AXX, ALU.min))
                link(dve.tensor_tensor(one[n][:, :, :], key[:, :, :], bce(small[:, 5, :]), ALU.is_equal))
                if n == 0:
                    link(dve.scalar_tensor_tensor(out=pr[:, :, :], in0=one[0][:, :, :], scalar=-2.0,
                                                  in1=pr[:, :, :], op0=ALU.mult, op1=ALU.add))
            link(dve.tensor_tensor(small[:, 6, :], small[:, 3, :], small[:, 4, :], ALU.add))
            link(dve.tensor_scalar(small[:, 6, :], small[:, 6, :], 1e-6, None, ALU.add))
            link(dve.reciprocal(small[:, 7, :], small[:, 6, :]))
            link(dve.tensor_scalar(small[:, 7, :], small[:, 7, :], SCALING, None, ALU.mult))
            for n in range(2):
                link(dve.tensor_tensor(small[:, 3 + n, :], small[:, 3 + n, :], small[:, 7, :], ALU.mult))
                link(dve.tensor_tensor(one[n][:, :, :], one[n][:, :, :], bce(small[:, 3 + n, :]), ALU.mult))
            link(dve.tensor_tensor(wt[:, :, :], one[0][:, :, :], one[1][:, :, :], ALU.add))

            def rows(b):
                if b >= 2:
                    dve.wait_ge(rows_turned, 2 * (b - 1))
                dve.tensor_tensor(ET[b % 2].rearrange("p (e r) -> p e r", e=EXPERTS),
                                  wt[:, b, :].unsqueeze(2).broadcast_to([P, EXPERTS, RANK]),
                                  res[:, b, 0:RANK].unsqueeze(1).broadcast_to([P, EXPERTS, RANK]),
                                  ALU.mult).then_inc(rows_done, 1)

            def rows_low_parts(n):
                b, g = n // 2, n % 2
                dve.wait_ge(rows_high, n + 1)
                part = (slice(None), slice(4 * g, 4 * g + 4), slice(b * P, (b + 1) * P))
                dve.tensor_tensor(EL[part], banks[4 + n % 4][:, :].rearrange("p (c t) -> p c t", c=4), f32(EH[part]),
                                  ALU.subtract).then_inc(rows_low, 1)

            def add_output(r, t, n, b):
                if isinstance(n, int) and n == NB - 1:
                    dve.wait_ge(last_done, b + 1)
                else:
                    dve.wait_ge(st.used, r * ROUND + t + 1)
                o = R[:, b, bass.ds(n * NT, NT)]
                dve.tensor_tensor(o, banks[b][:, :], o, ALU.add).then_inc(out_added, 1)

            for t in range(SIDE_AT + 4 - LEAD, PER):
                st.at_vector(dve, 0, t)
                if ROWS_AT - 2 <= t < ROWS_AT - 2 + B:
                    rows(t - ROWS_AT + 2)
                if ROWS_AT <= t < ROWS_AT + 2 * B:
                    rows_low_parts(t - ROWS_AT)
            dve.wait_ge(bias_added, B)
            for b in range(B):
                add_output(0, PER - 1, 0, b)

            def block_of(n):
                for t in range(PER):
                    st.at_vector(dve, n * ROUNDS, t)
                for b in range(B):
                    add_output(n * ROUNDS, PER - 1, n, b)

            with dve.Fori(1, NB - 1) as n:
                block_of(n)
            block_of(NB - 1)

        @block.scalar
        def _(act):
            norm.scalar(act, banks[4:8], st)
            act.wait_ge(small_loaded, 48)
            act.activation(AH[:, :, :], A[:, :, :], ACT.Copy).then_inc(a_high, 1)
            def rows_high_parts(n):
                b, g = n // 2, n % 2
                act.wait_ge(rows_turned, n + 1)
                act.activation(EH[:, 4 * g:4 * g + 4, b * P:(b + 1) * P],
                               banks[4 + n % 4][:, :].rearrange("p (c t) -> p c t", c=4), ACT.Copy).then_inc(rows_high, 1)

            def store(n):
                act.wait_ge(out_added, (n + 1) * B)
                act.dma_start(out[:, :, bass.ds(n * NT, NT)].rearrange("b p d -> p b d"),
                              R[:, :, bass.ds(n * NT, NT)]).then_inc(out_stored, 16)

            for t in range(SIDE_AT - LEAD, PER):
                st.at_scalar(act, 0, t)
                if t == SIDE_AT:
                    act.wait_ge(side_done, 1)
                    act.activation(sideT[:, :], banks[4][0:AR, :], ACT.Copy).then_inc(side_copied, 1)
                if t == SIDE_AT + 4 - LEAD:
                    act.wait_ge(shifted, 1)
                    act.activation(pr[:, :, :], pr[:, :, :], ACT.Exp).then_inc(exp_done, 1)
                if ROWS_AT <= t < ROWS_AT + 2 * B:
                    rows_high_parts(t - ROWS_AT)

            def block_of(n):
                for t in range(PER):
                    st.at_scalar(act, n * ROUNDS, t)
                    if t == 4:
                        store(n - 1)

            with act.Fori(1, NB - 1) as n:
                block_of(n)
            block_of(NB - 1)
            for b in range(B):
                act.wait_ge(out_added, (NB - 1) * B + b + 1)
                act.dma_start(out[b, :, (NB - 1) * NT:], R[:, b, (NB - 1) * NT:]).then_inc(out_stored, 16)
            act.wait_ge(out_stored, 16 * (NB - 1 + B))

        @block.tensor
        def _(pe):
            XH, XL = norm.XH, norm.XL
            norm.tensor(pe, banks[4:8], st, banks[0:4])
            pe.wait_ge(a_low, 1)
            for k in range(KD):
                pe.matmul(banks[4][0:AR, :], AH[:, k, :], XH[:, k, :], start=k == 0, stop=False)
                pe.matmul(banks[4][0:AR, :], AL[:, k, :], XH[:, k, :], start=False, stop=False)
                mm = pe.matmul(banks[4][0:AR, :], AH[:, k, :], XL[:, k, :], start=False, stop=k == KD - 1)
            mm.then_inc(side_done, 1)

            def turn_side():
                pe.wait_ge(side_copied, 1)
                for b in range(B):
                    mm = pe.transpose(banks[5][:, b * AR:(b + 1) * AR], sideT[:, b * P:(b + 1) * P], ident[0:AR, 0:AR])
                mm.then_inc(res_done, 1)

            def turn_rows(n):
                b, g = n // 2, n % 2
                pe.wait_ge(rows_done, b + 1)
                if n >= 4:
                    pe.wait_ge(rows_low, n - 3)
                elif n == 0:
                    pe.wait_ge(steps, 1)
                for c in range(4):
                    mm = pe.transpose(banks[4 + n % 4][:, c * P:(c + 1) * P], ET[b % 2][:, (4 * g + c) * P:(4 * g + c + 1) * P],
                                      ident[:, :])
                mm.then_inc(rows_turned, 1)

            def products(r, t, free):
                xh, xl = (XH[:, t, :], XL[:, t, :]) if t < KD else (EH[:, t - KD, :], EL[:, t - KD, :])
                st.product_tokens(pe, r, t, xh, xl, banks[0:4], t == 0, t == PER - 1, free if t == 0 else None)

            for t in range(SIDE_AT, PER):
                if t == SIDE_AT + 1:
                    turn_side()
                if ROWS_AT <= t < ROWS_AT + 2 * B:
                    turn_rows(t - ROWS_AT)
                if t == KD:
                    pe.wait_ge(rows_low, 2 * B)
                products(0, t, None)
            with pe.Fori(1, NB - 1) as n:
                for t in range(PER):
                    products(n * ROUNDS, t, lambda b: pe.wait_ge(out_added, (n - 1) * B + b + 1))
            for t in range(PER - PART_SLOTS):
                products((NB - 1) * ROUNDS, t, lambda b: pe.wait_ge(out_added, (NB - 2) * B + b + 1))
            k = KE - PART_SLOTS
            st.products_by_batch(pe, (NB - 1) * ROUNDS, PER - PART_SLOTS, EH[:, k:, :], EL[:, k:, :], banks[0:4], False, True,
                                 done=last_done)


def _tiles(w, k, n):
    t = w[k * P:(k + 1) * P, n * NT:(n + 1) * NT]
    return t if t.shape[1] == NT else np.pad(t, ((0, 0), (0, NT - t.shape[1])))


def _stream(tiles):
    tiles = list(tiles) + [np.zeros_like(tiles[0])] * (-len(tiles) % ROUND)
    return np.ascontiguousarray(np.stack(tiles).reshape(-1, GROUP, P, NT).transpose(0, 2, 1, 3))


def _read_tiles(w):
    h, outs, c = w.shape
    full = np.zeros((h // 32, 32, c, P // 32, 32), w.dtype)
    for i in range(32):
        full[:, i, :, :outs, i] = w.reshape(h // 32, 32, outs, c)[:, i].transpose(0, 2, 1)
    pieces = full.reshape(KD, P, P)
    return pieces.reshape(KD // PIECE, PIECE, P, P).transpose(2, 0, 1, 3).reshape(P, -1, NT)


def _side(wod, wab):
    n = wod.shape[1]
    A = wab[:RH * AC]
    Bp = wab[RH * AC:2 * RH * AC]
    skip = wab[2 * RH * AC:]
    low = wod[FEAT:]
    return np.concatenate([low, np.zeros((RH - low.shape[0], n), wod.dtype), skip, A, Bp], 0).T


def _side_tiles(wod, wab):
    w = _side(wod, wab)
    k = w.shape[0] // P
    return list(w.reshape(k // 4, 4, P, P).transpose(0, 2, 1, 3).reshape(k // 4, P, NT))


def _side_bias(b):
    one = np.zeros(RH, b.dtype)
    one[8] = 1.0
    return np.concatenate([one, b[2 * RH * AC:], b[:2 * RH * AC]]).reshape(P, 1)


def _columns(g):
    return np.ascontiguousarray(g.reshape(-1, P).T)


def _layouts(i):
    x = lambda name: np.asarray(i["L0_xattn_" + name])
    out = {"x": np.asarray(i["x"]), "pos": np.ascontiguousarray(np.asarray(i["pos_BxS"]).T)}
    wod = x("attn_wod_w")
    out["a_stream"] = _stream([_tiles(x("qkv_w")[o].T, k, 0) for o in range(3) for k in range(4)]
                              + [_tiles(wod[:FEAT].T, k, 0) for k in range(4)])
    out["a_side"], = _side_tiles(wod, x("attn_wab_w"))
    ctx = np.asarray(i["ctx_1024"])
    wod = x("mlp_wod_w")
    out["m_stream"] = _stream([_tiles(ctx[o].T, k, n) for n in range(4) for o in range(2) for k in range(4)]
                              + _side_tiles(wod, x("mlp_wab_w")) + [_tiles(wod[:FEAT].T, k, 0) for k in range(16)])
    for p, q in (("a", "attn"), ("m", "mlp")):
        out[p + "_read"] = _read_tiles(x(q + "_read_w"))
        out[p + "_gamma"] = _columns(x(q + "_read_g"))
        out[p + "_beta"] = _columns(x(q + "_read_b"))
        out[p + "_side_bias"] = _side_bias(x(q + "_wab_b"))
        out[p + "_du"] = np.concatenate([x(q + "_du_w").T, x(q + "_du_b")[None]], 0)
    order = [(m, k, n) for m, n in (("v", 0), ("k", 0), ("k", 1), ("q", 0), ("v", 1)) for k in range(KD)]
    for step in range(1, 9):
        order += [("q", k, step) for k in range(KD) if step < 8]
        order += [("o", 4 * step - 4 + j, n) for n in range(4) for j in range(4)]
    w = {m: np.asarray(i["L0_attn_qw_" + m]) for m in "qkvo"}
    sc = {m: np.asarray(i["L0_attn_scales_" + m]) for m in "qkvo"}
    out["g_stream"] = _stream([_tiles(w[m], k, n) for m, k, n in order])
    out["g_scales"] = np.stack([sc[m][k, n * NT:(n + 1) * NT] for m, k, n in order]).reshape(-1, GROUP * NT)
    base = np.concatenate([np.asarray(i["L0_ffn_base_w"]).T, np.asarray(i["L0_ffn_B"]).transpose(0, 2, 1).reshape(-1, D)], 0)
    out["f_stream"] = _stream([_tiles(base, k, n) for n in range(D // NT) for k in range(base.shape[0] // P)])
    router = np.concatenate([np.asarray(i["L0_ffn_A"]), np.asarray(i["L0_ffn_router_w"])], 0).T
    out["f_router"] = np.ascontiguousarray(router.reshape(KD, P, -1).transpose(1, 0, 2))
    out["f_bias"] = np.asarray(i["L0_ffn_base_b"]).reshape(1, D)

    half = 16
    inv = np.float32(1.0) / np.float32(10000.0) ** (np.arange(half, dtype=np.float32) / np.float32(half))
    out["x_inv"] = np.tile(inv.astype(np.float32), (P, 1))
    inv = (np.float32(1.0) / np.float32(10000.0) ** (np.arange(0, P, 2, dtype=np.float32) / np.float32(P))).astype(np.float32)
    ang = (np.arange(P, dtype=np.float32)[None, :] * inv[:, None]).astype(np.float64)
    cos, sin = np.cos(ang), np.sin(ang)
    out["g_rope"] = np.stack([np.concatenate([cos, cos]), np.concatenate([sin, -sin])], 1).astype(np.float32)
    out["causal"] = np.where(np.tril(np.ones((P, P))) > 0, 0.0, -3e38).astype(np.float32)
    out["iota"] = np.tile(np.arange(16, dtype=np.float32), (P, 1))
    out["ident"] = np.eye(P, dtype=np.float32)
    return {k: np.ascontiguousarray(v) for k, v in out.items()}


def perceiver_layer(nc, t, out):
    with ExitStack() as ctx:
        R = ctx.enter_context(nc.sbuf_tensor("residual", [P, B, D], F32))
        ident = ctx.enter_context(nc.sbuf_tensor("identity", [P, P], F32))
        with nc.sbuf_tensor("hidden", [P, B, D], F32) as H:
            xattn_attention(nc, R, H, ident, t["ident"], t["x"], t["a_read"], t["a_stream"], t["a_gamma"], t["a_beta"], t["pos"], t["x_inv"],
                            t["causal"], t["a_side"], t["a_side_bias"], t["a_du"])
            xattn_mlp(nc, R, H, ident, t["m_read"], t["m_stream"], t["m_gamma"], t["m_beta"], t["m_side_bias"], t["m_du"])
        grouped_query_attention(nc, R, ident, t["g_stream"], t["g_scales"], t["g_rope"], t["causal"])
        routed_ffn(nc, R, ident, t["f_stream"], t["f_router"], t["iota"], t["f_bias"], out)


def kernel(**inputs):
    import concourse.bacc as bacc
    from concourse.bass_utils import run_bass_kernel_spmd

    nc = bacc.Bacc("TRN2", target_bir_lowering=False, num_devices=1)
    arrays = _layouts(inputs)
    tensors = {n: nc.dram_tensor("in_" + n, a.shape, mybir.dt.from_np(a.dtype), kind="ExternalInput").ap() for n, a in arrays.items()}
    out = nc.dram_tensor("out", (B, P, D), F32, kind="ExternalOutput").ap()
    perceiver_layer(nc, tensors, out)
    r = run_bass_kernel_spmd(nc, [{"in_" + n: a for n, a in arrays.items()}], core_ids=[0])
    return r.results[0]["out"]
```
